# Optimizing a Trainium2 kernel written in Bass

```python
import numpy as np
import jax
import jax.numpy as jnp

def _softmax(x, axis=-1):
    return jax.nn.softmax(x, axis=axis)

def _gelu(x):
    return jax.nn.gelu(x, approximate=True)

def _silu(x):
    return jax.nn.silu(x)

def _sigmoid(x):
    return jax.nn.sigmoid(x)

def _layernorm(x, axis=-1, eps=1e-05):
    m = jnp.mean(x, axis=axis, keepdims=True)
    v = jnp.var(x, axis=axis, keepdims=True)
    return (x - m) / jnp.sqrt(v + eps)

def _scatter_add(tgt, idx, src, axis=0):
    return tgt.at[idx].add(src)

def _segment_sum(src, seg, n):
    return jax.ops.segment_sum(src, seg, n)
kernel_name = 'mk_vit_tower_postln_d1_tok_img256_r4_9f76ac'

def setup_inputs(seed: int=0):
    np.random.seed(seed)
    _w = jnp.asarray

    def _rec_inputs():
        import jax
        import jax.numpy as jnp
        _rk = jax.random.key(seed)
        x = -0.000928989 + 1.00043 * jax.random.normal(jax.random.fold_in(_rk, 1), (64, 64, 64, 1), jnp.float32)
        return x
    x = _rec_inputs()

    def _L0_tok_setup():
        import jax, jax.numpy as jnp
        import numpy as np
        B, S, D_A, D_V, D_U, L, M1, M2 = (16, 64, 3, 32, 1, 4, 12, 12)
        MID = 4 * D_U

        def conv1x1(x, w, b):
            return jnp.einsum('bixy,oi->boxy', x, w) + b[None, :, None, None]

        def fourier_layer(x, fw_i):
            Bm, C, M, N = x.shape
            x_ft = jnp.fft.rfft2(x, s=(M, N), norm='ortho')
            w_lo = fw_i[0, ..., 0] + 1j * fw_i[0, ..., 1]
            w_hi = fw_i[1, ..., 0] + 1j * fw_i[1, ..., 1]
            lo = jnp.einsum('bixy,ioxy->boxy', x_ft[:, :, :M1, :M2], w_lo)
            hi = jnp.einsum('bixy,ioxy->boxy', x_ft[:, :, -M1:, :M2], w_hi)
            out_ft = jnp.zeros(x_ft.shape, dtype=x_ft.dtype)
            out_ft = out_ft.at[:, :, :M1, :M2].set(lo)
            out_ft = out_ft.at[:, :, -M1:, :M2].set(hi)
            return jnp.fft.irfft2(out_ft, s=(M, N), norm='ortho')

        def make_grid(b, sx, sy):
            gx = jnp.broadcast_to(jnp.linspace(0.0, 1.0, sx)[None, :, None], (b, sx, sy))
            gy = jnp.broadcast_to(jnp.linspace(0.0, 1.0, sy)[None, None, :], (b, sx, sy))
            return jnp.stack([gx, gy], axis=-1)
        key = jax.random.key(seed)
        ks = jax.random.split(key, 12)
        sc_v = 1.0 / np.sqrt(D_V)
        inp = {'x': jax.random.normal(ks[0], (B, S, S, D_A - 2), dtype=jnp.float32), 'p_w': jax.random.normal(ks[1], (D_V, D_A), dtype=jnp.float32) / np.sqrt(D_A), 'p_b': jnp.zeros((D_V,), dtype=jnp.float32), 'fw': jax.random.normal(ks[2], (L, 2, D_V, D_V, M1, M2, 2), dtype=jnp.float32) * sc_v, 'w1_w': jax.random.normal(ks[3], (L, D_V, D_V), dtype=jnp.float32) * sc_v, 'w1_b': jnp.zeros((L, D_V), dtype=jnp.float32), 'w2_w': jax.random.normal(ks[4], (L, D_V, D_V), dtype=jnp.float32) * sc_v, 'w2_b': jnp.zeros((L, D_V), dtype=jnp.float32), 'q1_w': jax.random.normal(ks[5], (MID, D_V), dtype=jnp.float32) * sc_v, 'q1_b': jnp.zeros((MID,), dtype=jnp.float32), 'q2_w': jax.random.normal(ks[6], (D_U, MID), dtype=jnp.float32) / np.sqrt(MID), 'q2_b': jnp.zeros((D_U,), dtype=jnp.float32)}
        return inp
    _L0_tok_all = _L0_tok_setup()
    _L0_tok_in = {k: v for k, v in _L0_tok_all.items() if k in ('p_w', 'p_b', 'fw', 'w1_w', 'w1_b', 'w2_w', 'w2_b', 'q1_w', 'q1_b', 'q2_w', 'q2_b')}
    del _L0_tok_all

    def _L0_attn_setup():
        import jax, jax.numpy as jnp
        import numpy as np
        U_DECAY = 0.97
        X_DECAY = 0.97
        LN_EPS = 1e-05
        L1_EPS = 1e-12

        def _ln(x):
            m = jnp.mean(x, axis=-1, keepdims=True)
            v = jnp.mean((x - m) ** 2, axis=-1, keepdims=True)
            return (x - m) * jax.lax.rsqrt(v + LN_EPS)
        key = jax.random.key(seed)
        k0, k1, k2, k3 = jax.random.split(key, 4)
        B, T, d, n = (8, 64, 64, 256)
        embeddings = jax.random.normal(k0, (B, T, d), dtype=jnp.float32)
        E = jax.random.normal(k1, (d, n), dtype=jnp.float32) / n ** 0.5
        Dx = jax.random.normal(k2, (n, d), dtype=jnp.float32) / d ** 0.5
        Dy = jax.random.normal(k3, (n, d), dtype=jnp.float32) / d ** 0.5
        return {'embeddings': embeddings, 'E': E, 'Dx': Dx, 'Dy': Dy}
    _L0_attn_all = _L0_attn_setup()
    _L0_attn_in = {k: v for k, v in _L0_attn_all.items() if k in ('E', 'Dx', 'Dy')}
    del _L0_attn_all

    def _L0_ffn_setup():
        import jax, jax.numpy as jnp
        import numpy as np
        DIM = 64
        HEADS = 8
        NUM_KEYS = 64
        NUM_KV = NUM_KEYS ** 2
        PK_TOPK = 16
        FINAL_TOPK = 16
        DIM_KEY = DIM // 2
        P = 2

        def _pk(x, Wq_pk, pk_keys):
            b, n, _ = x.shape
            q = (x @ Wq_pk).reshape(b, n, P, HEADS, DIM_KEY).transpose(2, 0, 1, 3, 4)
            sim = jnp.einsum('pbnhd,pkhd->pbnhk', q, pk_keys)
            scores, idx = jax.lax.top_k(sim, PK_TOPK)
            idx0 = idx[0]
            idx1 = idx[1] * NUM_KEYS
            index = (idx0[..., :, None] + idx1[..., None, :]).reshape(b, n, HEADS, PK_TOPK * PK_TOPK)
            score = (scores[0][..., :, None] + scores[1][..., None, :]).reshape(b, n, HEADS, PK_TOPK * PK_TOPK)
            final_scores, pk_idx = jax.lax.top_k(score, FINAL_TOPK)
            final_indices = jnp.take_along_axis(index, pk_idx, axis=-1)
            final_scores = jax.nn.softmax(final_scores, axis=-1)
            return (final_scores, final_indices)
        key = jax.random.key(seed)
        ks = jax.random.split(key, 7)
        b, n = (2, 256)
        std = 0.02
        x = jax.random.normal(ks[0], (b, n, DIM), dtype=jnp.float32)
        Wq_pk = jax.random.normal(ks[1], (DIM, P * HEADS * DIM_KEY), dtype=jnp.float32) * std
        pk_keys = jax.random.normal(ks[2], (P, NUM_KEYS, HEADS, DIM_KEY), dtype=jnp.float32) * std
        Wq = jax.random.normal(ks[3], (DIM, HEADS * DIM), dtype=jnp.float32) * std
        keys_table = jax.random.normal(ks[4], (NUM_KV * HEADS, DIM), dtype=jnp.float32) * std
        values_table = jax.random.normal(ks[5], (NUM_KV * HEADS, DIM), dtype=jnp.float32) * std
        Wo = jax.random.normal(ks[6], (DIM * HEADS, DIM), dtype=jnp.float32) * std
        return {'x': x, 'Wq_pk': Wq_pk, 'pk_keys': pk_keys, 'Wq': Wq, 'keys_table': keys_table, 'values_table': values_table, 'Wo': Wo}
    _L0_ffn_all = _L0_ffn_setup()
    _L0_ffn_in = {k: v for k, v in _L0_ffn_all.items() if k in ('Wq_pk', 'pk_keys', 'Wq', 'keys_table', 'values_table', 'Wo')}
    del _L0_ffn_all
    return {'x': x, 'L0_tok_p_w': _L0_tok_in['p_w'], 'L0_tok_p_b': _L0_tok_in['p_b'], 'L0_tok_fw': _L0_tok_in['fw'], 'L0_tok_w1_w': _L0_tok_in['w1_w'], 'L0_tok_w1_b': _L0_tok_in['w1_b'], 'L0_tok_w2_w': _L0_tok_in['w2_w'], 'L0_tok_w2_b': _L0_tok_in['w2_b'], 'L0_tok_q1_w': _L0_tok_in['q1_w'], 'L0_tok_q1_b': _L0_tok_in['q1_b'], 'L0_tok_q2_w': _L0_tok_in['q2_w'], 'L0_tok_q2_b': _L0_tok_in['q2_b'], 'L0_attn_E': _L0_attn_in['E'], 'L0_attn_Dx': _L0_attn_in['Dx'], 'L0_attn_Dy': _L0_attn_in['Dy'], 'L0_ffn_Wq_pk': _L0_ffn_in['Wq_pk'], 'L0_ffn_pk_keys': _L0_ffn_in['pk_keys'], 'L0_ffn_Wq': _L0_ffn_in['Wq'], 'L0_ffn_keys_table': _L0_ffn_in['keys_table'], 'L0_ffn_values_table': _L0_ffn_in['values_table'], 'L0_ffn_Wo': _L0_ffn_in['Wo']}

def reference(x, L0_tok_p_w, L0_tok_p_b, L0_tok_fw, L0_tok_w1_w, L0_tok_w1_b, L0_tok_w2_w, L0_tok_w2_b, L0_tok_q1_w, L0_tok_q1_b, L0_tok_q2_w, L0_tok_q2_b, L0_attn_E, L0_attn_Dx, L0_attn_Dy, L0_ffn_Wq_pk, L0_ffn_pk_keys, L0_ffn_Wq, L0_ffn_keys_table, L0_ffn_values_table, L0_ffn_Wo):
    import jax
    import jax.numpy as jnp

    def _L0_tok_ref(x, p_w, p_b, fw, w1_w, w1_b, w2_w, w2_b, q1_w, q1_b, q2_w, q2_b):
        import jax, jax.numpy as jnp
        import numpy as np
        B, S, D_A, D_V, D_U, L, M1, M2 = (16, 64, 3, 32, 1, 4, 12, 12)
        MID = 4 * D_U

        def conv1x1(x, w, b):
            return jnp.einsum('bixy,oi->boxy', x, w) + b[None, :, None, None]

        def fourier_layer(x, fw_i):
            Bm, C, M, N = x.shape
            x_ft = jnp.fft.rfft2(x, s=(M, N), norm='ortho')
            w_lo = fw_i[0, ..., 0] + 1j * fw_i[0, ..., 1]
            w_hi = fw_i[1, ..., 0] + 1j * fw_i[1, ..., 1]
            lo = jnp.einsum('bixy,ioxy->boxy', x_ft[:, :, :M1, :M2], w_lo)
            hi = jnp.einsum('bixy,ioxy->boxy', x_ft[:, :, -M1:, :M2], w_hi)
            out_ft = jnp.zeros(x_ft.shape, dtype=x_ft.dtype)
            out_ft = out_ft.at[:, :, :M1, :M2].set(lo)
            out_ft = out_ft.at[:, :, -M1:, :M2].set(hi)
            return jnp.fft.irfft2(out_ft, s=(M, N), norm='ortho')

        def make_grid(b, sx, sy):
            gx = jnp.broadcast_to(jnp.linspace(0.0, 1.0, sx)[None, :, None], (b, sx, sy))
            gy = jnp.broadcast_to(jnp.linspace(0.0, 1.0, sy)[None, None, :], (b, sx, sy))
            return jnp.stack([gx, gy], axis=-1)
        b, sx, sy = (x.shape[0], x.shape[1], x.shape[2])
        grid = make_grid(b, sx, sy)
        h = jnp.concatenate([x, grid], axis=-1)
        h = jnp.transpose(h, (0, 3, 1, 2))
        h = conv1x1(h, p_w, p_b)
        for i in range(L):
            x1 = fourier_layer(h, fw[i])
            x1 = jax.nn.relu(conv1x1(x1, w1_w[i], w1_b[i]))
            x1 = conv1x1(x1, w2_w[i], w2_b[i])
            h = h + x1
        h = conv1x1(h, q1_w, q1_b)
        h = jax.nn.relu(h)
        h = conv1x1(h, q2_w, q2_b)
        return jnp.squeeze(h)

    def _L0_attn_ref(embeddings, E, Dx, Dy):
        import jax, jax.numpy as jnp
        import numpy as np
        U_DECAY = 0.97
        X_DECAY = 0.97
        LN_EPS = 1e-05
        L1_EPS = 1e-12

        def _ln(x):
            m = jnp.mean(x, axis=-1, keepdims=True)
            v = jnp.mean((x - m) ** 2, axis=-1, keepdims=True)
            return (x - m) * jax.lax.rsqrt(v + LN_EPS)
        B, T, d = embeddings.shape
        n = E.shape[1]

        def step(carry, v_prev):
            x_state, rho = carry
            x_update = jax.nn.relu(v_prev @ Dx.T)
            x_t = X_DECAY * x_state + x_update
            x_t = x_t / jnp.maximum(jnp.sum(jnp.abs(x_t), axis=-1, keepdims=True), L1_EPS)
            a_star = jnp.einsum('bdn,bn->bd', rho, x_t)
            y_core = _ln(a_star) @ Dy.T
            y_t = jax.nn.relu(y_core) * jax.nn.relu(x_t)
            v_star = _ln(y_t @ E.T)
            rho_t = U_DECAY * rho + _ln(v_prev)[:, :, None] * x_t[:, None, :]
            return ((x_t, rho_t), v_star)
        x0 = jnp.zeros((B, n), dtype=embeddings.dtype)
        rho0 = jnp.zeros((B, d, n), dtype=embeddings.dtype)
        _, vs = jax.lax.scan(step, (x0, rho0), jnp.swapaxes(embeddings, 0, 1))
        return jnp.swapaxes(vs, 0, 1)

    def _L0_ffn_ref(x, Wq_pk, pk_keys, Wq, keys_table, values_table, Wo):
        import jax, jax.numpy as jnp
        import numpy as np
        DIM = 64
        HEADS = 8
        NUM_KEYS = 64
        NUM_KV = NUM_KEYS ** 2
        PK_TOPK = 16
        FINAL_TOPK = 16
        DIM_KEY = DIM // 2
        P = 2

        def _pk(x, Wq_pk, pk_keys):
            b, n, _ = x.shape
            q = (x @ Wq_pk).reshape(b, n, P, HEADS, DIM_KEY).transpose(2, 0, 1, 3, 4)
            sim = jnp.einsum('pbnhd,pkhd->pbnhk', q, pk_keys)
            scores, idx = jax.lax.top_k(sim, PK_TOPK)
            idx0 = idx[0]
            idx1 = idx[1] * NUM_KEYS
            index = (idx0[..., :, None] + idx1[..., None, :]).reshape(b, n, HEADS, PK_TOPK * PK_TOPK)
            score = (scores[0][..., :, None] + scores[1][..., None, :]).reshape(b, n, HEADS, PK_TOPK * PK_TOPK)
            final_scores, pk_idx = jax.lax.top_k(score, FINAL_TOPK)
            final_indices = jnp.take_along_axis(index, pk_idx, axis=-1)
            final_scores = jax.nn.softmax(final_scores, axis=-1)
            return (final_scores, final_indices)
        b, n, d = x.shape
        q = (x @ Wq).reshape(b, n, HEADS, DIM) * DIM ** (-0.5)
        kv_scores, indices = _pk(x, Wq_pk, pk_keys)
        offsets = jnp.arange(HEADS, dtype=indices.dtype) * NUM_KV
        ind = indices + offsets[None, None, :, None]
        k = jnp.einsum('bnhk,bnhkd->bnhd', kv_scores, keys_table[ind])
        v = jnp.einsum('bnhk,bnhkd->bnhd', kv_scores, values_table[ind])
        sim = jnp.einsum('bihd,bjhd->bhij', q, k)
        neg = -jnp.finfo(sim.dtype).max
        causal = jnp.tril(jnp.ones((n, n), dtype=bool))
        sim = jnp.where(causal, sim, neg)
        attn = jax.nn.softmax(sim, axis=-1)
        out = jnp.einsum('bhij,bjhd->bhid', attn, v)
        out = out.transpose(0, 2, 1, 3).reshape(b, n, HEADS * DIM)
        return out @ Wo
    h = _L0_tok_ref(x, L0_tok_p_w, L0_tok_p_b, L0_tok_fw, L0_tok_w1_w, L0_tok_w1_b, L0_tok_w2_w, L0_tok_w2_b, L0_tok_q1_w, L0_tok_q1_b, L0_tok_q2_w, L0_tok_q2_b)
    h = _layernorm(h + _L0_attn_ref(h, L0_attn_E, L0_attn_Dx, L0_attn_Dy), axis=-1)
    h = _layernorm(h + _L0_ffn_ref(h, L0_ffn_Wq_pk, L0_ffn_pk_keys, L0_ffn_Wq, L0_ffn_keys_table, L0_ffn_values_table, L0_ffn_Wo), axis=-1)
    return h

_drawn_inputs = setup_inputs


def setup_inputs(seed=0):
    import zlib

    import numpy as np

    out = dict(_drawn_inputs(seed))
    spreads = {'L0_tok_p_b': (0.0, 0.1),
     'L0_tok_w1_b': (0.0, 0.1),
     'L0_tok_w2_b': (0.0, 0.1),
     'L0_tok_q1_b': (0.0, 0.1)}
    factors = {'L0_ffn_Wq_pk': 8.0,
     'L0_ffn_pk_keys': 8.0,
     'L0_ffn_Wq': 64.0,
     'L0_ffn_keys_table': 64.0,
     'L0_ffn_values_table': 8.0,
     'L0_ffn_Wo': 8.0}
    for name, (base, spread) in spreads.items():
        noise = np.random.default_rng([zlib.crc32(name.encode()), seed]).standard_normal(out[name].shape)
        drawn = base * np.exp(spread * noise) if base else spread * noise
        out[name] = jnp.asarray(drawn.astype(out[name].dtype))
    for name, factor in factors.items():
        out[name] = (out[name] * factor).astype(out[name].dtype)
    return out
```

```python
import numpy as np
import concourse.bass as bass
from concourse import mybir
from contextlib import ExitStack

F32 = mybir.dt.float32
U32 = mybir.dt.uint32
ALU = mybir.AluOpType
ACT = mybir.ActivationFunctionType
AX = mybir.AxisListType

B, S, C, L, MODES, MID = 64, 64, 32, 4, 12, 4
K1, K2 = 2 * MODES, MODES
GB, B8 = B // 8, 8
BP = B // 2


def host_constants():
    f = np.float64
    kx = np.concatenate([np.arange(MODES), np.arange(S - MODES, S)]).astype(f)
    ky = np.arange(K2).astype(f)
    pos = np.arange(S).astype(f)
    cx = np.cos(2 * np.pi * np.outer(kx, pos) / S)
    sx = np.sin(2 * np.pi * np.outer(kx, pos) / S)
    cy = np.cos(2 * np.pi * np.outer(ky, pos) / S)
    sy = np.sin(2 * np.pi * np.outer(ky, pos) / S)
    two = np.eye(2)
    half_ri_kx = np.stack([cx.reshape(2, MODES, S), -sx.reshape(2, MODES, S)], 1).reshape(2 * K1, S)
    inv_x = np.kron(two, half_ri_kx)
    alpha = np.where(ky == 0, 1.0, 2.0)[:, None] / S
    inv_y = np.stack([alpha * cy, -alpha * sy])
    inv_y = np.einsum("vky,bc->vkbcy", inv_y, np.eye(4)).reshape(2 * K2 * 4, 4 * S)
    fwd_y = np.stack([cy, -sy]).transpose(2, 0, 1).reshape(S, 2 * K2)
    fwd_y = np.kron(two, fwd_y)
    re_part = np.stack([cx.T, -sx.T], 1) / S
    im_part = np.stack([sx.T, cx.T], 1) / S
    fwd_x = np.stack([np.kron(two, a.reshape(S, 2 * K1)) for a in (re_part, im_part)])
    ri = (np.arange(128) // 32) % 2
    sign = np.stack([np.where(ri == 0, 1.0, -1.0), np.where(ri == 0, -1.0, 1.0)], 1)
    px = (np.arange(128) // 32)[:, None]
    pmask = (px == (np.arange(16) // MID)[None, :]).astype(f)
    grid = np.linspace(0.0, 1.0, S)
    fx = lambda img: _dft(img, kx, ky)
    feats = [None, fx(np.repeat(grid[:, None], S, 1)), fx(np.repeat(grid[None, :], S, 0)), fx(np.ones((S, S)))]
    e = np.zeros((2, 2, 4, GB, MODES, B8, K2))
    for n in (1, 2, 3):
        z = feats[n].reshape(2, MODES, K2)
        e[:, 0, n] = z.real[:, None, :, None, :]
        e[:, 1, n] = z.imag[:, None, :, None, :]
    gridc = np.concatenate([np.tile(grid, 2)[:, None], np.tile(grid[None, :], (128, 1))], 1)
    out = dict(inv_x=inv_x, inv_y=inv_y, fwd_y=fwd_y, fwd_x=fwd_x, sign=sign, pmask=pmask,
               e_const=e.reshape(16, GB * MODES * B8 * K2), gridc=gridc)
    return {k: np.ascontiguousarray(v.astype(np.float32)) for k, v in out.items()}


def _dft(img, kx, ky):
    pos = np.arange(S)
    return np.exp(-2j * np.pi * np.outer(kx, pos) / S) @ img @ np.exp(-2j * np.pi * np.outer(pos, ky) / S) / S


def host_layout(x, L0_tok_p_w, L0_tok_p_b, L0_tok_fw, L0_tok_w1_w, L0_tok_w1_b, L0_tok_w2_w, L0_tok_w2_b,
                L0_tok_q1_w, L0_tok_q1_b, L0_tok_q2_w, L0_tok_q2_b):
    a = {}
    a["xt"] = x[..., 0].reshape(BP, 2, S, S).transpose(1, 3, 0, 2).reshape(128, BP * S)
    fw = L0_tok_fw.transpose(0, 1, 6, 2, 4, 5, 3).reshape(L, 2, 2, C, MODES * K2, C)
    a["fwt"] = np.stack([np.stack([fw[:, :, 0], fw[:, :, 1]], 4), np.stack([fw[:, :, 1], fw[:, :, 0]], 4)], 2)\
        .reshape(L, 128, MODES * K2 * 2 * C)
    w1 = np.zeros((L, 2, 4, C, 4, C), np.float32)
    w2 = np.zeros((L, 4, C, 4, C), np.float32)
    for q in range(4):
        w1[:, 0, q, :, q] = L0_tok_w1_w.transpose(0, 2, 1)
        w1[:, 1, q, :, q ^ 1] = L0_tok_w1_w.transpose(0, 2, 1)
        w2[:, q, :, q] = L0_tok_w2_w.transpose(0, 2, 1)
    a["w1bd"] = w1.reshape(L, 2, 128, 128).transpose(0, 2, 1, 3).reshape(L, 128, 256)
    a["w2bd"] = w2.reshape(L, 128, 128)
    a["w2rep"] = np.tile(L0_tok_w2_w, (1, 1, 4))
    bias = np.zeros((L, 4, C, 3), np.float32)
    bias[:, 0, :, 0] = L0_tok_w1_b
    bias[:, 1, :, 1] = L0_tok_w1_b
    bias[:, 0, :, 2] = L0_tok_w2_b
    a["dcbias"] = bias.reshape(L, 128, 3)
    pw = np.concatenate([L0_tok_p_w, L0_tok_p_b[:, None]], 1)
    p0 = np.zeros((4, 4, 4, C), np.float32)
    for q in range(4):
        p0[q, :, q] = pw.T
    a["p0"] = p0.reshape(16, 128)
    a["tail"] = np.concatenate([pw, L0_tok_q1_w.T, L0_tok_w2_b.T], 1)
    a["tailb"] = np.tile(np.concatenate([L0_tok_q1_b, L0_tok_q2_w[0], L0_tok_q2_b])[None], (128, 1))
    return {k: np.ascontiguousarray(v) for k, v in a.items()}

T_, D = 64, 64
N = 256
H, NK, TOPK, DK = 8, 64, 16, 32
DECAY = 0.97
CAND = [(0, 1, 16), (1, 2, 8), (2, 3, 5), (3, 4, 4), (4, 5, 3), (5, 8, 2), (8, 16, 1)]
NC = sum((b - a) * n for a, b, n in CAND)
NEG = -3.0e38


def ffn_constants():
    s, t = np.meshgrid(np.arange(S), np.arange(S), indexing="ij")
    decay = np.where(s < t, DECAY ** np.maximum(t - 1 - s, 0).astype(np.float64), 0.0)
    i, j = np.meshgrid(np.arange(128), np.arange(128), indexing="ij")
    causal = np.where((i // S == j // S) & (j <= i), 0.0, NEG)
    rowbase = np.tile((np.repeat(np.arange(H), TOPK) * NK * NK)[None], (128, 1))
    iota = np.tile(np.arange(NC)[None], (128, 1))
    return dict(masks=np.concatenate([np.tile(decay, (2, 1)), causal, rowbase, iota], 1).astype(np.float32))


def ffn_layout(L0_attn_E, L0_attn_Dx, L0_attn_Dy, L0_ffn_Wq_pk, L0_ffn_pk_keys, L0_ffn_Wq, L0_ffn_keys_table,
               L0_ffn_values_table, L0_ffn_Wo):
    a = dict(
        dxt=np.tile(L0_attn_Dx.T, (2, 1)), dyt=L0_attn_Dy.T,
        et=L0_attn_E.T.reshape(2, 128, D).transpose(1, 0, 2).reshape(128, 2 * D),
        wqpk=L0_ffn_Wq_pk.reshape(D, 2 * H, DK).transpose(2, 1, 0).reshape(DK, 2 * H * D),
        pkk=L0_ffn_pk_keys.transpose(3, 0, 2, 1).reshape(DK, 2 * H * NK),
        wq=L0_ffn_Wq, wo=L0_ffn_Wo.reshape(4, 128, D).transpose(1, 0, 2).reshape(128, 4 * D),
        kvtab=np.concatenate([L0_ffn_keys_table, L0_ffn_values_table], 1))
    return {k: np.ascontiguousarray(v) for k, v in a.items()}



def token_mixer(nc, ctx, T, arena, bank, hT_, ident_):
    if True:
        at = [0]

        def sb(name, shape):
            cols = int(np.prod(shape[1:]))
            at[0] += cols
            a = arena[0:shape[0], at[0] - cols:at[0]]
            if len(shape) == 3:
                a = a.rearrange("p (a b) -> p a b", a=shape[1])
            return a
        sem = lambda name: ctx.enter_context(nc.semaphore(name))
        dram = lambda name, shape: nc.dram_tensor(name, shape, F32, kind="Internal").ap()

        gd = dram("gd", (GB, 128, MODES, 2 * K2 * B8))
        fr = dram("fr", (GB, 96, 16, B8 * K2))
        fx = dram("fx", (2 * 2 * MODES, B * K2))

        NM = MODES * K2
        Wt = sb("Wt", [128, NM * 2 * C])
        St = sb("St", [128, GB * MODES * B8 * K2])
        Gc = sb("Gc", [128, 2, K2 * B])
        Gp = sb("Gp", [128, 2, GB * 2 * K2 * B8])
        big = sb("big", [128, 9216])
        Dt = big[0:96, 0:16 * 192]
        Tt = big[0:96, 3072:3072 + 2048]
        Rt = big[:, 5120:5120 + 4096]
        Et = big[0:16, :]
        Yt = sb("Yt", [128, 2, 2048])
        Qt = sb("Qt", [128, 2, 768])
        Ft = sb("Ft", [96, 16 * B8 * K2])
        FRt = Gp[:, :, 0:MODES * B8 * K2]
        Pt = sb("Pt", [128, BP * S * MID])
        hT = hT_
        invx = sb("invx", [96, 128]); invy = sb("invy", [96, 256]); fwdy = sb("fwdy", [128, 48])
        fwdx = sb("fwdx", [128, 2, 96]); sign = sb("sign", [128, 2]); pmask = sb("pmask", [128, 16])
        gridc = sb("gridc", [128, 65]); ident = ident_
        w1t = sb("w1t", [128, 2, 128]); w2t = sb("w2t", [128, 128]); w2r = sb("w2r", [32, 128])
        dcb = sb("dcb", [128, 3]); p0 = sb("p0", [16, 128]); tail = sb("tail", [32, 12]); tailb = sb("tailb", [128, 9])
        pw = sb("pw", [128, 16]); prod = sb("prod", [32, 16]); ones = sb("ones", [32, 128])
        cf = sb("cf", [128, 16]); t4 = sb("t4", [128, 4]); base = sb("base", [128, 256])
        ptail = sb("ptail", [32, 4])

        names = """consts fw small wfix drdy mix_a mix_d gp_a gp_d i1 t_a t_d i2 r_a r_d xf x_a x_d pf p_d
            qf q_a q_d ff f_a f_d i1_it fst w2f w2d srdy mixf w1f pwf pw_d e_in fxp fxq fxf fxs idn init0 init1
            cfd prodd cff c1 c2 c3 s0f s0d pool_i sgn1 hfin h1_ h2_ dcl xin passed""".split()
        s = {n: sem("s_" + n) for n in names}
        gst = [sem("gst0"), sem("gst1")]
        frt = [sem("frt0"), sem("frt1")]

        Sv = St[:, :].rearrange("p (g k b y) -> p g k b y", g=GB, k=MODES, b=B8)
        Wv = Wt[:, :].rearrange("p (m r o) -> p m (r o)", m=NM, r=2)
        Wn = Wt[:, :].rearrange("p (m r o) -> p m r o", m=NM, r=2)
        Gpv = Gp[:, :, :].rearrange("p s (g v y b) -> p s g v y b", g=2 * GB, v=2, y=K2)
        Dv = Dt.rearrange("p (s u c) -> p s u c", s=16, u=2)
        Tv = Tt.rearrange("p (x j s) -> p s j x", x=S, j=2)
        Pv = Pt[:, :].rearrange("p (u c) -> p u c", u=BP)
        Fv = Ft[:, :].rearrange("p (o b y) -> p o b y", o=16, b=B8)
        Yv = Yt[:, :, :].rearrange("p m (z o) -> p m z o", o=16)
        Yw = Yt[:, :, :].rearrange("p m (q x o) -> p m x q o", q=2, x=S)
        Qv = Qt[:, :, :].rearrange("p m (o b r y) -> p m r o b y", o=16, b=2, r=2)
        TB, RB, XB, PB, FB = bank[0:2], bank[2:4], bank[4:6], bank[6], bank[7]
        MB, WB = bank[0:2], bank[2:6]

        assert at[0] <= ARENA

        def sync_program(sp):
            def load_modes(l):
                sp.dma_start(Wt[:, :], T["fwt"][bass.ds(l, 1)].rearrange("a p c -> (a p) c")).then_inc(s["fw"], 16)

            def load_layer(l):
                d = bass.ds(l, 1)
                for dst, src in ((w1t[:, :, :].rearrange("p a b -> p (a b)"), T["w1bd"]), (w2t[:, :], T["w2bd"]),
                                 (w2r[:, :], T["w2rep"]), (dcb[:, :], T["dcbias"])):
                    sp.dma_start(dst, src[d].rearrange("a p c -> (a p) c")).then_inc(s["small"], 16)

            for n in ("i1", "fst", "f_d", "w2d"):
                sp.sem_inc(s[n], 1)
            for dst, n in ((hT[:, :], "xt"), (fwdy[:, :], "fwd_y"), (fwdx[:, 0, :], 0), (fwdx[:, 1, :], 1),
                           (sign[:, :], "sign"), (pmask[:, :], "pmask"), (gridc[:, :], "gridc"), (p0[:, :], "p0"),
                           (tail[:, :], "tail"), (tailb[:, :], "tailb"), (invx[:, :], "inv_x"), (invy[:, :], "inv_y")):
                src = T["fwd_x"][n] if isinstance(n, int) else T[n]
                sp.dma_start(dst, src).then_inc(s["consts"], 16)
            sp.dma_start(Et, T["e_const"]).then_inc(s["e_in"], 16)
            load_layer(0)
            load_modes(0)
            sp.wait_ge(s["fxs"], 3)
            sp.dma_start(fx, Yt[0:48, 0, 0:768]).then_inc(s["xin"], 16)
            sp.wait_ge(s["xin"], 16)
            sp.wait_ge(s["e_in"], 16)
            for q in range(4):
                hf, ri = q // 2, q % 2
                r0 = (ri * 2 + hf) * MODES
                sp.dma_start(big[q * 4:q * 4 + 1, :].rearrange("p (g k c) -> p g k c", g=GB, k=MODES),
                             fx[r0:r0 + MODES, :].rearrange("k (a g c) -> a g k c", a=1, g=GB)).then_inc(s["e_in"], 16)

            def spectrum_store(l):
                for kx in range(MODES):
                    sp.wait_ge(s["gp_a"], l * 24 + 2 * kx + 2)
                    sp.sem_inc(s["passed"], 1)
                    sp.wait_ge(s["gp_d"], l * 24 + 2 * kx + 2)
                    sp.sem_inc(s["passed"], 1)
                    sp.dma_start(gd[:, :, kx, :].rearrange("g p c -> p g c"),
                                 Gp[:, kx % 2, :].rearrange("p (g c) -> p g c", g=GB)).then_inc(gst[kx % 2], 16)

            def space_loads(l, more):
                for k in (0, 1):
                    sp.wait_ge(gst[k], 96 * l + 96)
                    sp.sem_inc(s["passed"], 1)
                with sp.Fori(0, GB) as g:
                    it = l * GB + g
                    sp.wait_ge(s["i1"], 8 * it + 1)
                    sp.sem_inc(s["passed"], 1)
                    for j in range(2):
                        for q in range(4):
                            sp.dma_start(Dt[(j * 4 + q) * MODES:(j * 4 + q + 1) * MODES, :].rearrange("k (s c) -> k s c", s=16),
                                         gd[bass.ds(g, 1), q * 32 + j * 16:q * 32 + j * 16 + 16, :, :]
                                         .rearrange("a s k c -> k (a s) c")).then_inc(s["drdy"], 16)
                    if more:
                        sp.wait_ge(s["f_a"], 2 * it + 2)
                        sp.sem_inc(s["passed"], 1)
                        sp.wait_ge(s["f_d"], 2 * it + 2 + 1)
                        sp.sem_inc(s["passed"], 1)
                        sp.dma_start(fr[bass.ds(g, 1)].rearrange("a p o c -> (a p) (o c)"), Ft[:, :]).then_inc(s["fst"], 16)

            def update_loads(l):
                sp.wait_ge(s["fst"], l * 128 + 128 + 1)
                sp.sem_inc(s["passed"], 1)
                with sp.Fori(0, GB // 2) as gg:
                    for k in range(2):
                        if k == 0:
                            sp.wait_ge(s["w2d"], l * GB + gg * 2 + 1)
                            sp.sem_inc(s["passed"], 1)
                        for o2 in range(2):
                            for ri in range(2):
                                for hf in range(2):
                                    r0 = ((o2 * 2 + ri) * 2 + hf) * MODES
                                    p0_ = hf * 64 + ri * 32 + o2 * 16
                                    sp.dma_start(FRt[p0_:p0_ + 16, k, :].rearrange("p (k c) -> p k c", k=MODES),
                                                 fr[bass.ds(gg * 2 + k, 1), r0:r0 + MODES, :, :]
                                                 .rearrange("a k o c -> (a o) k c")).then_inc(frt[k], 16)

            with sp.Fori(0, L - 1) as l:
                spectrum_store(l)
                load_modes(l + 1)
                space_loads(l, True)
                update_loads(l)
                sp.wait_ge(s["srdy"], l + 2)
                sp.sem_inc(s["passed"], 1)
                load_layer(l + 1)
            spectrum_store(L - 1)
            space_loads(L - 1, False)

        def tensor_program(pe):
            mm = nc.tensor.matmul
            pe.wait_ge(s["consts"], 12 * 16)
            for f in range(4):
                for k in range(8):
                    u = f * 8 + k
                    last = mm(bank[f][0:64, k * 48:k * 48 + 48], hT[:, u * 64:u * 64 + 64], fwdy[:, :], start=True, stop=True)
                last.then_inc(s["fxp"], 1)
            for f in range(2):
                pe.wait_ge(s["fxq"], 4)
                for r in range(2):
                    rhs = Yt[0:64, 1, 0:1536].rearrange("p (u r y) -> p u r y", r=2, y=K2)[:, f * 32:f * 32 + 32, r, :]
                    last = mm(bank[4 + f][0:48, 0:384], fwdx[0:64, r, 0:48], rhs, start=(r == 0), stop=(r == 1))
                last.then_inc(s["fxf"], 1)
            pe.wait_ge(s["prodd"], 1)
            mm(bank[6][:, 0:16], ones[:, :], prod[:, :], start=True, stop=True).then_inc(s["cff"], 1)
            pe.wait_ge(s["idn"], 2)
            pe.wait_ge(s["e_in"], 5 * 16)
            for c in range(24):
                if c >= 4:
                    pe.wait_ge(s["s0d"], c - 3)
                elif c == 0:
                    pe.wait_ge(s["fxq"], 4)
                mm(bank[c % 4][:, 0:384], p0[:, :], Et[:, c * 384:c * 384 + 384], start=True, stop=True).then_inc(s["s0f"], 1)

            def spectrum(l):
                pe.wait_ge(s["small"], l * 64 + 64)
                pe.wait_ge(s["srdy"], l + 1)
                mm(bank[6][:, 0:4], w2r[:, :], tail[:, 4:8], start=True, stop=True).then_inc(s["pwf"], 1)
                pe.wait_ge(s["wfix"], l + 1)
                pe.sem_inc(s["passed"], 1)
                for kx in range(MODES + 1):
                    if kx < MODES:
                        for h2 in range(2):
                            if kx >= 1:
                                pe.wait_ge(s["mix_a" if h2 == 0 else "mix_d"], l * MODES + kx)
                                pe.sem_inc(s["passed"], 1)
                            for y in range(6):
                                ky = h2 * 6 + y
                                for hf in range(2):
                                    last = mm(MB[h2][64 * hf:64 * hf + 64, y * 64:y * 64 + 64],
                                              Wv[64 * hf:64 * hf + 64, kx * K2 + ky, :],
                                              Sv[64 * hf:64 * hf + 64, :, kx, :, ky], start=True, stop=True)
                            last.then_inc(s["mixf"], 1)
                    if kx >= 1:
                        k = kx - 1
                        pe.wait_ge(s["mix_a"], l * MODES + k + 1)
                        pe.wait_ge(s["mix_d"], l * MODES + k + 1)
                        for v in range(2):
                            for h2 in range(2):
                                if k >= 1:
                                    pe.wait_ge(s["gp_a" if v == 0 else "gp_d"], l * 24 + 2 * (k - 1) + h2 + 1)
                                mm(WB[2 * v + h2][:, 0:384], w1t[:, v, :], Gc[:, k % 2, h2 * 384:h2 * 384 + 384],
                                   start=True, stop=True).then_inc(s["w1f"], 1)

            def space(l, more):
                with pe.Fori(0, GB) as g:
                    it = l * GB + g
                    pe.wait_ge(s["drdy"], 128 * it + 128)
                    for sub in range(2):
                        u = 2 * it + sub
                        for q in range(4):
                            if q >= 2:
                                pe.wait_ge(s["t_a" if q == 2 else "t_d"], 2 * u + 1)
                            for k in range(4):
                                last = mm(TB[q % 2][0:96, k * 128:k * 128 + 128],
                                          Dv[:, q * 4 + k, sub, :], invx[:, :], start=True, stop=True)
                            last.then_inc(s["i1"], 1)
                        pe.wait_ge(s["t_a"], 2 * u + 2)
                        pe.wait_ge(s["t_d"], 2 * u + 2)
                        for f in range(8):
                            if f >= 2:
                                pe.wait_ge(s["r_a" if f % 2 == 0 else "r_d"], 4 * u + f // 2)
                            for k in range(2):
                                xq = 2 * f + k
                                last = mm(RB[f % 2][:, k * 256:k * 256 + 256], Tt[:, xq * 128:xq * 128 + 128], invy[:, :],
                                          start=True, stop=True)
                            last.then_inc(s["i2"], 1)
                        pe.wait_ge(s["p_d"], u + 1)
                        pe.wait_ge(s["pw_d"], l + 1)
                        for f in range(8):
                            m = f // 4
                            if m == 0:
                                pe.wait_ge(s["r_a"], 4 * u + f + 1)
                                pe.wait_ge(s["r_d"], 4 * u + f + 1)
                            if more and f >= 2:
                                pe.wait_ge(s["x_a" if f % 2 == 0 else "x_d"], 4 * u + f // 2)
                            for k in range(4):
                                xq = 4 * (f % 4) + k
                                tile = Rt[:, xq * 256 + m * 128:xq * 256 + m * 128 + 128]
                                if more:
                                    last = nc.tensor.transpose(XB[f % 2][:, k * 128:k * 128 + 128], tile, ident[:, :])
                                    if k == 3:
                                        last.then_inc(s["xf"], 1)
                                last = mm(PB[:, m * 256 + xq * 16:m * 256 + xq * 16 + 16], tile, pw[:, :], start=True, stop=True)
                        last.then_inc(s["pf"], 1)
                        if not more:
                            continue
                        for f in range(4):
                            m = f // 2
                            if f % 2 == 0:
                                pe.wait_ge(s["x_a"], 4 * u + 2 * m + 2)
                                pe.wait_ge(s["x_d"], 4 * u + 2 * m + 2)
                            if f >= 2:
                                pe.wait_ge(s["q_a" if f % 2 == 0 else "q_d"], 2 * u + 1)
                            for k in range(8):
                                op = (f % 2) * 8 + k
                                last = mm(TB[f % 2][:, k * 48:k * 48 + 48], Yv[:, m, :, op], fwdy[:, :], start=True, stop=True)
                            last.then_inc(s["qf"], 1)
                        for m in range(2):
                            pe.wait_ge(s["q_a"], 2 * u + m + 1)
                            pe.wait_ge(s["q_d"], 2 * u + m + 1)
                            if m == 1:
                                pe.wait_ge(s["f_a"], u + 1)
                            else:
                                pe.wait_ge(s["f_d"], u + 1)
                            for r in range(2):
                                last = mm(FB[0:96, 0:384], fwdx[:, r, :], Qv[:, m, r], start=(r == 0), stop=(r == 1))
                            last.then_inc(s["ff"], 1)

            def update(l):
                with pe.Fori(0, GB // 2) as gg:
                    for k in range(2):
                        pe.wait_ge(frt[k], l * 512 + 128 * gg + 128)
                        for c in range(3):
                            if c == 0:
                                pe.wait_ge(s["w2d"], l * GB + gg * 2 + k + 1)
                            mm(bank[c][:, 0:384], w2t[:, :], FRt[:, k, c * 384:c * 384 + 384], start=True, stop=True)\
                                .then_inc(s["w2f"], 1)

            with pe.Fori(0, L - 1) as l:
                spectrum(l)
                space(l, True)
                update(l)
            spectrum(L - 1)
            space(L - 1, False)

        def scalar_program(act):
            cp = lambda o, i, f=ACT.Copy: nc.scalar.activation(o, i, f)
            for f in (0, 2):
                act.wait_ge(s["fxp"], f + 1)
                cp(Yt[0:64, 1, f * 384:f * 384 + 384], bank[f][0:64, 0:384]).then_inc(s["fxq"], 1)
            act.wait_ge(s["fxf"], 1)
            cp(Yt[0:48, 0, 0:384], bank[4][0:48, 0:384]).then_inc(s["fxs"], 1)

            def spectrum(l):
                act.wait_ge(s["fw"], l * 16 + 16)
                act.wait_ge(s["consts"], 192)
                nc.scalar.activation(Wn[:, :, 0, :], Wn[:, :, 0, :], ACT.Copy, scale=sign[:, 0:1]).then_inc(s["wfix"], 1)
                for kx in range(MODES + 1):
                    if kx < MODES:
                        act.wait_ge(s["mixf"], l * 24 + 2 * kx + 1)
                        if kx >= 2:
                            act.wait_ge(s["w1f"], l * 48 + 4 * (kx - 2) + 4)
                        cp(Gc[:, kx % 2, 0:384], MB[0][:, 0:384]).then_inc(s["mix_a"], 1)
                    if kx >= 1:
                        k = kx - 1
                        if k >= 2:
                            act.wait_ge(gst[k % 2], 96 * l + 16 * (k // 2))
                        for h2 in range(2):
                            act.wait_ge(s["w1f"], l * 48 + 4 * k + h2 + 1)
                            src = WB[h2][:, 0:384].rearrange("p (y g b) -> p g y b", y=6, g=2 * GB)
                            dst = Gpv[:, k % 2, :, 0, h2 * 6:h2 * 6 + 6, :]
                            if k == 0 and h2 == 0:
                                act.wait_ge(s["dcl"], l + 1)
                                nc.scalar.activation(dst[:, :, 0, :], src[:, :, 0, :], ACT.Identity, bias=dcb[:, 0:1])
                                dst, src = dst[:, :, 1:6, :], src[:, :, 1:6, :]
                            cp(dst, src).then_inc(s["gp_a"], 1)

            def space(l, more):
                with act.Fori(0, GB) as g:
                    it = l * GB + g
                    for sub in range(2):
                        u = 2 * it + sub
                        for q in (0, 2):
                            act.wait_ge(s["i1"], 4 * u + q + 1 + 1)
                            cp(Tv[:, q * 4:q * 4 + 4], TB[0][0:96, :].rearrange("p (s j x) -> p s j x", s=4, j=2)).then_inc(s["t_a"], 1)
                        for f in (0, 2, 4, 6):
                            act.wait_ge(s["i2"], 8 * u + f + 1)
                            cp(Rt[:, f * 512:f * 512 + 512], RB[0][:, :], ACT.Relu).then_inc(s["r_a"], 1)
                        if not more:
                            continue
                        for f in (0, 2, 4, 6):
                            act.wait_ge(s["xf"], 8 * u + f + 1)
                            cp(Yw[:, f // 4, (f % 4) * 16:(f % 4) * 16 + 16], XB[0][:, :].rearrange("p (x q o) -> p x q o", x=16, q=2)).then_inc(s["x_a"], 1)
                        for f in (0, 2):
                            act.wait_ge(s["qf"], 4 * u + f + 1)
                            cp(Qt[:, f // 2, 0:384], TB[0][:, 0:384]).then_inc(s["q_a"], 1)
                        act.wait_ge(s["ff"], 2 * u + 1)
                        if sub == 0:
                            act.wait_ge(s["fst"], 16 * it + 1)
                        cp(Fv[:, :, sub * 4:sub * 4 + 2, :], FB[0:96, 0:384].rearrange("p (o b y) -> p o b y", o=16, b=2)).then_inc(s["f_a"], 1)

            with act.Fori(0, L - 1) as l:
                spectrum(l)
                space(l, True)
            spectrum(L - 1)
            space(L - 1, False)

        def vector_program(dve):
            V = nc.vector
            cp = lambda o, i: V.tensor_copy(o, i)
            V.memset(ones[:, :], 1.0)
            dve.wait_ge(s["consts"], 192)
            V.tensor_tensor(prod[:, :].rearrange("p (f m) -> p f m", f=4),
                            tail[:, 0:4].unsqueeze(2).to_broadcast([32, 4, 4]),
                            tail[:, 4:8].unsqueeze(1).to_broadcast([32, 4, 4]), ALU.mult).then_inc(s["c1"], 1)
            V.tensor_reduce(ptail[:, 0:1], tail[:, 8:12], AX.X, ALU.add).then_inc(s["c1"], 1)
            dve.wait_ge(s["c1"], 2)
            V.scalar_tensor_tensor(prod[:, 12:16], tail[:, 4:8], ptail[:, 0:1], prod[:, 12:16], ALU.mult, ALU.add).then_inc(s["prodd"], 1)
            for f in (1, 3):
                dve.wait_ge(s["fxp"], f + 1)
                cp(Yt[0:64, 1, f * 384:f * 384 + 384], bank[f][0:64, 0:384]).then_inc(s["fxq"], 1)
            dve.wait_ge(s["fxf"], 2)
            cp(Yt[0:48, 0, 384:768], bank[5][0:48, 0:384]).then_inc(s["fxs"], 2)
            dve.wait_ge(s["cff"], 1)
            cp(cf[:, :], bank[6][:, 0:16]).then_inc(s["cfd"], 1)
            dve.wait_ge(s["cfd"], 1)
            V.scalar_tensor_tensor(t4[:, :], cf[:, 8:12], gridc[:, 0:1], cf[:, 12:16], ALU.mult, ALU.add).then_inc(s["cfd"], 1)
            V.tensor_tensor(base[:, :].rearrange("p (x m) -> p x m", m=4), gridc[:, 1:65].unsqueeze(2).to_broadcast([128, 64, 4]),
                            cf[:, 4:8].unsqueeze(1).to_broadcast([128, 64, 4]), ALU.mult).then_inc(s["cfd"], 1)
            dve.wait_ge(s["cfd"], 3)
            V.tensor_tensor(t4[:, :], t4[:, :], tailb[:, 0:4], ALU.add).then_inc(s["cfd"], 1)
            dve.wait_ge(s["cfd"], 4)
            V.tensor_tensor(base[:, :].rearrange("p (x m) -> p x m", m=4), base[:, :].rearrange("p (x m) -> p x m", m=4),
                            t4[:, :].unsqueeze(1).to_broadcast([128, 64, 4]), ALU.add).then_inc(s["init0"], 1)
            for c in range(24):
                dve.wait_ge(s["s0f"], c + 1)
                last = cp(St[:, c * 384:c * 384 + 384], bank[c % 4][:, 0:384])
                last.then_inc(s["s0d"], 1)
            dve.wait_ge(s["s0d"], 24)
            V.memset(ptail[:, 0:1], 0.0).then_inc(s["srdy"], 1)

            def spectrum(l):
                dve.wait_ge(s["small"], l * 64 + 64)
                V.tensor_scalar(w1t[:, 1, :], w1t[:, 1, :], sign[:, 1:2], None, ALU.mult).then_inc(s["c2"], 1)
                V.tensor_scalar(dcb[:, 0:3], dcb[:, 0:3], float(S), None, ALU.mult).then_inc(s["c3"], 1)
                dve.wait_ge(s["c3"], l + 1)
                V.tensor_scalar(dcb[:, 1:2], dcb[:, 1:2], -1.0, None, ALU.mult).then_inc(s["dcl"], 1)
                dve.wait_ge(s["pwf"], l + 1)
                V.tensor_tensor(pw[:, :].rearrange("p (x m) -> p x m", m=4), pmask[:, :].rearrange("p (x m) -> p x m", m=4),
                                bank[6][:, 0:4].unsqueeze(1).to_broadcast([128, 4, 4]), ALU.mult).then_inc(s["pw_d"], 1)
                for kx in range(MODES + 1):
                    if kx < MODES:
                        dve.wait_ge(s["mixf"], l * 24 + 2 * kx + 2)
                        if kx >= 2:
                            dve.wait_ge(s["w1f"], l * 48 + 4 * (kx - 2) + 4)
                        if kx == 0:
                            dve.wait_ge(s["c2"], l + 1)
                        cp(Gc[:, kx % 2, 384:768], MB[1][:, 0:384]).then_inc(s["mix_d"], 1)
                    if kx >= 1:
                        k = kx - 1
                        if k >= 2:
                            dve.wait_ge(gst[k % 2], 96 * l + 16 * (k // 2))
                        for h2 in range(2):
                            dve.wait_ge(s["w1f"], l * 48 + 4 * k + 2 + h2 + 1)
                            src = WB[2 + h2][:, 0:384].rearrange("p (y g b) -> p g y b", y=6, g=2 * GB)
                            dst = Gpv[:, k % 2, :, 1, h2 * 6:h2 * 6 + 6, :]
                            if k == 0 and h2 == 0:
                                dve.wait_ge(s["dcl"], l + 1)
                                V.tensor_scalar(dst[:, :, 0, :], src[:, :, 0, :], dcb[:, 1:2], None, ALU.add)
                                dst, src = dst[:, :, 1:6, :], src[:, :, 1:6, :]
                            cp(dst, src).then_inc(s["gp_d"], 1)

            def space(l, more):
                with dve.Fori(0, GB) as g:
                    it = l * GB + g
                    for sub in range(2):
                        u = 2 * it + sub
                        for q in (1, 3):
                            dve.wait_ge(s["i1"], 4 * u + q + 1 + 1)
                            cp(Tv[:, q * 4:q * 4 + 4], TB[1][0:96, :].rearrange("p (s j x) -> p s j x", s=4, j=2)).then_inc(s["t_d"], 1)
                        for f in (1, 3, 5, 7):
                            dve.wait_ge(s["i2"], 8 * u + f + 1)
                            V.tensor_scalar(Rt[:, f * 512:f * 512 + 512], RB[1][:, :], 0.0, None, ALU.max).then_inc(s["r_d"], 1)
                        if more:
                            for f in (1, 3, 5, 7):
                                dve.wait_ge(s["xf"], 8 * u + f + 1)
                                cp(Yw[:, f // 4, (f % 4) * 16:(f % 4) * 16 + 16], XB[1][:, :].rearrange("p (x q o) -> p x q o", x=16, q=2)).then_inc(s["x_d"], 1)
                        dve.wait_ge(s["pf"], u + 1)
                        pv = Pv[:, bass.ds(g * 4 + 2 * sub, 2), :].rearrange("p u c -> p (u c)")
                        V.tensor_tensor(pv, pv, PB[:, :], ALU.add).then_inc(s["p_d"], 1)
                        if not more:
                            continue
                        for f in (1, 3):
                            dve.wait_ge(s["qf"], 4 * u + f + 1)
                            cp(Qt[:, f // 2, 384:768], TB[1][:, 0:384]).then_inc(s["q_d"], 1)
                        dve.wait_ge(s["ff"], 2 * u + 2)
                        if sub == 0:
                            dve.wait_ge(s["fst"], 16 * it + 1)
                        cp(Fv[:, :, sub * 4 + 2:sub * 4 + 4, :], FB[0:96, 0:384].rearrange("p (o b y) -> p o b y", o=16, b=2)).then_inc(s["f_d"], 1)

            def update(l):
                SG = St[:, :].rearrange("p (g c) -> p g c", g=GB)
                with dve.Fori(0, GB // 2) as gg:
                    for k in range(2):
                        for c in range(3):
                            dve.wait_ge(s["w2f"], 3 * l * GB + 6 * gg + 3 * k + c + 1)
                            sv = SG[:, bass.ds(gg * 2 + k, 1), c * 384:c * 384 + 384].rearrange("p a c -> p (a c)")
                            last = V.tensor_tensor(sv, sv, bank[c][:, 0:384], ALU.add)
                        last.then_inc(s["w2d"], 1)
                dve.wait_ge(s["w2d"], l * GB + GB + 1)
                dc = St[:, :].rearrange("p (g k b y) -> p g k b y", g=GB, k=MODES, b=B8)[:, :, 0, :, 0]
                V.tensor_scalar(dc, dc, dcb[:, 2:3], None, ALU.add).then_inc(s["srdy"], 1)

            dve.wait_ge(s["init1"], 2)
            V.memset(ptail[:, 1:2], 0.0).then_inc(s["p_d"], 1)
            with dve.Fori(0, L - 1) as l:
                spectrum(l)
                space(l, True)
                update(l)
            spectrum(L - 1)
            space(L - 1, False)
            dve.wait_ge(s["p_d"], 1 + 2 * GB * L)
            q2 = tailb[:, 4:8].unsqueeze(1).to_broadcast([128, BP * S, 4])
            P4 = Pt[:, :].rearrange("p (n m) -> p n m", m=4)
            V.scalar_tensor_tensor(P4, P4, 0.0, q2, ALU.max, ALU.mult).then_inc(s["h2_"], 1)
            dve.wait_ge(s["h2_"], 1)
            V.tensor_reduce(hT[:, :], P4, AX.X, ALU.add).then_inc(s["h2_"], 1)
            dve.wait_ge(s["h2_"], 2)
            V.tensor_scalar(hT[:, :], hT[:, :], tailb[:, 8:9], None, ALU.add).then_inc(s["hfin"], 1)

        def gpsimd_program(pool):
            nc.gpsimd.memset(ident[:, :], 0.0).then_inc(s["idn"], 1)
            pool.wait_ge(s["idn"], 1)
            nc.gpsimd.affine_select(out=ident[:, :], in_=ident[:, :], compare_op=ALU.not_equal, fill=1.0, base=0,
                                    pattern=[[-1, 128]], channel_multiplier=1).then_inc(s["idn"], 1)
            pool.wait_ge(s["consts"], 192)
            pool.wait_ge(s["cfd"], 1)
            P4 = Pt[:, :].rearrange("p (n m) -> p n m", m=4)
            nc.gpsimd.tensor_tensor(P4, hT[:, :].unsqueeze(2).to_broadcast([128, BP * S, 4]),
                                    cf[:, 0:4].unsqueeze(1).to_broadcast([128, BP * S, 4]), ALU.mult).then_inc(s["init1"], 1)
            pool.wait_ge(s["init1"], 1)
            pool.wait_ge(s["init0"], 1)
            nc.gpsimd.tensor_tensor(Pv, Pv, base[:, :].unsqueeze(1).to_broadcast([128, BP, 256]), ALU.add).then_inc(s["init1"], 1)
        return sync_program, tensor_program, scalar_program, vector_program, gpsimd_program, s["hfin"]


def token_and_channel_mixers(nc, ctx, T, out, arena, bank, hT, ident, h_ready):
    if True:
        sem = lambda name: ctx.enter_context(nc.semaphore("b_" + name))
        at = [0]

        def sb(cols, rows=128):
            at[0] += cols
            assert at[0] <= ARENA, at[0]
            return arena[0:rows, at[0] - cols:at[0]]
        masks = sb(64 + 128 + 128 + NC + 14)
        decay, causal, rowbase, iota = masks[:, 0:64], masks[:, 64:192], masks[:, 192:320], masks[:, 320:320 + NC]
        dxt, dyt, et, ones = sb(256), sb(256, 64), sb(128), sb(128)
        wqpk, pkk = sb(1024, 32), sb(1024, 32)
        wq, wo, simw = sb(512, 64), sb(256), sb(1024, 64)
        h1 = sb(2048)
        mark = at[0]
        X = sb(8192)
        nsum, cc, dd = sb(4096), sb(4096), sb(4096)
        htok, lnv, gm, la, sq = sb(2048), sb(2048), sb(2048), sb(2048), sb(2048)
        laT = sb(4096, 64)
        st, sum_, var = sb(64), sb(32), sb(32)
        at[0] = mark
        sim, tmp = sb(1024), sb(1024)
        A, If = sb(256), sb(256)
        Iu = sb(256).bitcast(U32)
        cand, pay, tmp2 = sb(H * NC), sb(H * NC), sb(H * NC)
        Vt, posf, pick = sb(128), sb(128), sb(128)
        posu = sb(128).bitcast(U32)
        eq = sb(128 * NC)
        rowidx = sb(256).bitcast(U32)
        wt, qT, hs = sb(256), sb(1024), sb(128)
        hsT = sb(128, 64)
        wsum = sb(8)
        KV = sb(4 * 2048)
        prodt = sb(2048)
        KVs = sb(1024)
        kT, sc, at_, ao, aoT = sb(512), sb(1024), sb(1024), sb(512), sb(512)
        mx, sm = sb(8), sb(8)
        res, rc, rq, rv, yt = sb(64), sb(64), sb(64), sb(4), sb(128)

        names = """ld h id one c_u c_x c_s c_n rec cd pf pd t_p t_e ch lsq lst g_p g_e a_p a_e lt_p lt_e yc_p yc_e v_p v_e
            sw_p sw_e h1ok out0 out1 fr_h fr_t fr_hT fr_s fr_se fr_q fr_qe fch fdif fexp idx bch kt_p kt_e sm_p sm_e bdif bexp
            aw at_p at_e av_p av_e ot_p ot_e wo_p rvv rst done fch2 fch3 b2 passed""".split()
        s = {n: sem(n) for n in names}
        slot = [sem(f"slot{i}") for i in range(4)]

        Av = A.rearrange("p (r k) -> p r k", r=16)
        Iv = Iu.rearrange("p (r k) -> p r k", r=16)
        Ifv = If.rearrange("p (r k) -> p r k", r=16)
        simv, tmpv = sim.rearrange("p (r k) -> p r k", r=16), tmp.rearrange("p (r k) -> p r k", r=16)
        hsv = lambda k: hs[:, k * 64:k * 64 + 64]
        h1v = h1.rearrange("p (u d) -> p u d", u=BP)
        NLD = 8

        def held(eng, sm_, v):
            eng.wait_ge(sm_, v)
            eng.sem_inc(s["passed"], 1)

        BCH = H * 2 + 1

        def schedule(eng, front, back):
            front(0, 0)
            with eng.Fori(0, BP // 2 - 1) as ii:
                for k in range(2):
                    front(2 * ii + k + 1, 1 - k)
                    back(2 * ii + k, k)
            front(BP - 1, 1)
            back(BP - 2, 0)
            back(BP - 1, 1)

        def sync_program(sp):
            sp.sem_inc(s["out0"], 1)
            sp.sem_inc(s["out1"], 1)
            sp.wait_ge(h_ready, 1)
            for dst, n in ((masks[:, 0:320 + NC], "masks"), (dxt, "dxt"), (dyt, "dyt"), (et, "et"), (wqpk, "wqpk"), (pkk, "pkk"),
                           (wq, "wq"), (wo, "wo")):
                sp.dma_start(dst, T[n]).then_inc(s["ld"], 16)

            def tile(i, k):
                held(sp, s["done"], i + 1)
                sp.dma_start(out[bass.ds(i, 1)].rearrange("a p d -> (a p) d"), yt[:, k * 64:k * 64 + 64]).then_inc(s[f"out{k}"], 16)
            with sp.Fori(0, BP // 2) as ii:
                for k in range(2):
                    tile(2 * ii + k, k)
            sp.wait_ge(s["out0"], 16 * (BP // 2) + 1)
            sp.wait_ge(s["out1"], 16 * (BP // 2) + 1)

        def tensor_program(pe):
            mm, tr = nc.tensor.matmul, nc.tensor.transpose
            pe.wait_ge(s["ld"], 16 * NLD)
            for f in range(2):
                for k in range(8):
                    r = f * 8 + k
                    last = mm(bank[f][0:64, k * 64:k * 64 + 64], wqpk[:, r * 64:r * 64 + 64], pkk[:, r * 64:r * 64 + 64],
                              start=True, stop=True)
                last.then_inc(s["sw_p"], 1)
            pe.wait_ge(s["sw_e"], 2)
            for f in range(16):
                nh, b2, c = f % 2, f // 8, (f // 2) % 4
                if f >= 4:
                    pe.wait_ge(s["c_x"], f - 3)
                mm(bank[f % 4][:, :], dxt[64 * b2:64 * b2 + 64, nh * 128:nh * 128 + 128],
                   hT[64 * b2:64 * b2 + 64, c * 512:c * 512 + 512], start=True, stop=True).then_inc(s["c_u"], 1)
            pe.wait_ge(s["one"], 1)
            for f in range(8):
                pe.wait_ge(s["c_x"], 2 * f + 2)
                if f >= 2:
                    pe.wait_ge(s["c_n"], f - 1)
                for nh in range(2):
                    last = mm(bank[4 + f % 2][:, :], ones, X[:, nh * 4096 + f * 512:nh * 4096 + f * 512 + 512],
                              start=(nh == 0), stop=(nh == 1))
                last.then_inc(s["c_s"], 1)
            for c in range(4):
                pe.wait_ge(s["c_x"], 16)
                for u in range(8):
                    for b2 in range(2):
                        last = mm(bank[c][64 * b2:64 * b2 + 64, u * 64:u * 64 + 64],
                                  hT[64 * b2:64 * b2 + 64, (c * 8 + u) * 64:(c * 8 + u) * 64 + 64],
                                  ident[64 * b2:64 * b2 + 64, 64 * b2:64 * b2 + 64], start=True, stop=True)
                last.then_inc(s["t_p"], 1)
            pe.wait_ge(s["cd"], 1)
            pe.wait_ge(s["t_e"], 4)
            for c in range(4):
                for u in range(8):
                    for b2 in range(2):
                        o = b2 * 2048 + (c * 8 + u) * 64
                        for nh in range(2):
                            xt = X[:, nh * 4096 + o:nh * 4096 + o + 64]
                            last = mm(bank[c][64 * b2:64 * b2 + 64, u * 64:u * 64 + 64], xt, xt, start=(nh == 0), stop=(nh == 1))
                last.then_inc(s["g_p"], 1)
            pe.wait_ge(s["lst"], 1)
            for c in range(4):
                pe.wait_ge(s["g_e"], c + 1)
                for u in range(8):
                    for b2 in range(2):
                        o = (c * 8 + u) * 64
                        last = mm(bank[4 + c][64 * b2:64 * b2 + 64, u * 64:u * 64 + 64], gm[64 * b2:64 * b2 + 64, o:o + 64],
                                  lnv[64 * b2:64 * b2 + 64, o:o + 64], start=True, stop=True)
                last.then_inc(s["a_p"], 1)
            pe.wait_ge(s["lst"], 2)
            for c in range(8):
                if c >= 2:
                    pe.wait_ge(s["lt_e"], c - 1)
                for k in range(4):
                    u = c * 4 + k
                    last = tr(bank[c % 2][0:64, k * 128:k * 128 + 128], la[:, u * 64:u * 64 + 64], ident)
                last.then_inc(s["lt_p"], 1)
            pe.wait_ge(s["lt_e"], 8)
            for f in range(16):
                nh, c = f % 2, f // 2
                if f >= 4:
                    pe.wait_ge(s["yc_e"], f - 3)
                mm(bank[2 + f % 4][:, :], dyt[:, nh * 128:nh * 128 + 128], laT[:, c * 512:c * 512 + 512], start=True, stop=True)\
                    .then_inc(s["yc_p"], 1)
            pe.wait_ge(s["yc_e"], 16)
            for c in range(4):
                for u in range(8):
                    for b2 in range(2):
                        o = b2 * 2048 + (c * 8 + u) * 64
                        for nh in range(2):
                            last = mm(bank[c][64 * b2:64 * b2 + 64, u * 64:u * 64 + 64], X[:, nh * 4096 + o:nh * 4096 + o + 64],
                                      et[:, nh * 64:nh * 64 + 64], start=(nh == 0), stop=(nh == 1))
                last.then_inc(s["v_p"], 1)

            def front_k(i, k):
                held(pe, s["fr_h"], i + 1)
                tr(bank[0][0:64, 0:128], hsv(k), ident).then_inc(s["fr_t"], 1)
                pe.wait_ge(s["fr_hT"], i + 1)
                for c in range(2):
                    last = mm(bank[1 + c][:, :], hsT, simw[:, c * 512:c * 512 + 512], start=True, stop=True)
                last.then_inc(s["fr_s"], 1)
                for c in range(4):
                    last = mm(bank[3][:, c * 128:c * 128 + 128], wq[:, c * 128:c * 128 + 128], hsT, start=True, stop=True)
                last.then_inc(s["fr_q"], 1)

            def back(i, k):
                held(pe, s["bch"], BCH * i + H * 2)
                for c in range(4):
                    last = tr(bank[4][:, c * 128:c * 128 + 128], KVs[:, c * 128:c * 128 + 128], ident)
                last.then_inc(s["kt_p"], 1)
                held(pe, s["kt_e"], i + 1)
                held(pe, s["fr_qe"], i + 1)
                for h in range(H):
                    r = 64 * (h % 2)
                    last = mm(bank[5 + h % 2][:, (h // 2) * 128:(h // 2) * 128 + 128],
                              qT[r:r + 64, k * 512 + (h // 2) * 128:k * 512 + (h // 2) * 128 + 128],
                              kT[r:r + 64, (h // 2) * 128:(h // 2) * 128 + 128], start=True, stop=True)
                last.then_inc(s["sm_p"], 1)
                held(pe, s["aw"], i + 1)
                for h in range(H):
                    last = tr(bank[5 + h // 4][:, (h % 4) * 128:(h % 4) * 128 + 128], sc[:, h * 128:h * 128 + 128], ident)
                last.then_inc(s["at_p"], 1)
                pe.wait_ge(s["at_e"], i + 1)
                for h in range(H):
                    last = mm(bank[4][:, h * 64:h * 64 + 64], at_[:, (4 * (h % 2) + h // 2) * 128:(4 * (h % 2) + h // 2) * 128 + 128],
                              KVs[:, 512 + h * 64:512 + h * 64 + 64],
                              start=True, stop=True)
                last.then_inc(s["av_p"], 1)
                pe.wait_ge(s["av_e"], i + 1)
                for c in range(4):
                    last = tr(bank[7][:, c * 128:c * 128 + 128], ao[:, c * 128:c * 128 + 128], ident)
                last.then_inc(s["ot_p"], 1)
                pe.wait_ge(s["ot_e"], i + 1)
                for c in range(4):
                    last = mm(bank[7][:, 0:64], aoT[:, c * 128:c * 128 + 128], wo[:, c * 64:c * 64 + 64], start=(c == 0), stop=(c == 3))
                last.then_inc(s["wo_p"], 1)
            schedule(pe, front_k, back)

        def scalar_program(act):
            A_ = nc.scalar.activation
            for f in range(2):
                act.wait_ge(s["sw_p"], f + 1)
                A_(simw[:, f * 512:f * 512 + 512], bank[f][0:64, :], ACT.Copy).then_inc(s["sw_e"], 1)
            for f in range(16):
                nh, c = f % 2, f // 2
                act.wait_ge(s["c_u"], f + 1)
                A_(X[:, nh * 4096 + c * 512:nh * 4096 + c * 512 + 512], bank[f % 4][:, :], ACT.Relu).then_inc(s["c_x"], 1)
            for c in range(4):
                act.wait_ge(s["t_p"], c + 1)
                A_(htok[:, c * 512:c * 512 + 512], bank[c][:, :], ACT.Copy).then_inc(s["t_e"], 1)
            for n in range(2):
                act.wait_ge(s["lsq"], n + 1)
                A_(var, var, ACT.Sqrt).then_inc(s["ch"], 1)
                if n == 0:
                    continue
            for c in range(8):
                act.wait_ge(s["lt_p"], c + 1)
                dst = laT.rearrange("p (b u t) -> p u b t", b=2, u=BP)[:, c * 4:c * 4 + 4]
                A_(dst, bank[c % 2][0:64, :].rearrange("p (u b t) -> p u b t", u=4, b=2), ACT.Copy).then_inc(s["lt_e"], 1)
            for n in range(2, 4):
                act.wait_ge(s["lsq"], n + 1)
                A_(var, var, ACT.Sqrt).then_inc(s["ch"], 1)

            def front(i, k):
                act.wait_ge(s["h1ok"], 1)
                A_(hsv(k), h1v[:, bass.ds(i, 1), :].rearrange("p a d -> p (a d)"), ACT.Copy).then_inc(s["fr_h"], 1)
                act.wait_ge(s["fr_t"], i + 1)
                A_(hsT, bank[0][0:64, 0:128], ACT.Copy).then_inc(s["fr_hT"], 1)
                act.wait_ge(s["fr_s"], i + 1)
                for c in range(2):
                    last = A_(sim[:, c * 512:c * 512 + 512], bank[1 + c][:, :], ACT.Copy)
                last.then_inc(s["fr_se"], 1)
                act.wait_ge(s["fr_q"], i + 1)
                A_(qT[:, k * 512:k * 512 + 512], bank[3][:, :], ACT.Copy, scale=D ** -0.5).then_inc(s["fr_qe"], 1)
                act.wait_ge(s["fdif"], i + 1)
                A_(wt[:, k * 128:k * 128 + 128], Vt, ACT.Exp).then_inc(s["fexp"], 1)

            def back(i, k):
                act.wait_ge(s["kt_p"], i + 1)
                A_(kT, bank[4][:, :], ACT.Copy).then_inc(s["kt_e"], 1)
                act.wait_ge(s["bdif"], i + 1)
                A_(sc, sc, ACT.Exp).then_inc(s["bexp"], 1)
                act.wait_ge(s["at_p"], i + 1)
                for c in range(2):
                    last = A_(at_[:, c * 512:c * 512 + 512], bank[5 + c][:, :], ACT.Copy)
                last.then_inc(s["at_e"], 1)
                act.wait_ge(s["av_p"], i + 1)
                A_(ao, bank[4][:, :], ACT.Copy).then_inc(s["av_e"], 1)
                act.wait_ge(s["ot_p"], i + 1)
                A_(aoT, bank[7][:, :], ACT.Copy).then_inc(s["ot_e"], 1)
                act.wait_ge(s["rvv"], i + 1)
                A_(rv[:, 1:2], rv[:, 0:1], ACT.Sqrt).then_inc(s["rst"], 1)
            schedule(act, front, back)

        def vector_program(dve):
            V = nc.vector
            own = [0]

            def link(ins, name="rec"):
                own[0] += 1
                ins.then_inc(s["rec"], 1)
                dve.wait_ge(s["rec"], own[0])
            V.memset(ones, 1.0).then_inc(s["one"], 1)
            for c in range(8):
                dve.wait_ge(s["c_s"], c + 1)
                V.tensor_copy(nsum[:, c * 512:c * 512 + 512], bank[4 + c % 2][:, :]).then_inc(s["c_n"], 1)
            dve.wait_ge(s["c_n"], 8)
            link(V.memset(st, 0.0))
            nv = nsum.rearrange("p (b t) -> p b t", t=T_)
            base = own[0]
            with dve.Fori(0, T_) as t:
                dve.wait_ge(s["rec"], base + 2 * t)
                nt = nv[:, :, bass.ds(t, 1)].rearrange("p b a -> p (b a)")
                V.scalar_tensor_tensor(nt, st, DECAY, nt, ALU.mult, ALU.add).then_inc(s["rec"], 1)
                dve.wait_ge(s["rec"], base + 2 * t + 1)
                V.tensor_scalar(st, nt, 1e12, 1.0, ALU.mult, ALU.min).then_inc(s["rec"], 1)
            own[0] = base + 2 * T_
            dve.wait_ge(s["rec"], own[0])
            link(V.tensor_scalar(nsum, nsum, 1e-12, None, ALU.max))
            link(V.reciprocal(cc, nsum))
            link(V.tensor_scalar(dd, cc, DECAY, None, ALU.mult))
            link(V.memset(dd.rearrange("p (b t) -> p b t", t=T_)[:, :, 0], 0.0))
            for nh in range(2):
                xs = X[:, nh * 4096:nh * 4096 + 4096]
                link(V.tensor_tensor(xs, xs, cc, ALU.mult))
                link(V.tensor_tensor_scan(xs, dd, xs, 0.0, ALU.mult, ALU.add))
            V.memset(st, 0.0).then_inc(s["cd"], 1)

            view = lambda a: a.rearrange("p (u d) -> p u d", d=D)
            wide = lambda a: a.unsqueeze(2).to_broadcast([128, BP, D])
            nln = [0]

            def layer_norm(dst, src):
                link(V.tensor_reduce(sum_, view(src), AX.X, ALU.add))
                link(V.tensor_scalar(sum_, sum_, 1.0 / D, None, ALU.mult))
                link(V.tensor_tensor(view(dst), view(src), wide(sum_), ALU.subtract))
                link(V.tensor_tensor(sq, dst, dst, ALU.mult))
                link(V.tensor_reduce(var, view(sq), AX.X, ALU.add))
                V.tensor_scalar(var, var, 1.0 / D, 1e-5, ALU.mult, ALU.add).then_inc(s["lsq"], 1)
                nln[0] += 1
                dve.wait_ge(s["ch"], nln[0])
                link(V.reciprocal(var, var))
                link(V.tensor_tensor(view(dst), view(dst), wide(var), ALU.mult))
            dve.wait_ge(s["t_e"], 4)
            layer_norm(lnv, htok)
            V.memset(st, 0.0).then_inc(s["lst"], 1)
            for c in range(4):
                dve.wait_ge(s["g_p"], c + 1)
                V.tensor_tensor(view(gm[:, c * 512:c * 512 + 512]), view(bank[c][:, :]),
                                decay.unsqueeze(1).to_broadcast([128, 8, 64]), ALU.mult).then_inc(s["g_e"], 1)
            for c in range(4):
                dve.wait_ge(s["a_p"], c + 1)
                link(V.tensor_copy(la[:, c * 512:c * 512 + 512], bank[4 + c][:, :]))
            layer_norm(la, la)
            V.memset(st, 0.0).then_inc(s["lst"], 1)
            for f in range(16):
                nh, c = f % 2, f // 2
                dve.wait_ge(s["yc_p"], f + 1)
                xs = X[:, nh * 4096 + c * 512:nh * 4096 + c * 512 + 512]
                V.scalar_tensor_tensor(xs, bank[2 + f % 4][:, :], 0.0, xs, ALU.max, ALU.mult).then_inc(s["yc_e"], 1)
            for c in range(4):
                dve.wait_ge(s["v_p"], c + 1)
                link(V.tensor_copy(la[:, c * 512:c * 512 + 512], bank[c][:, :]))
            layer_norm(la, la)
            link(V.tensor_tensor(la, la, htok, ALU.add))
            layer_norm(h1, la)
            V.memset(st, 0.0).then_inc(s["h1ok"], 1)

            FCH = 12
            candv, payv, tmp2v = (a.rearrange("p (h c) -> p h c", h=H) for a in (cand, pay, tmp2))
            Vv, posv = Vt.rearrange("p (h k) -> p h k", h=H), posu.rearrange("p (h k) -> p h k", h=H)
            eqv = eq.rearrange("p (g c) -> p g c", c=NC)

            def front(i, k):
                n = [0]

                def step(ins):
                    n[0] += 1
                    ins.then_inc(s["fch"], 1)
                    held(dve, s["fch"], FCH * i + n[0])
                held(dve, s["fr_se"], i + 1)
                for r in range(16):
                    last = V.max(Av[:, r, 0:8], simv[:, r, :])
                step(last)
                for r in range(16):
                    V.match_replace(tmpv[:, r, :], Av[:, r, 0:8], simv[:, r, :], NEG)
                for r in range(16):
                    last = V.max_index(Iv[:, r, 0:8], Av[:, r, 0:8], simv[:, r, :])
                step(last)
                for r in range(16):
                    last = V.max(Av[:, r, 8:16], tmpv[:, r, :])
                step(last)
                for r in range(16):
                    last = V.max_index(Iv[:, r, 8:16], Av[:, r, 8:16], tmpv[:, r, :])
                step(last)
                V.tensor_copy(If[:, 0:128], Iu[:, 0:128])
                step(V.tensor_scalar(If[:, 128:256], Iu[:, 128:256], float(NK), None, ALU.mult))
                for dst, src in ((candv, Av), (payv, Ifv)):
                    o = 0
                    for a, b, m in CAND:
                        shape = [128, H, b - a, m]
                        last = V.tensor_tensor(dst[:, :, o:o + (b - a) * m].rearrange("p h (i j) -> p h i j", j=m),
                                               src[:, 0:8, a:b].unsqueeze(3).to_broadcast(shape),
                                               src[:, 8:16, 0:m].unsqueeze(2).to_broadcast(shape), ALU.add)
                        o += (b - a) * m
                step(last)
                for h in range(H):
                    last = V.max(Vv[:, h, 0:8], candv[:, h, :])
                step(last)
                for h in range(H):
                    V.match_replace(tmp2v[:, h, :], Vv[:, h, 0:8], candv[:, h, :], NEG)
                for h in range(H):
                    last = V.max_index(posv[:, h, 0:8], Vv[:, h, 0:8], candv[:, h, :])
                step(last)
                for h in range(H):
                    last = V.max(Vv[:, h, 8:16], tmp2v[:, h, :])
                step(last)
                for h in range(H):
                    last = V.max_index(posv[:, h, 8:16], Vv[:, h, 8:16], tmp2v[:, h, :])
                step(last)
                V.tensor_copy(posf, posu)
                step(V.tensor_copy(wsum, Vv[:, :, 0]))
                V.tensor_tensor(Vv, Vv, wsum.unsqueeze(2).to_broadcast([128, H, TOPK]), ALU.subtract).then_inc(s["fdif"], 1)
                V.tensor_tensor(eqv, posf.unsqueeze(2).to_broadcast([128, 128, NC]),
                                iota.unsqueeze(1).to_broadcast([128, 128, NC]), ALU.is_equal).then_inc(s["fch"], 1)
                n[0] += 1
                held(dve, s["fch"], FCH * i + n[0])
                e4 = eq.rearrange("p (h k c) -> p h k c", h=H, k=TOPK)
                V.tensor_tensor(e4, e4, payv.unsqueeze(2).to_broadcast([128, H, TOPK, NC]), ALU.mult).then_inc(s["fch2"], 1)
                held(dve, s["fch2"], 3 * i + 1)
                V.tensor_reduce(pick, eqv, AX.X, ALU.add).then_inc(s["fch2"], 1)
                held(dve, s["fch2"], 3 * i + 2)
                V.tensor_tensor(rowidx[:, k * 128:k * 128 + 128], pick, rowbase, ALU.add).then_inc(s["idx"], 1)
                w = wt[:, k * 128:k * 128 + 128].rearrange("p (h k) -> p h k", h=H)
                held(dve, s["fexp"], i + 1)
                V.tensor_reduce(wsum, w, AX.X, ALU.add).then_inc(s["fch2"], 1)
                held(dve, s["fch2"], 3 * i + 3)
                V.reciprocal(wsum, wsum).then_inc(s["fch3"], 1)
                held(dve, s["fch3"], 2 * i + 1)
                V.tensor_tensor(w, w, wsum.unsqueeze(2).to_broadcast([128, H, TOPK]), ALU.mult).then_inc(s["fch3"], 1)
                assert n[0] == FCH, n[0]

            def back(i, k):
                held(dve, s["fch3"], 2 * i + 2)
                w = wt[:, k * 128:k * 128 + 128].rearrange("p (h k) -> p h k", h=H)
                for h in range(H):
                    held(dve, slot[h % 4], 256 * (2 * i + h // 4) + 256)
                    kv = KV[:, (h % 4) * 2048:(h % 4) * 2048 + 2048]
                    V.tensor_tensor(prodt.rearrange("p (k d) -> p k d", k=TOPK), kv.rearrange("p (k d) -> p k d", k=TOPK),
                                    w[:, h, :].unsqueeze(2).to_broadcast([128, TOPK, 128]), ALU.mult).then_inc(s["bch"], 1)
                    held(dve, s["bch"], BCH * i + 2 * h + 1)
                    V.tensor_reduce(KVs.rearrange("p (c h d) -> p c h d", c=2, h=H)[:, :, h, :],
                                    prodt.rearrange("p (k c d) -> p c d k", k=TOPK, c=2), AX.X, ALU.add).then_inc(s["bch"], 1)
                    held(dve, s["bch"], BCH * i + 2 * h + 2)
                scv = sc.rearrange("p (h j) -> p h j", h=H)
                for c in range(2):
                    held(dve, s["sm_p"], i + 1)
                    last = V.tensor_tensor(scv[:, 4 * c:4 * c + 4], bank[5 + c][:, :].rearrange("p (h j) -> p h j", h=4),
                                           causal.unsqueeze(1).to_broadcast([128, 4, 128]), ALU.add)
                last.then_inc(s["bch"], 1)
                held(dve, s["bch"], BCH * i + 2 * H + 1)
                V.tensor_reduce(mx, scv, AX.X, ALU.max).then_inc(s["b2"], 1)
                held(dve, s["b2"], 10 * i + 1)
                V.tensor_tensor(scv, scv, mx.unsqueeze(2).to_broadcast([128, H, 128]), ALU.subtract).then_inc(s["bdif"], 1)
                held(dve, s["bexp"], i + 1)
                V.tensor_reduce(sm, scv, AX.X, ALU.add).then_inc(s["b2"], 1)
                held(dve, s["b2"], 10 * i + 2)
                V.reciprocal(sm, sm).then_inc(s["b2"], 1)
                held(dve, s["b2"], 10 * i + 3)
                V.tensor_tensor(scv, scv, sm.unsqueeze(2).to_broadcast([128, H, 128]), ALU.mult).then_inc(s["aw"], 1)
                held(dve, s["wo_p"], i + 1)
                V.tensor_tensor(res, hsv(k), bank[7][:, 0:64], ALU.add).then_inc(s["b2"], 1)
                held(dve, s["b2"], 10 * i + 4)
                V.tensor_reduce(rv[:, 0:1], res, AX.X, ALU.add).then_inc(s["b2"], 1)
                held(dve, s["b2"], 10 * i + 5)
                V.tensor_scalar(rv[:, 0:1], rv[:, 0:1], 1.0 / D, None, ALU.mult).then_inc(s["b2"], 1)
                held(dve, s["b2"], 10 * i + 6)
                V.tensor_scalar(rc, res, rv[:, 0:1], None, ALU.subtract).then_inc(s["b2"], 1)
                held(dve, s["b2"], 10 * i + 7)
                V.tensor_tensor(rq, rc, rc, ALU.mult).then_inc(s["b2"], 1)
                held(dve, s["b2"], 10 * i + 8)
                V.tensor_reduce(rv[:, 2:3], rq, AX.X, ALU.add).then_inc(s["b2"], 1)
                held(dve, s["b2"], 10 * i + 9)
                V.tensor_scalar(rv[:, 0:1], rv[:, 2:3], 1.0 / D, 1e-5, ALU.mult, ALU.add).then_inc(s["rvv"], 1)
                held(dve, s["rst"], i + 1)
                V.reciprocal(rv[:, 3:4], rv[:, 1:2]).then_inc(s["b2"], 1)
                held(dve, s["b2"], 10 * i + 10)
                held(dve, s[f"out{k}"], 8 * (i - k) + 1)
                V.tensor_scalar(yt[:, k * 64:k * 64 + 64], rc, rv[:, 3:4], None, ALU.mult).then_inc(s["done"], 1)
            schedule(dve, front, back)

        def gpsimd_program(pool):

            def tile(i, k):
                held(pool, s["idx"], i + 1)
                for h in range(H):
                    if h >= 4:
                        held(pool, s["bch"], BCH * i + 2 * (h - 4) + 1)
                    elif isinstance(i, int):
                        held(pool, s["bch"], BCH * (i - 1) + 2 * (h + 4) + 1) if i else None
                    else:
                        held(pool, s["bch"], BCH * (i - 1) + 2 * (h + 4) + 1)
                    for j in range(TOPK):
                        n = k * 128 + h * TOPK + j
                        nc.gpsimd.indirect_dma_start(KV[:, (h % 4) * 2048 + j * 128:(h % 4) * 2048 + j * 128 + 128], None, T["kvtab"],
                                                     bass.IndirectOffsetOnAxis(ap=rowidx[:, n:n + 1], axis=0)).then_inc(slot[h % 4], 16)
            tile(0, 0)
            with pool.Fori(0, BP // 2 - 1) as ii:
                for k in range(2):
                    tile(2 * ii + k + 1, 1 - k)
            tile(BP - 1, 1)
        return sync_program, tensor_program, scalar_program, vector_program, gpsimd_program


ARENA = 50000


def vision_tower(nc, T, out):
    ctx = ExitStack()
    with ctx:
        arena = ctx.enter_context(nc.sbuf_tensor("arena", [128, ARENA], F32))
        hT = ctx.enter_context(nc.sbuf_tensor("h_transposed", [128, BP * S], F32))[:, :]
        ident = ctx.enter_context(nc.sbuf_tensor("identity", [128, 128], F32))[:, :]
        bank = [ctx.enter_context(nc.psum_tensor(f"bank{i}", [128, 512], F32)) for i in range(8)]
        *first, h_ready = token_mixer(nc, ctx, T, arena, bank, hT, ident)
        second = token_and_channel_mixers(nc, ctx, T, out, arena, bank, hT, ident, h_ready)
        block = ctx.enter_context(nc.Block())

        @block.sync
        def _(sp):
            first[0](sp)
            second[0](sp)

        @block.tensor
        def _(pe):
            first[1](pe)
            second[1](pe)

        @block.scalar
        def _(act):
            first[2](act)
            second[2](act)

        @block.vector
        def _(dve):
            first[3](dve)
            second[3](dve)

        @block.gpsimd
        def _(pool):
            first[4](pool)
            second[4](pool)


def kernel(**inputs):
    import concourse.bacc as bacc
    from concourse.bass_utils import run_bass_kernel_spmd

    x = {k: np.asarray(v) for k, v in inputs.items()}
    arrays = {**host_constants(), **ffn_constants(),
              **host_layout(**{k: v for k, v in x.items() if k == "x" or k.startswith("L0_tok")}),
              **ffn_layout(**{k: v for k, v in x.items() if not (k == "x" or k.startswith("L0_tok"))})}
    nc = bacc.Bacc("TRN2", target_bir_lowering=False, num_devices=1)
    T = {k: nc.dram_tensor(f"in_{k}", v.shape, mybir.dt.from_np(v.dtype), kind="ExternalInput").ap() for k, v in arrays.items()}
    out = nc.dram_tensor("out", (BP, 128, D), F32, kind="ExternalOutput").ap()
    vision_tower(nc, T, out)
    r = run_bass_kernel_spmd(nc, [{f"in_{k}": v for k, v in arrays.items()}], core_ids=[0])
    return r.results[0]["out"].reshape(B, S, S)
```

```python
import numpy as np
import concourse.bass as bass
from concourse import mybir
from contextlib import ExitStack

F32 = mybir.dt.float32
U32 = mybir.dt.uint32
ALU = mybir.AluOpType
ACT = mybir.ActivationFunctionType
AX = mybir.AxisListType

B, S, C, L, MODES, MID = 64, 64, 32, 4, 12, 4
K1, K2 = 2 * MODES, MODES
NB = 16
CH = B // NB
BP = B // 2
TC = NB // 2
NM = MODES * K2
D = 64
N = 256
H, NK, TOPK, DK = 8, 64, 16, 32
DECAY = 0.97
NEG = -3.0e38
CAND = [(0, 1, 16), (1, 2, 8), (2, 3, 5), (3, 4, 4), (4, 5, 3), (5, 8, 2), (8, 16, 1)]
NC = sum((b - a) * n for a, b, n in CAND)
FILLS = [(m, x, min(3, 16 - x) if x < 12 else 2) for m in range(2) for x in (0, 3, 6, 9, 12, 14)]


def host_constants():
    f = np.float64
    kx = np.concatenate([np.arange(MODES), np.arange(S - MODES, S)]).astype(f)
    ky = np.arange(K2).astype(f)
    pos = np.arange(S).astype(f)
    cx = np.cos(2 * np.pi * np.outer(kx, pos) / S)
    sx = np.sin(2 * np.pi * np.outer(kx, pos) / S)
    cy = np.cos(2 * np.pi * np.outer(ky, pos) / S)
    sy = np.sin(2 * np.pi * np.outer(ky, pos) / S)
    two = np.eye(2)
    half_ri_kx = np.stack([cx.reshape(2, MODES, S), -sx.reshape(2, MODES, S)], 1).reshape(2 * K1, S)
    inv_x = np.kron(two, half_ri_kx)
    alpha = np.where(ky == 0, 1.0, 2.0)[:, None] / S
    inv_y = np.stack([alpha * cy, -alpha * sy])
    inv_y = np.einsum("vky,bc->vkbcy", inv_y, np.eye(4)).reshape(2 * K2 * 4, 4 * S)
    fwd_y = np.stack([cy, -sy]).transpose(2, 0, 1).reshape(S, 2 * K2)
    fwd_y = np.kron(two, fwd_y)
    re_part = np.stack([cx.T, -sx.T], 1) / S
    im_part = np.stack([sx.T, cx.T], 1) / S
    fwd_x0 = np.stack([a.reshape(S, 2 * K1) for a in (re_part, im_part)])
    fwd_x = np.stack([np.kron(two, a).reshape(2, S, 4 * K1).transpose(1, 0, 2).reshape(2 * S, 4 * K1) for a in fwd_x0])
    ri = (np.arange(128) // 32) % 2
    sign = np.stack([np.where(ri == 0, 1.0, -1.0), np.where(ri == 0, -1.0, 1.0)], 1)
    px = (np.arange(128) // 32)[:, None]
    pmask = (px == (np.arange(16) // MID)[None, :]).astype(f)
    grid = np.linspace(0.0, 1.0, S)
    fx = lambda img: _dft(img, kx, ky)
    feats = [None, fx(np.repeat(grid[:, None], S, 1)), fx(np.repeat(grid[None, :], S, 0)), fx(np.ones((S, S)))]
    e = np.zeros((2, 2, 4, NB // 8, MODES, 8, K2))
    for n in (1, 2, 3):
        z = feats[n].reshape(2, MODES, K2)
        e[:, 0, n] = z.real[:, None, :, None, :]
        e[:, 1, n] = z.imag[:, None, :, None, :]
    gridc = np.concatenate([np.tile(grid, 2)[:, None], np.tile(grid[None, :], (128, 1))], 1)
    out = dict(inv_x=inv_x, inv_y=inv_y, fwd_y=fwd_y, fwd_x=fwd_x, fwd_x0=fwd_x0, sign=sign, pmask=pmask,
               e_const=e.reshape(16, NB * NM), gridc=gridc)
    return {k: np.ascontiguousarray(v.astype(np.float32)) for k, v in out.items()}


def _dft(img, kx, ky):
    pos = np.arange(S)
    return np.exp(-2j * np.pi * np.outer(kx, pos) / S) @ img @ np.exp(-2j * np.pi * np.outer(pos, ky) / S) / S


def host_layout(x, L0_tok_p_w, L0_tok_p_b, L0_tok_fw, L0_tok_w1_w, L0_tok_w1_b, L0_tok_w2_w, L0_tok_w2_b,
                L0_tok_q1_w, L0_tok_q1_b, L0_tok_q2_w, L0_tok_q2_b):
    a = {}
    a["xt"] = x[..., 0].reshape(BP, 2, S, S).transpose(1, 3, 0, 2).reshape(128, BP * S)
    fw = L0_tok_fw.transpose(0, 1, 6, 2, 4, 5, 3).reshape(L, 2, 2, C, MODES * K2, C)
    a["fwt"] = np.stack([np.stack([fw[:, :, 0], fw[:, :, 1]], 4), np.stack([fw[:, :, 1], fw[:, :, 0]], 4)], 2)\
        .reshape(L, 128, MODES * K2 * 2 * C)
    w1 = np.zeros((L, 2, 4, C, 4, C), np.float32)
    w2 = np.zeros((L, 4, C, 4, C), np.float32)
    for q in range(4):
        w1[:, 0, q, :, q] = L0_tok_w1_w.transpose(0, 2, 1)
        w1[:, 1, q, :, q ^ 1] = L0_tok_w1_w.transpose(0, 2, 1)
        w2[:, q, :, q] = L0_tok_w2_w.transpose(0, 2, 1)
    a["w1bd"] = w1.reshape(L, 2, 128, 128).transpose(0, 2, 1, 3).reshape(L, 128, 256)
    a["w2bd"] = w2.reshape(L, 128, 128)
    a["w2rep"] = np.tile(L0_tok_w2_w, (1, 1, 4))
    bias = np.zeros((L, 4, C, 3), np.float32)
    bias[:, 0, :, 0] = L0_tok_w1_b
    bias[:, 1, :, 1] = L0_tok_w1_b
    bias[:, 0, :, 2] = L0_tok_w2_b
    a["dcbias"] = bias.reshape(L, 128, 3)[:, :, 0:2]
    a["b2col"] = bias.reshape(L, 128, 3)[:, :, 2:3]
    pw = np.concatenate([L0_tok_p_w, L0_tok_p_b[:, None]], 1)
    p0 = np.zeros((4, 4, 4, C), np.float32)
    for q in range(4):
        p0[q, :, q] = pw.T
    a["p0"] = p0.reshape(16, 128)
    a["tail"] = np.concatenate([pw, L0_tok_q1_w.T, L0_tok_w2_b.T], 1)
    a["tailb"] = np.tile(np.concatenate([L0_tok_q1_b, L0_tok_q2_w[0], L0_tok_q2_b])[None], (128, 1))
    return {k: np.ascontiguousarray(v) for k, v in a.items()}


def ffn_constants():
    s, t = np.meshgrid(np.arange(S), np.arange(S), indexing="ij")
    decay = np.where(s < t, DECAY ** np.maximum(t - 1 - s, 0).astype(np.float64), 0.0)
    i, j = np.meshgrid(np.arange(128), np.arange(128), indexing="ij")
    causal = np.where((i // S == j // S) & (j <= i), 0.0, NEG)
    rowbase = np.tile((np.repeat(np.arange(H), TOPK) * NK * NK)[None], (128, 1))
    iota = np.tile(np.arange(NC)[None], (128, 1))
    return dict(masks=np.concatenate([np.tile(decay, (2, 1)), causal, rowbase, iota], 1).astype(np.float32))


def ffn_layout(L0_attn_E, L0_attn_Dx, L0_attn_Dy, L0_ffn_Wq_pk, L0_ffn_pk_keys, L0_ffn_Wq, L0_ffn_keys_table,
               L0_ffn_values_table, L0_ffn_Wo):
    a = dict(
        dxt=np.tile(L0_attn_Dx.T, (2, 1)), dyt=L0_attn_Dy.T,
        et=L0_attn_E.T.reshape(2, 128, D).transpose(1, 0, 2).reshape(128, 2 * D),
        wqpk=L0_ffn_Wq_pk.reshape(D, 2 * H, DK).transpose(2, 1, 0).reshape(DK, 2 * H * D),
        pkk=L0_ffn_pk_keys.transpose(3, 0, 2, 1).reshape(DK, 2 * H * NK),
        wq=L0_ffn_Wq, wo=L0_ffn_Wo.reshape(4, 128, D).transpose(1, 0, 2).reshape(128, 4 * D),
        kvtab=np.concatenate([L0_ffn_keys_table, L0_ffn_values_table], 1))
    return {k: np.ascontiguousarray(v) for k, v in a.items()}



ARENA = 53100


def vision_tower(nc, T, out):
    ctx = ExitStack()
    with ctx:
        arena = ctx.enter_context(nc.sbuf_tensor("arena", [128, ARENA], F32))
        bank = [ctx.enter_context(nc.psum_tensor(f"bank{i}", [128, 512], F32)) for i in range(8)]
        TB, RB, PB, FB = bank[0:2], bank[2:4], bank[4], bank[5:8]
        gd = nc.dram_tensor("modes_mixed", (128, MODES, 4 * 96), F32, kind="Internal").ap()
        fr = nc.dram_tensor("modes_relu", (2, 96, 16, 96), F32, kind="Internal").ap()
        fx = nc.dram_tensor("modes_x", (2 * K1, B * K2), F32, kind="Internal").ap()

        used = [0]

        def sb(cols, rows=128):
            used[0] += cols
            assert used[0] <= ARENA, used[0]
            return arena[0:rows, used[0] - cols:used[0]]
        Wt = sb(NM * 2 * C)
        St = sb(NB * NM)
        Dt = sb(16 * 192, 96)
        TG = sb(2048)
        Tt = TG[0:96]
        Gc = TG[:, 0:768]
        Ft = sb(16 * 96, 96)
        Pt = sb(TC * S * MID)
        scratch = sb(4096 + 4096 + 1536)
        Rt = scratch[:, 0:4096]
        Yt = scratch[:, 4096:8192]
        Qt = scratch[:, 8192:9728]
        Gp = scratch[:, 4096:4096 + MODES * 384]
        FRt = scratch[:, 0:NB * NM]
        Et = scratch[0:16, 0:NB * NM]
        hTc, h1 = sb(512), sb(512)
        xc = hTc
        Pj = hTc
        invx, invy, fwdy, fwdx = sb(128, 96), sb(256, 96), sb(48), sb(192)
        sign, pmask, gridc, ones = sb(2), sb(16), sb(65), sb(128)
        ipw = sb(144)
        ident, pw = ipw[:, 0:128], ipw[:, 128:144]
        w1t, w2t, w2r, dcb, b2c = sb(256), sb(128), sb(128, 32), sb(2), sb(1)
        p0, tail, tailb = sb(128, 16), sb(12, 32), sb(9)
        prod, cf, t4, base = sb(16, 32), sb(16), sb(4), sb(256)
        b2sum = sb(1, 32)
        X = scratch[:, 0:2048]
        nsum, cc, dd = (scratch[:, 2048 + k * 1024:3072 + k * 1024] for k in range(3))
        htok, lnv, gm, la, sq = (scratch[:, 5120 + k * 512:5632 + k * 512] for k in range(5))
        laT = scratch[0:64, 7680:8704]
        st, mean, var = sb(16), sb(8), sb(8)
        dxt, dyt, et = sb(256), sb(256, 64), sb(128)
        simw, wq, wo = sb(1024, 64), sb(512, 64), sb(256)
        masks = sb(320 + NC)
        decay, causal, rowbase, iota = masks[:, 0:64], masks[:, 64:192], masks[:, 192:320], masks[:, 320:320 + NC]
        sim, A, If = sb(1024), sb(256), sb(256)
        Iu = If.bitcast(U32)
        cand, pay = sb(H * NC), sb(H * NC)
        Vt, posf, pick, best = sb(128), sb(128), sb(128), sb(8)
        posu = posf.bitcast(U32)
        rowidx = sb(256).bitcast(U32)
        wt, qT, hs, hsT, wsum = sb(256), sb(1024), sb(128), sb(128, 64), sb(8)
        KV = sb(4 * 2048)
        kT = sb(512)
        eq = sb(64 * NC)
        sc, at, KVs = eq[:, 0:1024], eq[:, 1024:2048], eq[:, 2048:3072]
        ao, aoT = sc[:, 0:512], kT
        mx, sm, res, rc, rq, rv, yt = sb(8), sb(8), sb(64), sb(64), sb(64), sb(4), sb(128)
        wqpk, pkk = scratch[0:32, 4096:5120], scratch[0:32, 5120:6144]
        x_all = scratch[:, 0:2048]
        xq = scratch[0:64, 6144:6144 + 1536]
        xm = scratch[0:48, 7680:7680 + 768]
        fwdx0 = scratch[0:64, 8448:8448 + 96]

        names = """const xload wld fxp fxq fxf fxs fxst swp swe cff prodd cfd base_d eload xcl s0f s0e s_rdy pinit
            w_in wa_in wb_in wfix w1fix dcfix pwf pw_e mixf g_e w1f gp_e gst drdy i1 t_e i2 r_e pf p_e xf x_e qf q_e ff f_e fst
            frt upf upd_e h_d xu_p xu_e cs_p cn th_p th_e rec cd gr_p gr_e a_p ln_in ln_out lt_p lt_e lnv_d la_d yc_p yc_e v_p h1ok
            fr_h fr_t fr_hT fr_s fr_se fr_q fr_qe b2f fch fdif fexp idx wch bch kt_p kt_e sm_p bdif bexp aw at_p at_e av_p av_e
            ot_p ot_e wo_p res_d lch rvv rst done out0 out1 id one passed""".split()
        s = {n: ctx.enter_context(nc.semaphore(n)) for n in names}
        slot = [ctx.enter_context(nc.semaphore(f"slot{i}")) for i in range(4)]
        CREDIT = ("i1", "f_e", "fst", "p_e", "res_d", "out0", "out1")
        NCONST = 22

        def held(eng, name, v):
            eng.wait_ge(s[name] if isinstance(name, str) else name, v)
            eng.sem_inc(s["passed"], 1)

        def schedule(eng, p):
            part = lambda name: p.get(name, lambda *a: None)
            begin, spectrum, space, update, recur = (part(n) for n in ("begin", "spectrum", "space", "update", "recur"))
            front, weigh, back = part("front"), part("weigh"), part("back")
            begin(0)
            with eng.Fori(0, L - 1) as l:
                spectrum(l, l)
                space(l, l, (0,))
                space(l, l, (1, 2, 3))
                update(l, l)
            spectrum(L - 1, None)
            space(L - 1, None, (0,))
            space(L - 1, None, (1, 2, 3))
            recur(0)
            front(0, 0, 0, 1)
            weigh(0, 0)
            with eng.Fori(0, CH - 1) as c:
                begin(c + 1)
                with eng.Fori(0, L - 1) as l:
                    i, lam, mu = TC * c + 2 * l, L * c + L + l, (L - 1) * c + (L - 1) + l
                    front(i + 1, 1, 2 * l + 1, c + 1)
                    spectrum(lam, mu, l)
                    space(lam, mu, (0,))
                    weigh(i + 1, 1)
                    back(i, 0, i + 2)
                    front(i + 2, 0, 2 * l + 2, c + 1)
                    space(lam, mu, (1, 2, 3))
                    weigh(i + 2, 0)
                    back(i + 1, 1, i + 3)
                    update(lam, mu, l)
                i, lam = TC * c + TC - 2, L * c + 2 * L - 1
                front(i + 1, 1, TC - 1, c + 1)
                spectrum(lam, None)
                space(lam, None, (0,))
                space(lam, None, (1, 2, 3))
                weigh(i + 1, 1)
                back(i, 0, i + 2)
                recur(c + 1)
                front(i + 2, 0, 0, c + 2)
                weigh(i + 2, 0)
                back(i + 1, 1, i + 3)
            i = BP - TC
            with eng.Fori(0, TC // 2 - 1) as n:
                front(i + 2 * n + 1, 1, 2 * n + 1, CH)
                weigh(i + 2 * n + 1, 1)
                back(i + 2 * n, 0, i + 2 * n + 2)
                front(i + 2 * n + 2, 0, 2 * n + 2, CH)
                weigh(i + 2 * n + 2, 0)
                back(i + 2 * n + 1, 1, i + 2 * n + 3)
            front(BP - 1, 1, TC - 1, CH)
            weigh(BP - 1, 1)
            back(BP - 2, 0, BP)
            back(BP - 1, 1, BP)

        block = ctx.enter_context(nc.Block())

        @block.sync
        def _(sp):
            for n in CREDIT:
                sp.sem_inc(s[n], 1)
            sp.dma_start(x_all, T["xt"]).then_inc(s["xload"], 16)
            for dst, n in ((fwdy, "fwd_y"), (fwdx[:, 0:96], 0), (fwdx[:, 96:192], 1), (sign, "sign"), (pmask, "pmask"),
                           (gridc, "gridc"), (p0, "p0"), (tail, "tail"), (tailb, "tailb"), (invx, "inv_x"), (invy, "inv_y"),
                           (masks[:, 0:320 + NC], "masks"), (dxt, "dxt"), (dyt, "dyt"), (et, "et"), (wqpk, "wqpk"), (pkk, "pkk"),
                           (wq, "wq"), (wo, "wo")):
                sp.dma_start(dst, T["fwd_x"][n] if isinstance(n, int) else T[n]).then_inc(s["const"], 16)
            for n in range(2):
                sp.dma_start(fwdx0[:, n * 48:n * 48 + 48], T["fwd_x0"][n]).then_inc(s["const"], 16)
            sp.dma_start(xc, T["xt"][:, 0:512]).then_inc(s["const"], 16)
            one = lambda name, l: T[name][bass.ds(l, 1)].rearrange("a p c -> (a p) c")

            def weights(l):
                sp.dma_start(Wt, one("fwt", l)).then_inc(s["w_in"], 16)
                for dst, n in ((w1t, "w1bd"), (dcb, "dcbias"), (w2r, "w2rep")):
                    sp.dma_start(dst, one(n, l)).then_inc(s["wa_in"], 16)

            def begin(c):
                if isinstance(c, int):
                    weights(0)
                    sp.wait_ge(s["fxs"], 2)
                    sp.dma_start(fx, xm).then_inc(s["fxst"], 16)
                    sp.wait_ge(s["fxst"], 16)
                else:
                    held(sp, "h1ok", c)
                    weights(0)
                    sp.dma_start(xc, T["xt"][:, bass.ds(c * 512, 512)]).then_inc(s["xcl"], 16)
                sp.dma_start(Et, T["e_const"]).then_inc(s["eload"], 16)
                held(sp, "eload", 80 * c + 16)
                for n in range(4):
                    r0 = ((n % 2) * 2 + n // 2) * MODES
                    sp.dma_start(Et[n * 4:n * 4 + 1, :].rearrange("p (g k c) -> p g k c", g=2, k=MODES),
                                 fx[r0:r0 + MODES, bass.ds(c * NB * K2, NB * K2)].rearrange("k (a g c) -> a g k c", a=1, g=2))\
                        .then_inc(s["eload"], 16)

            def spectrum(lam, mu, l=None):
                for f in range(6):
                    held(sp, "gp_e", 24 * lam + 4 * f + 4)
                    sp.dma_start(gd[:, 2 * f:2 * f + 2, :], Gp[:, f * 768:f * 768 + 768].rearrange("p (k c) -> p k c", k=2))\
                        .then_inc(s["gst"], 16)
                held(sp, "gst", 96 * lam + 96)

            def modes_in(lam, g):
                held(sp, "i1", 8 * (2 * lam + g) + 1)
                for q in range(2):
                    for n in range(4):
                        sp.dma_start(Dt[(q * 4 + n) * MODES:(q * 4 + n + 1) * MODES, :].rearrange("k (s c) -> k s c", s=16),
                                     gd[n * 32 + q * 16:n * 32 + q * 16 + 16, :, g * 192:g * 192 + 192]
                                     .rearrange("s k c -> k s c")).then_inc(s["drdy"], 16)

            def space(lam, mu, subs):
                g = len(subs) // 2
                modes_in(lam, g)
                if mu is None or g == 0:
                    return
                l = mu_layer[0]
                weights(l + 1)
                sp.dma_start(w2t, one("w2bd", l)).then_inc(s["wb_in"], 16)
                sp.dma_start(b2c, one("b2col", l)).then_inc(s["wb_in"], 16)
                for g in range(2):
                    held(sp, "f_e", 4 * (2 * mu + g) + 4 + 1)
                    sp.dma_start(fr[g].rearrange("p o c -> p (o c)"), Ft).then_inc(s["fst"], 16)

            def update(lam, mu, l=None):
                held(sp, "fst", 16 * (2 * mu + 2) + 1)
                for g in range(2):
                    for q in range(2):
                        for ri in range(2):
                            for hf in range(2):
                                r0, d0 = ((q * 2 + ri) * 2 + hf) * MODES, hf * 64 + ri * 32 + q * 16
                                sp.dma_start(FRt[d0:d0 + 16, g * 1152:g * 1152 + 1152].rearrange("p (k c) -> p k c", k=MODES),
                                             fr[g, r0:r0 + MODES, :, :].rearrange("k o c -> o k c")).then_inc(s["frt"], 16)

            mu_layer = [None]

            def spectrum_(lam, mu, l=None):
                mu_layer[0] = lam if l is None else l
                spectrum(lam, mu)

            def back(i, k, fronts):
                held(sp, "done", i + 1)
                sp.dma_start(out[bass.ds(i, 1)].rearrange("a p d -> (a p) d"), yt[:, k * 64:k * 64 + 64]).then_inc(s[f"out{k}"], 16)
            schedule(sp, dict(begin=begin, spectrum=spectrum_, space=space, update=update, back=back))
            sp.wait_ge(s["out0"], 16 * (BP // 2) + 1)
            sp.wait_ge(s["out1"], 16 * (BP // 2) + 1)

        @block.tensor
        def _(pe):
            mm, tr = nc.tensor.matmul, nc.tensor.transpose
            Wv = Wt.rearrange("p (m r) -> p m r", m=NM)
            Sv = St.rearrange("p (g k b y) -> p g k b y", g=2, k=MODES, b=8)
            Dv = Dt.rearrange("p (s u c) -> p s u c", s=16, u=2)
            Yv = Yt.rearrange("p (m z o) -> p m z o", m=2, o=16)
            Qv = Qt.rearrange("p (m o b r y) -> p m r o b y", m=2, o=16, b=2, r=2)

            def start():
                pe.wait_ge(s["const"], 16 * NCONST)
                for f in range(2):
                    for k in range(8):
                        r = (f * 8 + k) * 64
                        last = mm(FB[f][0:64, k * 64:k * 64 + 64], wqpk[:, r:r + 64], pkk[:, r:r + 64], start=True, stop=True)
                    last.then_inc(s["swp"], 1)
                pe.wait_ge(s["xload"], 16)
                for f in range(4):
                    for k in range(8):
                        u = f * 8 + k
                        last = mm(bank[f][0:64, k * 48:k * 48 + 48], x_all[:, u * 64:u * 64 + 64], fwdy, start=True, stop=True)
                    last.then_inc(s["fxp"], 1)
                pe.wait_ge(s["prodd"], 1)
                mm(PB[:, 0:16], ones[0:32, :], prod, start=True, stop=True).then_inc(s["cff"], 1)
                xv = xq.rearrange("p (u r y) -> p u r y", r=2, y=K2)
                pe.wait_ge(s["fxq"], 4)
                for f in range(2):
                    for r in range(2):
                        last = mm(TB[f][0:48, 0:384], fwdx0[:, r * 48:r * 48 + 48], xv[:, f * 32:f * 32 + 32, r, :],
                                  start=(r == 0), stop=(r == 1))
                    last.then_inc(s["fxf"], 1)
                pe.wait_ge(s["fxs"], 2)
                pe.wait_ge(s["cfd"], 1)
                pe.wait_ge(s["id"], 2)

            def begin(c):
                if isinstance(c, int):
                    start()
                pe.wait_ge(s["eload"], 80 * c + 80)
                for n in range(6):
                    if n >= 2:
                        pe.wait_ge(s["s0e"], 6 * c + n - 1)
                    mm(TB[n % 2][:, 0:384], p0, Et[:, n * 384:n * 384 + 384], start=True, stop=True).then_inc(s["s0f"], 1)

            def spectrum(lam, mu, l=None):
                pe.wait_ge(s["wa_in"], 48 * lam + 48)
                held(pe, "p_e", 4 * lam + 1)
                mm(PB[:, 0:4], w2r, tail[:, 4:8], start=True, stop=True).then_inc(s["pwf"], 1)
                pe.wait_ge(s["s_rdy"], lam + 1)
                held(pe, "wfix", lam + 1)
                for f in range(7):
                    if f < 6:
                        if f >= 2:
                            held(pe, "g_e", 6 * lam + f - 1)
                        for k in range(24):
                            for hf in range(2):
                                p = slice(64 * hf, 64 * hf + 64)
                                last = mm(TB[f % 2][p, k * 16:k * 16 + 16], Wv[p, f * 24 + k, :], Sv[p, :, 2 * f + k // K2, :, k % K2],
                                          start=True, stop=True)
                        last.then_inc(s["mixf"], 1)
                    if f >= 1:
                        pe.wait_ge(s["g_e"], 6 * lam + f)
                        if f == 1:
                            pe.wait_ge(s["w1fix"], lam + 1)
                        for v in range(2):
                            if f >= 2:
                                pe.wait_ge(s["gp_e"], 24 * lam + 4 * (f - 2) + 2 * v + 2)
                            mm(RB[v][:, 0:384], w1t[:, v * 128:v * 128 + 128], Gc[:, ((f - 1) % 2) * 384:((f - 1) % 2) * 384 + 384],
                               start=True, stop=True).then_inc(s["w1f"], 1)

            def x_back(lam, sub):
                u = 4 * lam + sub
                if sub % 2 == 0:
                    pe.wait_ge(s["drdy"], 128 * (2 * lam + sub // 2) + 128)
                for q in range(4):
                    if q >= 2:
                        pe.wait_ge(s["t_e"], 4 * u + q - 1)
                    for k in range(4):
                        last = mm(TB[q % 2][0:96, k * 128:k * 128 + 128], Dv[:, q * 4 + k, sub % 2, :], invx, start=True, stop=True)
                    last.then_inc(s["i1"], 1)

            def space(lam, mu, subs):
                x_back(lam, subs[0])
                for sub in subs:
                    u = 4 * lam + sub
                    pe.wait_ge(s["t_e"], 4 * u + 4)
                    if mu is not None:
                        w = 4 * mu + sub
                        pe.wait_ge(s["f_e"], 2 * w + 1)
                    for f in range(8):
                        if f >= 2:
                            pe.wait_ge(s["r_e"], 8 * u + f - 1)
                        for k in range(2):
                            xq_ = 2 * f + k
                            last = mm(RB[f % 2][:, k * 256:k * 256 + 256], Tt[:, xq_ * 128:xq_ * 128 + 128], invy, start=True, stop=True)
                        last.then_inc(s["i2"], 1)
                    pe.wait_ge(s["p_e"], u + 1)
                    pe.wait_ge(s["pw_e"], lam + 1)
                    if sub == 0:
                        pe.wait_ge(s["pinit"], (lam_chunk[0]) + 1)
                    if mu is None:
                        mm(PB[:, :], ident, Pt[:, sub * 512:sub * 512 + 512], start=True, stop=False, skip_group_check=True)
                        pe.wait_ge(s["r_e"], 8 * u + 8)
                        for k in range(32):
                            m, x_ = k // 16, k % 16
                            last = mm(PB[:, k * 16:k * 16 + 16], Rt[:, x_ * 256 + m * 128:x_ * 256 + m * 128 + 128], pw,
                                      start=False, stop=k == 31, skip_group_check=True)
                        last.then_inc(s["pf"], 1)
                        if sub != subs[-1]:
                            x_back(lam, sub + 1)
                        continue
                    pe.wait_ge(s["r_e"], 8 * u + 8)
                    for f, (m, x0, n) in enumerate(FILLS):
                        if f >= 2:
                            pe.wait_ge(s["x_e"], 12 * w + f - 1)
                        for k in range(n):
                            o = (x0 + k) * 256 + m * 128
                            last = mm(RB[f % 2][:, k * 144:k * 144 + 144], Rt[:, o:o + 128], ipw, start=True, stop=True)
                        last.then_inc(s["xf"], 1)
                    for f in range(4):
                        m = f // 2
                        if f % 2 == 0:
                            pe.wait_ge(s["x_e"], 12 * w + 6 * m + 6)
                        if f >= 2:
                            pe.wait_ge(s["q_e"], 4 * w + f - 1)
                        for k in range(8):
                            last = mm(TB[f % 2][:, k * 48:k * 48 + 48], Yv[:, m, :, (f % 2) * 8 + k], fwdy, start=True, stop=True)
                        last.then_inc(s["qf"], 1)
                    mm(PB[:, :], ident, Pt[:, sub * 512:sub * 512 + 512], start=True, stop=False)
                    mm(PB[:, :], ident, Pj, start=False, stop=True).then_inc(s["pf"], 1)
                    pe.wait_ge(s["q_e"], 4 * w + 4)
                    if sub != subs[-1]:
                        x_back(lam, sub + 1)
                    for m in range(2):
                        for r in range(2):
                            last = mm(RB[m][0:96, 0:384], fwdx[:, r * 96:r * 96 + 96], Qv[:, m, r], start=(r == 0), stop=(r == 1))
                        last.then_inc(s["ff"], 1)

            def update(lam, mu, l=None):
                pe.wait_ge(s["frt"], 256 * mu + 256)
                pe.wait_ge(s["wb_in"], 32 * mu + 32)
                pe.wait_ge(s["f_e"], 2 * (4 * mu + 4) + 1)
                for n in range(6):
                    if n >= 2:
                        pe.wait_ge(s["upd_e"], 6 * mu + n - 1)
                    cols = slice(n * 384, n * 384 + 384)
                    mm(RB[n % 2][:, 0:384], ident, St[:, cols], start=True, stop=False)
                    mm(RB[n % 2][:, 0:384], w2t, FRt[:, cols], start=False, stop=True).then_inc(s["upf"], 1)

            def recur(c):
                held(pe, "h_d", c + 1)
                B4 = TB + RB
                for f in range(4):
                    nh, b2 = f % 2, f // 2
                    mm(B4[f][:, :], dxt[64 * b2:64 * b2 + 64, nh * 128:nh * 128 + 128], hTc[64 * b2:64 * b2 + 64, :],
                       start=True, stop=True).then_inc(s["xu_p"], 1)
                held(pe, "h_d", c + 1)
                for u in range(TC):
                    for b2 in range(2):
                        p = slice(64 * b2, 64 * b2 + 64)
                        last = mm(PB[p, u * 64:u * 64 + 64], hTc[p, u * 64:u * 64 + 64], ident[p, 64 * b2:64 * b2 + 64], start=True, stop=True)
                last.then_inc(s["th_p"], 1)
                pe.wait_ge(s["one"], 1)
                pe.wait_ge(s["xu_e"], 4 * c + 4)
                for b2 in range(2):
                    for nh in range(2):
                        last = mm(TB[b2][:, :], ones, X[:, nh * 1024 + b2 * 512:nh * 1024 + b2 * 512 + 512], start=(nh == 0), stop=(nh == 1))
                    last.then_inc(s["cs_p"], 1)
                pe.wait_ge(s["cd"], c + 1)
                for u in range(TC):
                    for b2 in range(2):
                        for nh in range(2):
                            o = nh * 1024 + b2 * 512 + u * 64
                            last = mm(RB[0][64 * b2:64 * b2 + 64, u * 64:u * 64 + 64], X[:, o:o + 64], X[:, o:o + 64], start=(nh == 0), stop=(nh == 1))
                last.then_inc(s["gr_p"], 1)
                held(pe, "lnv_d", c + 1)
                held(pe, "gr_e", c + 1)
                for u in range(TC):
                    for b2 in range(2):
                        p = slice(64 * b2, 64 * b2 + 64)
                        last = mm(RB[1][p, u * 64:u * 64 + 64], gm[p, u * 64:u * 64 + 64], lnv[p, u * 64:u * 64 + 64], start=True, stop=True)
                last.then_inc(s["a_p"], 1)
                held(pe, "la_d", c + 1)
                for f in range(2):
                    for k in range(4):
                        o = (4 * f + k) * 64
                        last = tr(TB[f][0:64, k * 128:k * 128 + 128], la[:, o:o + 64], ident)
                    last.then_inc(s["lt_p"], 1)
                pe.wait_ge(s["lt_e"], 2 * c + 2)
                for f in range(4):
                    nh, b2 = f % 2, f // 2
                    mm((RB + [PB] + TB)[f][:, :], dyt[:, nh * 128:nh * 128 + 128], laT[:, b2 * 512:b2 * 512 + 512], start=True, stop=True)\
                        .then_inc(s["yc_p"], 1)
                pe.wait_ge(s["yc_e"], 4 * c + 4)
                for u in range(TC):
                    for b2 in range(2):
                        for nh in range(2):
                            o = nh * 1024 + b2 * 512 + u * 64
                            last = mm(TB[1][64 * b2:64 * b2 + 64, u * 64:u * 64 + 64], X[:, o:o + 64], et[:, nh * 64:nh * 64 + 64],
                                      start=(nh == 0), stop=(nh == 1))
                last.then_inc(s["v_p"], 1)

            def front(i, k, tile, chunks):
                held(pe, "fr_h", i + 1)
                tr(FB[0][0:64, 0:128], hs[:, k * 64:k * 64 + 64], ident).then_inc(s["fr_t"], 1)
                pe.wait_ge(s["fr_hT"], i + 1)
                if not isinstance(i, int) or i > 0:
                    pe.wait_ge(s["res_d"], i)
                for n in range(2):
                    last = mm(FB[1 + n][:, :], hsT, simw[:, n * 512:n * 512 + 512], start=True, stop=True)
                last.then_inc(s["fr_s"], 1)
                for n in range(4):
                    last = mm(FB[0][:, n * 128:n * 128 + 128], wq[:, n * 128:n * 128 + 128], hsT, start=True, stop=True)
                last.then_inc(s["fr_q"], 1)

            def back(i, k, fronts):
                held(pe, "fr_qe", fronts)
                held(pe, "bch", BCH * i + 2 * H)
                for n in range(4):
                    last = tr(FB[0][:, n * 128:n * 128 + 128], KVs[:, n * 128:n * 128 + 128], ident)
                last.then_inc(s["kt_p"], 1)
                held(pe, "kt_e", i + 1)
                for h in range(H):
                    r, m = 64 * (h % 2), h // 2
                    last = mm(FB[1 + h % 2][:, m * 128:m * 128 + 128], qT[r:r + 64, k * 512 + m * 128:k * 512 + m * 128 + 128],
                              kT[r:r + 64, m * 128:m * 128 + 128], start=True, stop=True)
                last.then_inc(s["sm_p"], 1)
                held(pe, "aw", i + 1)
                for h in range(H):
                    last = tr(FB[1 + h // 4][:, (h % 4) * 128:(h % 4) * 128 + 128], sc[:, h * 128:h * 128 + 128], ident)
                last.then_inc(s["at_p"], 1)
                pe.wait_ge(s["at_e"], i + 1)
                for h in range(H):
                    a = 4 * (h % 2) + h // 2
                    last = mm(FB[0][:, h * 64:h * 64 + 64], at[:, a * 128:a * 128 + 128], KVs[:, 512 + h * 64:512 + h * 64 + 64],
                              start=True, stop=True)
                last.then_inc(s["av_p"], 1)
                pe.wait_ge(s["av_e"], i + 1)
                for n in range(4):
                    last = tr(FB[1][:, n * 128:n * 128 + 128], ao[:, n * 128:n * 128 + 128], ident)
                last.then_inc(s["ot_p"], 1)
                pe.wait_ge(s["ot_e"], i + 1)
                for n in range(4):
                    last = mm(FB[2][:, 0:64], aoT[:, n * 128:n * 128 + 128], wo[:, n * 64:n * 64 + 64], start=(n == 0), stop=(n == 3))
                last.then_inc(s["wo_p"], 1)

            lam_chunk = [0]

            def begin_(c):
                lam_chunk[0] = c
                begin(c)
            schedule(pe, dict(begin=begin_, spectrum=spectrum, space=space, update=update, recur=recur, front=front, back=back))

        @block.scalar
        def _(act):
            A_ = nc.scalar.activation

            def cp(o, i, f=ACT.Copy, **kw):
                return A_(o, i, f, **kw)
            Wn = Wt.rearrange("p (m r o) -> p m r o", m=NM, r=2)
            Gpv = Gp.rearrange("p (k u v y b) -> p k u v y b", k=MODES, u=4, v=2, y=K2)
            Tv = Tt.rearrange("p (x j s) -> p s j x", x=S, j=2)
            Fv = Ft.rearrange("p (o b y) -> p o b y", o=16, b=8)

            def begin(c):
                if isinstance(c, int):
                    for f in range(2):
                        act.wait_ge(s["swp"], f + 1)
                        cp(simw[:, f * 512:f * 512 + 512], FB[f][0:64, :])
                    for f in range(4):
                        act.wait_ge(s["fxp"], f + 1)
                        cp(xq[:, f * 384:f * 384 + 384], bank[f][0:64, 0:384]).then_inc(s["fxq"], 1)
                    for f in range(2):
                        act.wait_ge(s["fxf"], f + 1)
                        cp(xm[:, f * 384:f * 384 + 384], TB[f][0:48, 0:384]).then_inc(s["fxs"], 1)
                for n in range(6):
                    act.wait_ge(s["s0f"], 6 * c + n + 1)
                    cp(St[:, n * 384:n * 384 + 384], TB[n % 2][:, 0:384]).then_inc(s["s0e" if n < 5 else "s_rdy"], 1)
                act.sem_inc(s["s0e"], 1)

            def spectrum(lam, mu, l=None):
                act.wait_ge(s["wa_in"], 48 * lam + 48)
                cp(w1t[:, 128:256], w1t[:, 128:256], scale=sign[:, 1:2]).then_inc(s["w1fix"], 1)
                cp(dcb[:, 0:1], dcb[:, 0:1], scale=float(S))
                cp(dcb[:, 1:2], dcb[:, 1:2], scale=-float(S)).then_inc(s["dcfix"], 1)
                act.wait_ge(s["w_in"], 16 * lam + 16)
                cp(Wn[:, :, 0, :], Wn[:, :, 0, :], scale=sign[:, 0:1]).then_inc(s["wfix"], 1)
                act.wait_ge(s["pwf"], lam + 1)
                for x4 in range(4):
                    last = cp(pw[:, x4 * 4:x4 * 4 + 4], PB[:, 0:4], scale=pmask[:, x4 * 4:x4 * 4 + 1])
                last.then_inc(s["pw_e"], 1)
                for f in range(7):
                    if f < 6:
                        act.wait_ge(s["mixf"], 6 * lam + f + 1)
                        if f >= 2:
                            act.wait_ge(s["w1f"], 12 * lam + 2 * (f - 2) + 2)
                        cp(Gc[:, (f % 2) * 384:(f % 2) * 384 + 384], TB[f % 2][:, 0:384]).then_inc(s["g_e"], 1)
                    if f >= 1:
                        for v in range(2):
                            act.wait_ge(s["w1f"], 12 * lam + 2 * (f - 1) + v + 1)
                            for kk in range(2):
                                kx = 2 * (f - 1) + kk
                                src = RB[v][:, kk * 192:kk * 192 + 192].rearrange("p (y u b) -> p y u b", y=K2, u=4)
                                dst = Gpv[:, kx, :, v].rearrange("p u y b -> p y u b")
                                if kx == 0:
                                    if v == 0:
                                        act.wait_ge(s["dcfix"], lam + 1)
                                    cp(dst[:, 0], src[:, 0], ACT.Identity, bias=dcb[:, v:v + 1])
                                    dst, src = dst[:, 1:K2], src[:, 1:K2]
                                cp(dst, src).then_inc(s["gp_e"], 1)

            def x_back(lam, sub):
                u = 4 * lam + sub
                for q in range(4):
                    act.wait_ge(s["i1"], 4 * u + q + 2)
                    cp(Tv[:, q * 4:q * 4 + 4], TB[q % 2][0:96, :].rearrange("p (s j x) -> p s j x", s=4, j=2)).then_inc(s["t_e"], 1)

            def space(lam, mu, subs):
                x_back(lam, subs[0])
                for sub in subs:
                    u = 4 * lam + sub
                    for f in range(8):
                        act.wait_ge(s["i2"], 8 * u + f + 1)
                        cp(Rt[:, f * 512:f * 512 + 512], RB[f % 2][:, :], ACT.Relu).then_inc(s["r_e"], 1)
                    if mu is None:
                        act.wait_ge(s["pf"], u + 1)
                        cp(Pt[:, sub * 512:sub * 512 + 512], PB[:, :]).then_inc(s["p_e"], 1)
                        if sub != subs[-1]:
                            x_back(lam, sub + 1)
                        continue
                    w = 4 * mu + sub
                    for f, (m, x0, n) in enumerate(FILLS):
                        act.wait_ge(s["xf"], 12 * w + f + 1)
                        both = RB[f % 2][:, 0:n * 144].rearrange("p (s c) -> p s c", s=n)
                        y0, j0 = m * 2048 + x0 * 128, m * 256 + x0 * 16
                        cp(Yt[:, y0:y0 + n * 128].rearrange("p (s c) -> p s c", s=n), both[:, :, 0:128])
                        cp(Pj[:, j0:j0 + n * 16].rearrange("p (s c) -> p s c", s=n), both[:, :, 128:144]).then_inc(s["x_e"], 1)
                    for f in range(4):
                        act.wait_ge(s["qf"], 4 * w + f + 1)
                        cp(Qt[:, f * 384:f * 384 + 384], TB[f % 2][:, 0:384]).then_inc(s["q_e"], 1)
                    act.wait_ge(s["pf"], u + 1)
                    cp(Pt[:, sub * 512:sub * 512 + 512], PB[:, :]).then_inc(s["p_e"], 1)
                    if sub != subs[-1]:
                        x_back(lam, sub + 1)
                    for m in range(2):
                        act.wait_ge(s["ff"], 2 * w + m + 1)
                        if m == 0 and sub % 2 == 0:
                            act.wait_ge(s["fst"], 16 * (2 * mu + sub // 2) + 1)
                        b = (sub % 2) * 4 + 2 * m
                        cp(Fv[:, :, b:b + 2, :], RB[m][0:96, 0:384].rearrange("p (o b y) -> p o b y", o=16, b=2)).then_inc(s["f_e"], 1)

            def update(lam, mu, l=None):
                act.wait_ge(s["wb_in"], 32 * mu + 32)
                cp(b2c, b2c, scale=float(S)).then_inc(s["b2f"], 1)
                for n in range(6):
                    act.wait_ge(s["upf"], 6 * mu + n + 1)
                    cp(St[:, n * 384:n * 384 + 384], RB[n % 2][:, 0:384]).then_inc(s["upd_e"], 1)
                act.wait_ge(s["upd_e"], 6 * mu + 6)
                act.wait_ge(s["b2f"], mu + 1)
                dc = St.rearrange("p (g k b y) -> p g k b y", g=2, k=MODES, b=8)[:, :, 0, :, 0]
                cp(dc, dc, ACT.Identity, bias=b2c).then_inc(s["s_rdy"], 1)

            def recur(c):
                B4 = TB + RB
                for f in range(4):
                    nh, b2 = f % 2, f // 2
                    act.wait_ge(s["xu_p"], 4 * c + f + 1)
                    cp(X[:, nh * 1024 + b2 * 512:nh * 1024 + b2 * 512 + 512], B4[f][:, :], ACT.Relu).then_inc(s["xu_e"], 1)
                act.wait_ge(s["th_p"], c + 1)
                cp(htok, PB[:, :]).then_inc(s["th_e"], 1)

                def root(n):
                    act.wait_ge(s["ln_in"], 4 * c + n)
                    cp(var, var, ACT.Sqrt).then_inc(s["ln_out"], 1)
                root(1)
                root(2)
                for f in range(2):
                    act.wait_ge(s["lt_p"], 2 * c + f + 1)
                    dst = laT.rearrange("p (b u t) -> p u b t", b=2, u=TC)[:, f * 4:f * 4 + 4]
                    cp(dst, TB[f][0:64, :].rearrange("p (u b t) -> p u b t", u=4, b=2)).then_inc(s["lt_e"], 1)
                root(3)
                root(4)

            def front(i, k, tile, chunks):
                act.wait_ge(s["h1ok"], chunks)
                cp(hs[:, k * 64:k * 64 + 64], h1[:, tile * 64:tile * 64 + 64] if isinstance(tile, int) else h1[:, bass.ds(tile * 64, 64)])\
                    .then_inc(s["fr_h"], 1)
                act.wait_ge(s["fr_t"], i + 1)
                cp(hsT, FB[0][0:64, 0:128]).then_inc(s["fr_hT"], 1)
                act.wait_ge(s["fr_s"], i + 1)
                for n in range(2):
                    last = cp(sim[:, n * 512:n * 512 + 512], FB[1 + n][:, :])
                last.then_inc(s["fr_se"], 1)
                act.wait_ge(s["fr_q"], i + 1)
                cp(qT[:, k * 512:k * 512 + 512], FB[0][:, :], scale=D ** -0.5).then_inc(s["fr_qe"], 1)

            def weigh(i, k):
                act.wait_ge(s["fdif"], i + 1)
                cp(wt[:, k * 128:k * 128 + 128], Vt, ACT.Exp).then_inc(s["fexp"], 1)

            def back(i, k, fronts):
                act.wait_ge(s["kt_p"], i + 1)
                cp(kT, FB[0][:, :]).then_inc(s["kt_e"], 1)
                act.wait_ge(s["bdif"], i + 1)
                cp(sc, sc, ACT.Exp).then_inc(s["bexp"], 1)
                act.wait_ge(s["at_p"], i + 1)
                for n in range(2):
                    last = cp(at[:, n * 512:n * 512 + 512], FB[1 + n][:, :])
                last.then_inc(s["at_e"], 1)
                act.wait_ge(s["av_p"], i + 1)
                cp(ao, FB[0][:, :]).then_inc(s["av_e"], 1)
                act.wait_ge(s["ot_p"], i + 1)
                cp(aoT, FB[1][:, :]).then_inc(s["ot_e"], 1)
                act.wait_ge(s["rvv"], i + 1)
                cp(rv[:, 1:2], rv[:, 0:1], ACT.Sqrt).then_inc(s["rst"], 1)

            act.wait_ge(s["const"], 16 * NCONST)
            schedule(act, dict(begin=begin, spectrum=spectrum, space=space, update=update, recur=recur, front=front, weigh=weigh, back=back))

        @block.vector
        def _(dve):
            V = nc.vector

            def start():
                V.memset(ones, 1.0).then_inc(s["one"], 1)
                dve.wait_ge(s["const"], 16 * NCONST)
                pw4, q1 = tail[:, 0:4], tail[:, 4:8]
                V.tensor_tensor(prod.rearrange("p (f m) -> p f m", f=4), pw4.unsqueeze(2).to_broadcast([32, 4, 4]),
                                q1.unsqueeze(1).to_broadcast([32, 4, 4]), ALU.mult).then_inc(s["base_d"], 1)
                V.tensor_reduce(b2sum, tail[:, 8:12], AX.X, ALU.add).then_inc(s["base_d"], 1)
                dve.wait_ge(s["base_d"], 2)
                dve.wait_ge(s["one"], 1)
                V.scalar_tensor_tensor(prod[:, 12:16], q1, b2sum[:, 0:1], prod[:, 12:16], ALU.mult, ALU.add).then_inc(s["prodd"], 1)
                dve.wait_ge(s["cff"], 1)
                V.tensor_copy(cf, PB[:, 0:16]).then_inc(s["cfd"], 1)
                dve.wait_ge(s["cfd"], 1)
                V.scalar_tensor_tensor(t4, cf[:, 8:12], gridc[:, 0:1], cf[:, 12:16], ALU.mult, ALU.add).then_inc(s["base_d"], 1)
                bv = base.rearrange("p (x m) -> p x m", m=MID)
                V.tensor_tensor(bv, gridc[:, 1:65].unsqueeze(2).to_broadcast([128, S, MID]),
                                cf[:, 4:8].unsqueeze(1).to_broadcast([128, S, MID]), ALU.mult).then_inc(s["base_d"], 1)
                dve.wait_ge(s["base_d"], 4)
                V.tensor_tensor(t4, t4, tailb[:, 0:4], ALU.add).then_inc(s["base_d"], 1)
                dve.wait_ge(s["base_d"], 5)
                V.tensor_tensor(bv, bv, t4.unsqueeze(1).to_broadcast([128, S, MID]), ALU.add).then_inc(s["base_d"], 1)
                dve.wait_ge(s["base_d"], 6)

            P4 = Pt.rearrange("p (n m) -> p n m", m=MID)
            Pb = Pt.rearrange("p (u c) -> p u c", u=TC)

            def begin(c):
                if isinstance(c, int):
                    start()
                else:
                    dve.wait_ge(s["xcl"], 16 * c)
                V.tensor_tensor(P4, xc.unsqueeze(2).to_broadcast([128, TC * S, MID]),
                                cf[:, 0:4].unsqueeze(1).to_broadcast([128, TC * S, MID]), ALU.mult).then_inc(s["wch"], 1)
                held(dve, "wch", WCH * c + 1)
                V.tensor_tensor(Pb, Pb, base.unsqueeze(1).to_broadcast([128, TC, 256]), ALU.add).then_inc(s["pinit"], 1)

            view = lambda a: a.rearrange("p (u d) -> p u d", d=D)
            wide = lambda a: a.unsqueeze(2).to_broadcast([128, TC, D])

            def recur(c):
                n = [0]

                def link(ins):
                    n[0] += 1
                    ins.then_inc(s["rec"], 1)
                    dve.wait_ge(s["rec"], NREC * c + n[0])
                roots = [0]

                def layer_norm(dst, src):
                    link(V.tensor_reduce(mean, view(src), AX.X, ALU.add))
                    link(V.tensor_scalar(mean, mean, 1.0 / D, None, ALU.mult))
                    link(V.tensor_tensor(view(dst), view(src), wide(mean), ALU.subtract))
                    link(V.tensor_tensor(sq, dst, dst, ALU.mult))
                    link(V.tensor_reduce(var, view(sq), AX.X, ALU.add))
                    V.tensor_scalar(var, var, 1.0 / D, 1e-5, ALU.mult, ALU.add).then_inc(s["ln_in"], 1)
                    roots[0] += 1
                    dve.wait_ge(s["ln_out"], 4 * c + roots[0])
                    link(V.reciprocal(var, var))
                    return V.tensor_tensor(view(dst), view(dst), wide(var), ALU.mult)
                dve.wait_ge(s["p_e"], 4 * L * (c + 1) + 1)
                link(V.scalar_tensor_tensor(P4, P4, 0.0, tailb[:, 4:8].unsqueeze(1).to_broadcast([128, TC * S, MID]), ALU.max, ALU.mult))
                link(V.tensor_reduce(hTc, P4, AX.X, ALU.add))
                V.tensor_scalar(hTc, hTc, tailb[:, 8:9], None, ALU.add).then_inc(s["h_d"], 1)
                link(V.memset(st, 0.0))
                for b2 in range(2):
                    dve.wait_ge(s["cs_p"], 2 * c + b2 + 1)
                    link(V.tensor_copy(nsum[:, b2 * 512:b2 * 512 + 512], TB[b2][:, :]))
                dve.sem_inc(s["passed"], 1)
                nv = nsum.rearrange("p (b t) -> p b t", t=S)
                with dve.Fori(0, S // 8) as t8:
                    for j in range(8):
                        dve.wait_ge(s["rec"], NREC * c + n[0] + 16 * t8 + 2 * j)
                        nt = nv[:, :, bass.ds(8 * t8 + j, 1)].rearrange("p b a -> p (b a)")
                        V.scalar_tensor_tensor(nt, st, DECAY, nt, ALU.mult, ALU.add).then_inc(s["rec"], 1)
                        dve.wait_ge(s["rec"], NREC * c + n[0] + 16 * t8 + 2 * j + 1)
                        V.tensor_scalar(st, nt, 1e12, 1.0, ALU.mult, ALU.min).then_inc(s["rec"], 1)
                n[0] += 2 * S
                dve.wait_ge(s["rec"], NREC * c + n[0])
                link(V.tensor_scalar(nsum, nsum, 1e-12, None, ALU.max))
                link(V.reciprocal(cc, nsum))
                link(V.tensor_scalar(dd, cc, DECAY, None, ALU.mult))
                link(V.memset(dd.rearrange("p (b t) -> p b t", t=S)[:, :, 0], 0.0))
                for nh in range(2):
                    xs = X[:, nh * 1024:nh * 1024 + 1024]
                    link(V.tensor_tensor(xs, xs, cc, ALU.mult))
                    last = V.tensor_tensor_scan(xs, dd, xs, 0.0, ALU.mult, ALU.add)
                    if nh == 0:
                        link(last)
                last.then_inc(s["cd"], 1)
                dve.wait_ge(s["th_e"], c + 1)
                layer_norm(lnv, htok).then_inc(s["lnv_d"], 1)
                dve.wait_ge(s["gr_p"], c + 1)
                V.tensor_tensor(view(gm), view(RB[0][:, :]), decay.unsqueeze(1).to_broadcast([128, TC, 64]), ALU.mult).then_inc(s["gr_e"], 1)
                dve.wait_ge(s["a_p"], c + 1)
                link(V.tensor_copy(la, RB[1][:, :]))
                layer_norm(la, la).then_inc(s["la_d"], 1)
                for f in range(4):
                    nh, b2 = f % 2, f // 2
                    dve.wait_ge(s["yc_p"], 4 * c + f + 1)
                    xs = X[:, nh * 1024 + b2 * 512:nh * 1024 + b2 * 512 + 512]
                    V.scalar_tensor_tensor(xs, (RB + [PB] + TB)[f][:, :], 0.0, xs, ALU.max, ALU.mult).then_inc(s["yc_e"], 1)
                dve.wait_ge(s["v_p"], c + 1)
                link(V.tensor_copy(la, TB[1][:, :]))
                link(layer_norm(la, la))
                link(V.tensor_tensor(la, la, htok, ALU.add))
                layer_norm(h1, la).then_inc(s["h1ok"], 1)
                assert n[0] == NREC, n[0]

            Av = A.rearrange("p (r k) -> p r k", r=16)
            Iv, Ifv = Iu.rearrange("p (r k) -> p r k", r=16), If.rearrange("p (r k) -> p r k", r=16)
            simv = sim.rearrange("p (r k) -> p r k", r=16)
            candv, payv = cand.rearrange("p (h c) -> p h c", h=H), pay.rearrange("p (h c) -> p h c", h=H)
            Vv, posv = Vt.rearrange("p (h k) -> p h k", h=H), posu.rearrange("p (h k) -> p h k", h=H)

            def top16(i, step, values, best_, index, rows):
                for r in range(rows):
                    last = V.max(best_[:, r, 0:8], values[:, r, :])
                step(last)
                for r in range(rows):
                    last = V.max_index(index[:, r, 0:8], best_[:, r, 0:8], values[:, r, :])
                step(last)
                for r in range(rows):
                    last = V.match_replace(values[:, r, :], best_[:, r, 0:8], values[:, r, :], NEG)
                step(last)
                for r in range(rows):
                    last = V.max(best_[:, r, 8:16], values[:, r, :])
                step(last)
                for r in range(rows):
                    last = V.max_index(index[:, r, 8:16], best_[:, r, 8:16], values[:, r, :])
                step(last)

            def front(i, k, tile, chunks):
                n = [0]

                def step(ins):
                    n[0] += 1
                    ins.then_inc(s["fch"], 1)
                    held(dve, "fch", FCH * i + n[0])
                held(dve, "fr_se", i + 1)
                top16(i, step, simv, Av, Iv, 16)
                V.tensor_copy(If[:, 0:128], Iu[:, 0:128])
                step(V.tensor_scalar(If[:, 128:256], Iu[:, 128:256], float(NK), None, ALU.mult))
                for dst, src in ((candv, Av), (payv, Ifv)):
                    o = 0
                    for a, b, m in CAND:
                        shape = [128, H, b - a, m]
                        last = V.tensor_tensor(dst[:, :, o:o + (b - a) * m].rearrange("p h (i j) -> p h i j", j=m),
                                               src[:, 0:8, a:b].unsqueeze(3).to_broadcast(shape),
                                               src[:, 8:16, 0:m].unsqueeze(2).to_broadcast(shape), ALU.add)
                        o += (b - a) * m
                step(last)
                top16(i, step, candv, Vv, posv, H)
                V.tensor_copy(posf, posu)
                step(V.tensor_copy(best, Vv[:, :, 0]))
                V.tensor_tensor(Vv, Vv, best.unsqueeze(2).to_broadcast([128, H, TOPK]), ALU.subtract).then_inc(s["fdif"], 1)
                hh = H // 2
                for z in range(2):
                    g0 = z * 64
                    eqv = eq.rearrange("p (g c) -> p g c", c=NC)
                    e4 = eq.rearrange("p (h k c) -> p h k c", h=hh, k=TOPK)
                    step(V.tensor_tensor(eqv, posf[:, g0:g0 + 64].unsqueeze(2).to_broadcast([128, 64, NC]),
                                         iota.unsqueeze(1).to_broadcast([128, 64, NC]), ALU.is_equal))
                    step(V.tensor_tensor(e4, e4, payv[:, z * hh:z * hh + hh].unsqueeze(2).to_broadcast([128, hh, TOPK, NC]), ALU.mult))
                    step(V.tensor_reduce(pick[:, g0:g0 + 64], eqv, AX.X, ALU.add))
                V.tensor_tensor(rowidx[:, k * 128:k * 128 + 128], pick, rowbase, ALU.add).then_inc(s["idx"], 1)
                assert n[0] == FCH, n[0]

            def back(i, k, fronts):
                w = wt[:, k * 128:k * 128 + 128].rearrange("p (h k) -> p h k", h=H)
                held(dve, "fexp", i + 1)
                nb = [0]

                def step(ins, name="lch", per=LCH):
                    nb[0] += 1
                    ins.then_inc(s[name], 1)
                    held(dve, name, per * i + nb[0])
                step(V.tensor_reduce(wsum, w, AX.X, ALU.add))
                step(V.reciprocal(wsum, wsum))
                step(V.tensor_tensor(w, w, wsum.unsqueeze(2).to_broadcast([128, H, TOPK]), ALU.mult))
                for h in range(H):
                    held(dve, slot[h % 4], 256 * (2 * i + h // 4) + 256)
                    kv = KV[:, (h % 4) * 2048:(h % 4) * 2048 + 2048]
                    kv3 = kv.rearrange("p (k d) -> p k d", k=TOPK)
                    V.tensor_tensor(kv3, kv3, w[:, h, :].unsqueeze(2).to_broadcast([128, TOPK, 128]), ALU.mult).then_inc(s["bch"], 1)
                    held(dve, "bch", BCH * i + 2 * h + 1)
                    V.tensor_reduce(KVs.rearrange("p (c h d) -> p c h d", c=2, h=H)[:, :, h, :],
                                    kv.rearrange("p (k c d) -> p c d k", k=TOPK, c=2), AX.X, ALU.add).then_inc(s["bch"], 1)
                scv = sc.rearrange("p (h j) -> p h j", h=H)
                held(dve, "sm_p", i + 1)
                for n in range(2):
                    last = V.tensor_tensor(scv[:, 4 * n:4 * n + 4], FB[1 + n][:, :].rearrange("p (h j) -> p h j", h=4),
                                           causal.unsqueeze(1).to_broadcast([128, 4, 128]), ALU.add)
                step(last)
                step(V.tensor_reduce(mx, scv, AX.X, ALU.max))
                V.tensor_tensor(scv, scv, mx.unsqueeze(2).to_broadcast([128, H, 128]), ALU.subtract).then_inc(s["bdif"], 1)
                held(dve, "bexp", i + 1)
                step(V.tensor_reduce(sm, scv, AX.X, ALU.add))
                step(V.reciprocal(sm, sm))
                V.tensor_tensor(scv, scv, sm.unsqueeze(2).to_broadcast([128, H, 128]), ALU.mult).then_inc(s["aw"], 1)
                held(dve, "wo_p", i + 1)
                V.tensor_tensor(res, hs[:, k * 64:k * 64 + 64], FB[2][:, 0:64], ALU.add).then_inc(s["res_d"], 1)
                held(dve, "res_d", i + 2)
                step(V.tensor_reduce(rv[:, 0:1], res, AX.X, ALU.add))
                step(V.tensor_scalar(rv[:, 0:1], rv[:, 0:1], 1.0 / D, None, ALU.mult))
                step(V.tensor_scalar(rc, res, rv[:, 0:1], None, ALU.subtract))
                step(V.tensor_tensor(rq, rc, rc, ALU.mult))
                step(V.tensor_reduce(rv[:, 2:3], rq, AX.X, ALU.add))
                V.tensor_scalar(rv[:, 0:1], rv[:, 2:3], 1.0 / D, 1e-5, ALU.mult, ALU.add).then_inc(s["rvv"], 1)
                held(dve, "rst", i + 1)
                step(V.reciprocal(rv[:, 3:4], rv[:, 1:2]))
                held(dve, f"out{k}", 8 * (i - k) + 1)
                V.tensor_scalar(yt[:, k * 64:k * 64 + 64], rc, rv[:, 3:4], None, ALU.mult).then_inc(s["done"], 1)
                assert nb[0] == LCH, nb[0]
            schedule(dve, dict(begin=begin, recur=recur, front=front, back=back))

        @block.gpsimd
        def _(pool):
            nc.gpsimd.memset(ident, 0.0).then_inc(s["id"], 1)
            pool.wait_ge(s["id"], 1)
            nc.gpsimd.affine_select(out=ident, in_=ident, compare_op=ALU.not_equal, fill=1.0, base=0,
                                    pattern=[[-1, 128]], channel_multiplier=1).then_inc(s["id"], 1)

            def tile(i, k):
                held(pool, "idx", i + 1)
                for h in range(H):
                    if h >= 4:
                        held(pool, "bch", BCH * i + 2 * (h - 4) + 2)
                    elif not isinstance(i, int) or i > 0:
                        held(pool, "bch", BCH * (i - 1) + 2 * (h + 4) + 2)
                    for j in range(TOPK):
                        n = k * 128 + h * TOPK + j
                        nc.gpsimd.indirect_dma_start(KV[:, (h % 4) * 2048 + j * 128:(h % 4) * 2048 + j * 128 + 128], None, T["kvtab"],
                                                     bass.IndirectOffsetOnAxis(ap=rowidx[:, n:n + 1], axis=0)).then_inc(slot[h % 4], 16)
            tile(0, 0)
            with pool.Fori(0, BP // 2 - 1) as ii:
                for k in range(2):
                    tile(2 * ii + k + 1, 1 - k)
            tile(BP - 1, 1)


FCH, LCH, BCH, WCH = 19, 13, 2 * H, 1
NREC = 168


def kernel(**inputs):
    import concourse.bacc as bacc
    from concourse.bass_utils import run_bass_kernel_spmd

    x = {k: np.asarray(v) for k, v in inputs.items()}
    mixer = {k: v for k, v in x.items() if k == "x" or k.startswith("L0_tok")}
    arrays = {**host_constants(), **ffn_constants(), **host_layout(**mixer), **ffn_layout(**{k: v for k, v in x.items() if k not in mixer})}
    nc = bacc.Bacc("TRN2", target_bir_lowering=False, num_devices=1)
    T = {k: nc.dram_tensor(f"in_{k}", v.shape, mybir.dt.from_np(v.dtype), kind="ExternalInput").ap() for k, v in arrays.items()}
    out = nc.dram_tensor("out", (BP, 128, D), F32, kind="ExternalOutput").ap()
    vision_tower(nc, T, out)
    r = run_bass_kernel_spmd(nc, [{f"in_{k}": v for k, v in arrays.items()}], core_ids=[0])
    return r.results[0]["out"].reshape(B, S, S)
```

```python
import numpy as np
import concourse.bass as bass
from concourse import mybir
from contextlib import ExitStack

F32 = mybir.dt.float32
U32 = mybir.dt.uint32
ALU = mybir.AluOpType
ACT = mybir.ActivationFunctionType
AX = mybir.AxisListType

B, S, C, L, MODES, MID = 64, 64, 32, 4, 12, 4
K1, K2 = 2 * MODES, MODES
NB = 16
CH = B // NB
BP = B // 2
TC = NB // 2
NM = MODES * K2
D = 64
N = 256
H, NK, TOPK, DK = 8, 64, 16, 32
DECAY = 0.97
NEG = -3.0e38
CAND = [(0, 1, 16), (1, 2, 8), (2, 3, 5), (3, 4, 4), (4, 5, 3), (5, 8, 2), (8, 16, 1)]
NC = sum((b - a) * n for a, b, n in CAND)
FILLS = [(m, x, min(3, 16 - x) if x < 12 else 2) for m in range(2) for x in (0, 3, 6, 9, 12, 14)]


def host_constants():
    f = np.float64
    kx = np.concatenate([np.arange(MODES), np.arange(S - MODES, S)]).astype(f)
    ky = np.arange(K2).astype(f)
    pos = np.arange(S).astype(f)
    cx = np.cos(2 * np.pi * np.outer(kx, pos) / S)
    sx = np.sin(2 * np.pi * np.outer(kx, pos) / S)
    cy = np.cos(2 * np.pi * np.outer(ky, pos) / S)
    sy = np.sin(2 * np.pi * np.outer(ky, pos) / S)
    two = np.eye(2)
    half_ri_kx = np.stack([cx.reshape(2, MODES, S), -sx.reshape(2, MODES, S)], 1).reshape(2 * K1, S)
    inv_x = np.kron(two, half_ri_kx)
    alpha = np.where(ky == 0, 1.0, 2.0)[:, None] / S
    inv_y = np.stack([alpha * cy, -alpha * sy])
    inv_y = np.einsum("vky,bc->vkbcy", inv_y, np.eye(4)).reshape(2 * K2 * 4, 4 * S)
    fwd_y = np.stack([cy, -sy]).transpose(2, 0, 1).reshape(S, 2 * K2)
    fwd_y = np.kron(two, fwd_y)
    re_part = np.stack([cx.T, -sx.T], 1) / S
    im_part = np.stack([sx.T, cx.T], 1) / S
    fwd_x0 = np.stack([a.reshape(S, 2 * K1) for a in (re_part, im_part)])
    fwd_x = np.stack([np.kron(two, a).reshape(2, S, 4 * K1).transpose(1, 0, 2).reshape(2 * S, 4 * K1) for a in fwd_x0])
    ri = (np.arange(128) // 32) % 2
    sign = np.stack([np.where(ri == 0, 1.0, -1.0), np.where(ri == 0, -1.0, 1.0)], 1)
    px = (np.arange(128) // 32)[:, None]
    pmask = (px == (np.arange(16) // MID)[None, :]).astype(f)
    grid = np.linspace(0.0, 1.0, S)
    fx = lambda img: _dft(img, kx, ky)
    feats = [None, fx(np.repeat(grid[:, None], S, 1)), fx(np.repeat(grid[None, :], S, 0)), fx(np.ones((S, S)))]
    e = np.zeros((2, 2, 4, NB // 8, MODES, 8, K2))
    for n in (1, 2, 3):
        z = feats[n].reshape(2, MODES, K2)
        e[:, 0, n] = z.real[:, None, :, None, :]
        e[:, 1, n] = z.imag[:, None, :, None, :]
    gridc = np.concatenate([np.tile(grid, 2)[:, None], np.tile(grid[None, :], (128, 1))], 1)
    out = dict(inv_x=inv_x, inv_y=inv_y, fwd_y=fwd_y, fwd_x=fwd_x, fwd_x0=fwd_x0, sign=sign, pmask=pmask,
               e_const=e.reshape(16, NB * NM), gridc=gridc)
    return {k: np.ascontiguousarray(v.astype(np.float32)) for k, v in out.items()}


def _dft(img, kx, ky):
    pos = np.arange(S)
    return np.exp(-2j * np.pi * np.outer(kx, pos) / S) @ img @ np.exp(-2j * np.pi * np.outer(pos, ky) / S) / S


def host_layout(x, L0_tok_p_w, L0_tok_p_b, L0_tok_fw, L0_tok_w1_w, L0_tok_w1_b, L0_tok_w2_w, L0_tok_w2_b,
                L0_tok_q1_w, L0_tok_q1_b, L0_tok_q2_w, L0_tok_q2_b):
    a = {}
    a["xt"] = x[..., 0].reshape(BP, 2, S, S).transpose(1, 3, 0, 2).reshape(128, BP * S)
    fw = L0_tok_fw.transpose(0, 1, 6, 2, 4, 5, 3).reshape(L, 2, 2, C, MODES * K2, C)
    a["fwt"] = np.stack([np.stack([fw[:, :, 0], fw[:, :, 1]], 4), np.stack([fw[:, :, 1], fw[:, :, 0]], 4)], 2)\
        .reshape(L, 128, MODES * K2 * 2 * C)
    w1 = np.zeros((L, 2, 4, C, 4, C), np.float32)
    w2 = np.zeros((L, 4, C, 4, C), np.float32)
    for q in range(4):
        w1[:, 0, q, :, q] = L0_tok_w1_w.transpose(0, 2, 1)
        w1[:, 1, q, :, q ^ 1] = L0_tok_w1_w.transpose(0, 2, 1)
        w2[:, q, :, q] = L0_tok_w2_w.transpose(0, 2, 1)
    a["w1bd"] = w1.reshape(L, 2, 128, 128).transpose(0, 2, 1, 3).reshape(L, 128, 256)
    a["w2bd"] = w2.reshape(L, 128, 128)
    a["w2rep"] = np.tile(L0_tok_w2_w, (1, 1, 4))
    bias = np.zeros((L, 4, C, 3), np.float32)
    bias[:, 0, :, 0] = L0_tok_w1_b
    bias[:, 1, :, 1] = L0_tok_w1_b
    bias[:, 0, :, 2] = L0_tok_w2_b
    a["dcbias"] = bias.reshape(L, 128, 3)[:, :, 0:2]
    a["b2col"] = bias.reshape(L, 128, 3)[:, :, 2:3]
    pw = np.concatenate([L0_tok_p_w, L0_tok_p_b[:, None]], 1)
    p0 = np.zeros((4, 4, 4, C), np.float32)
    for q in range(4):
        p0[q, :, q] = pw.T
    a["p0"] = p0.reshape(16, 128)
    a["tail"] = np.concatenate([pw, L0_tok_q1_w.T, L0_tok_w2_b.T], 1)
    a["tailb"] = np.tile(np.concatenate([L0_tok_q1_b, L0_tok_q2_w[0], L0_tok_q2_b])[None], (128, 1))
    return {k: np.ascontiguousarray(v) for k, v in a.items()}


def ffn_constants():
    s, t = np.meshgrid(np.arange(S), np.arange(S), indexing="ij")
    decay = np.where(s < t, DECAY ** np.maximum(t - 1 - s, 0).astype(np.float64), 0.0)
    i, j = np.meshgrid(np.arange(128), np.arange(128), indexing="ij")
    causal = np.where((i // S == j // S) & (j <= i), 0.0, NEG)
    rowbase = np.tile((np.repeat(np.arange(H), TOPK) * NK * NK)[None], (128, 1))
    iota = np.tile(np.arange(NC)[None], (128, 1))
    return dict(masks=np.concatenate([np.tile(decay, (2, 1)), causal, rowbase, iota], 1).astype(np.float32))


def ffn_layout(L0_attn_E, L0_attn_Dx, L0_attn_Dy, L0_ffn_Wq_pk, L0_ffn_pk_keys, L0_ffn_Wq, L0_ffn_keys_table,
               L0_ffn_values_table, L0_ffn_Wo):
    a = dict(
        dxt=np.tile(L0_attn_Dx.T, (2, 1)), dyt=L0_attn_Dy.T,
        et=L0_attn_E.T.reshape(2, 128, D).transpose(1, 0, 2).reshape(128, 2 * D),
        wqpk=L0_ffn_Wq_pk.reshape(D, 2 * H, DK).transpose(2, 1, 0).reshape(DK, 2 * H * D),
        pkk=L0_ffn_pk_keys.transpose(3, 0, 2, 1).reshape(DK, 2 * H * NK),
        wq=L0_ffn_Wq, wo=L0_ffn_Wo.reshape(4, 128, D).transpose(1, 0, 2).reshape(128, 4 * D),
        kvtab=np.concatenate([L0_ffn_keys_table, L0_ffn_values_table], 1))
    return {k: np.ascontiguousarray(v) for k, v in a.items()}



ARENA = 53100


def vision_tower(nc, T, out):
    ctx = ExitStack()
    with ctx:
        arena = ctx.enter_context(nc.sbuf_tensor("arena", [128, ARENA], F32))
        bank = [ctx.enter_context(nc.psum_tensor(f"bank{i}", [128, 512], F32)) for i in range(8)]
        TB, RB, PB, FB = bank[0:2], bank[2:4], bank[4], bank[5:8]
        YB = TB[1:2] + RB
        gd = nc.dram_tensor("modes_mixed", (128, MODES, 4 * 96), F32, kind="Internal").ap()
        fr = nc.dram_tensor("modes_relu", (2, 96, 16, 96), F32, kind="Internal").ap()
        fx = nc.dram_tensor("modes_x", (2 * K1, B * K2), F32, kind="Internal").ap()

        used = [0]

        def sb(cols, rows=128):
            used[0] += cols
            assert used[0] <= ARENA, used[0]
            return arena[0:rows, used[0] - cols:used[0]]
        Wt = sb(NM * 2 * C)
        St = sb(NB * NM)
        Dt = sb(16 * 192, 96)
        TG = sb(2048)
        Tt = TG[0:96]
        Gc = TG[:, 0:768]
        Ft = sb(16 * 96, 96)
        Pt = sb(TC * S * MID)
        scratch = sb(4096 + 4096 + 1536)
        Rt = scratch[:, 0:4096]
        Yt = scratch[:, 4096:8192]
        Qt = scratch[:, 8192:9728]
        Gp = scratch[:, 4096:4096 + MODES * 384]
        FRt = scratch[:, 0:NB * NM]
        Et = scratch[0:16, 0:NB * NM]
        hTc, h1 = sb(512), sb(512)
        xc = hTc
        Pj = hTc
        invx, invy, fwdy, fwdx = sb(128, 96), sb(256, 96), sb(48), sb(192)
        sign, pmask, gridc, ones = sb(2), sb(16), sb(65), sb(128)
        ipw = sb(144)
        ident, pw = ipw[:, 0:128], ipw[:, 128:144]
        w1t, w2t, w2r, dcb, b2c = sb(256), sb(128), sb(128, 32), sb(2), sb(1)
        p0, tail, tailb = sb(128, 16), sb(12, 32), sb(9)
        prod, cf, t4, base = sb(16, 32), sb(16), sb(4), sb(256)
        b2sum = sb(1, 32)
        X = scratch[:, 0:2048]
        nsum, cc, dd = (scratch[:, 2048 + k * 1024:3072 + k * 1024] for k in range(3))
        htok, lnv, gm, la, sq = (scratch[:, 5120 + k * 512:5632 + k * 512] for k in range(5))
        laT = scratch[0:64, 7680:8704]
        st, mean, var = sb(16), sb(8), sb(8)
        dxt, dyt, et = sb(256), sb(256, 64), sb(128)
        simw, wq, wo = sb(1024, 64), sb(512, 64), sb(256)
        masks = sb(320 + NC)
        decay, causal, rowbase, iota = masks[:, 0:64], masks[:, 64:192], masks[:, 192:320], masks[:, 320:320 + NC]
        sim, A, If = sb(1024), sb(256), sb(256)
        Iu = If.bitcast(U32)
        cand, pay = sb(H * NC), sb(H * NC)
        Vt, posf, pick, best = sb(128), sb(128), sb(128), sb(8)
        posu = posf.bitcast(U32)
        rowidx = sb(256).bitcast(U32)
        wt, qT, hs, hsT, wsum = sb(256), sb(1024), sb(128), sb(128, 64), sb(8)
        KV = sb(4 * 2048)
        kT = sb(512)
        eq = sb(64 * NC)
        sc, at = eq[:, 0:1024], eq[:, 1024:2048]
        KVs = sim
        KVe = scratch[:, 8704:9728]
        ao, aoT = sc[:, 0:512], kT
        mx, sm, res, rc, rq, rv, yt = sb(8), sb(8), sb(64), sb(64), sb(64), sb(4), sb(128)
        wqpk, pkk = scratch[0:32, 4096:5120], scratch[0:32, 5120:6144]
        x_all = scratch[:, 0:2048]
        xq = scratch[0:64, 6144:6144 + 1536]
        xm = scratch[0:48, 7680:7680 + 768]
        fwdx0 = scratch[0:64, 8448:8448 + 96]

        names = """const xload fxp fxq fxf fxs fxst swp cff prodd cfd base_d eload xcl s0f s0e s_rdy pinit w_in wa_in wb_in
            wfix w1fix dcfix pwf pw_e mixf g_e w1f gp_e gst drdy i1 t_e i2 r_e pf p_e xf x_e qf q_e ff f_e fst frt
            upf upd_e h_d xu_p xu_e cs_p th_p th_e rec cd gr_p gr_e a_p ln_in ln_out lt_p lt_e lnv_d la_d yc_p yc_e
            v_p h1ok fr_h fr_t fr_hT fr_s fr_se fr_q fr_qe b2f fch fdif fexp idx wch bch kt_p kt_e sm_p bdif bexp aw
            at_p at_e av_p av_e ot_p ot_e wo_p res_d lch rvv rst done out0 out1 id one passed""".split()
        s = {n: ctx.enter_context(nc.semaphore(n)) for n in names}
        slot = [ctx.enter_context(nc.semaphore(f"slot{i}")) for i in range(4)]
        CREDIT = ("i1", "f_e", "fst", "p_e", "res_d", "out0", "out1")
        NCONST = 22

        def held(eng, name, v):
            eng.wait_ge(s[name] if isinstance(name, str) else name, v)
            eng.sem_inc(s["passed"], 1)

        def schedule(eng, p):
            part = lambda name: p.get(name, lambda *a: None)
            begin, spectrum, space, update, recur = (part(n) for n in ("begin", "spectrum", "space", "update", "recur"))
            front, weigh, sums, back = part("front"), part("weigh"), part("sums"), part("back")

            def chunk(c, more):
                with eng.Fori(0, L - 1) as l:
                    i, lam, mu = TC * c + 2 * l, L * c + L + l, (L - 1) * c + (L - 1) + l
                    space(lam, mu, (0,), l, c + 1)
                    weigh(i + 1, 1)
                    back(i, 0, i + 2)
                    front(i + 2, 0, 2 * l + 2, c + 1)
                    space(lam, mu, (1, 2, 3), l, c + 1)
                    weigh(i + 2, 0)
                    back(i + 1, 1, i + 3)
                    front(i + 3, 1, 2 * l + 3, c + 1)
                    update(lam, mu)
                    spectrum(lam + 1)
                i, lam = TC * c + TC - 2, L * c + 2 * L - 1
                space(lam, None, (0,), None, c + 1)
                weigh(i + 1, 1)
                back(i, 0, i + 2)
                sums(i + 1, 1)
                space(lam, None, (1, 2, 3), None, c + 1)
                recur(c + 1, i + 1)
                front(i + 2, 0, 0, c + 2)
                weigh(i + 2, 0)
                if more:
                    begin(c + 2)
                    spectrum(L * c + 2 * L, 0, 4)
                back(i + 1, 1, i + 3, True)
                if more:
                    front(i + 3, 1, 1, c + 2)
                    spectrum(L * c + 2 * L, 4)

            begin(0)
            with eng.Fori(0, L - 1) as l:
                spectrum(l)
                space(l, l, (0,), l, 0)
                space(l, l, (1, 2, 3), l, 0)
                update(l, l)
            spectrum(L - 1)
            space(L - 1, None, (0,), None, 0)
            space(L - 1, None, (1, 2, 3), None, 0)
            recur(0, None)
            front(0, 0, 0, 1)
            weigh(0, 0)
            front(1, 1, 1, 1)
            begin(1)
            spectrum(L)
            with eng.Fori(0, CH - 2) as c:
                chunk(c, True)
            chunk(CH - 2, False)
            i = BP - TC
            with eng.Fori(0, TC // 2 - 1) as n:
                front(i + 2 * n + 1, 1, 2 * n + 1, CH)
                weigh(i + 2 * n + 1, 1)
                back(i + 2 * n, 0, i + 2 * n + 2)
                front(i + 2 * n + 2, 0, 2 * n + 2, CH)
                weigh(i + 2 * n + 2, 0)
                back(i + 2 * n + 1, 1, i + 2 * n + 3)
            front(BP - 1, 1, TC - 1, CH)
            weigh(BP - 1, 1)
            back(BP - 2, 0, BP)
            back(BP - 1, 1, BP)

        block = ctx.enter_context(nc.Block())

        @block.sync
        def _(sp):
            for n in CREDIT:
                sp.sem_inc(s[n], 1)
            sp.dma_start(x_all, T["xt"]).then_inc(s["xload"], 16)
            for dst, n in ((fwdy, "fwd_y"), (fwdx[:, 0:96], 0), (fwdx[:, 96:192], 1), (sign, "sign"), (pmask, "pmask"),
                           (gridc, "gridc"), (p0, "p0"), (tail, "tail"), (tailb, "tailb"), (invx, "inv_x"), (invy, "inv_y"),
                           (masks[:, 0:320 + NC], "masks"), (dxt, "dxt"), (dyt, "dyt"), (et, "et"), (wqpk, "wqpk"), (pkk, "pkk"),
                           (wq, "wq"), (wo, "wo")):
                sp.dma_start(dst, T["fwd_x"][n] if isinstance(n, int) else T[n]).then_inc(s["const"], 16)
            for n in range(2):
                sp.dma_start(fwdx0[:, n * 48:n * 48 + 48], T["fwd_x0"][n]).then_inc(s["const"], 16)
            sp.dma_start(xc, T["xt"][:, 0:512]).then_inc(s["const"], 16)
            one = lambda name, l: T[name][bass.ds(l, 1)].rearrange("a p c -> (a p) c")

            def weights(l):
                sp.dma_start(Wt, one("fwt", l)).then_inc(s["w_in"], 16)
                for dst, n in ((w1t, "w1bd"), (dcb, "dcbias"), (w2r, "w2rep")):
                    sp.dma_start(dst, one(n, l)).then_inc(s["wa_in"], 16)

            def begin(c):
                if isinstance(c, int) and c == 0:
                    weights(0)
                    sp.wait_ge(s["fxs"], 2)
                    sp.dma_start(fx, xm).then_inc(s["fxst"], 16)
                    sp.wait_ge(s["fxst"], 16)
                else:
                    held(sp, "h1ok", c)
                    weights(0)
                    sp.dma_start(xc, T["xt"][:, bass.ds(c * 512, 512)]).then_inc(s["xcl"], 16)
                sp.dma_start(Et, T["e_const"]).then_inc(s["eload"], 16)
                held(sp, "eload", 80 * c + 16)
                for n in range(4):
                    r0 = ((n % 2) * 2 + n // 2) * MODES
                    sp.dma_start(Et[n * 4:n * 4 + 1, :].rearrange("p (g k c) -> p g k c", g=2, k=MODES),
                                 fx[r0:r0 + MODES, bass.ds(c * NB * K2, NB * K2)].rearrange("k (a g c) -> a g k c", a=1, g=2))\
                        .then_inc(s["eload"], 16)

            def spectrum(lam, f0=0, f1=7):
                for f in range(f0, min(f1, 6)):
                    held(sp, "gp_e", 24 * lam + 4 * f + 4)
                    sp.dma_start(gd[:, 2 * f:2 * f + 2, :], Gp[:, f * 768:f * 768 + 768].rearrange("p (k c) -> p k c", k=2))\
                        .then_inc(s["gst"], 16)
                if f1 == 7:
                    held(sp, "gst", 96 * lam + 96)

            def modes_in(lam, g):
                held(sp, "i1", 8 * (2 * lam + g) + 1)
                for q in range(2):
                    for n in range(4):
                        sp.dma_start(Dt[(q * 4 + n) * MODES:(q * 4 + n + 1) * MODES, :].rearrange("k (s c) -> k s c", s=16),
                                     gd[n * 32 + q * 16:n * 32 + q * 16 + 16, :, g * 192:g * 192 + 192]
                                     .rearrange("s k c -> k s c")).then_inc(s["drdy"], 16)

            def modes_back(g):
                for q in range(2):
                    for ri in range(2):
                        for hf in range(2):
                            r0, d0 = ((q * 2 + ri) * 2 + hf) * MODES, hf * 64 + ri * 32 + q * 16
                            sp.dma_start(FRt[d0:d0 + 16, g * 1152:g * 1152 + 1152].rearrange("p (k c) -> p k c", k=MODES),
                                         fr[g, r0:r0 + MODES, :, :].rearrange("k o c -> o k c")).then_inc(s["frt"], 16)

            def space(lam, mu, subs, l, c):
                g = len(subs) // 2
                modes_in(lam, g)
                if mu is None or g == 0:
                    return
                weights(l + 1)
                sp.dma_start(w2t, one("w2bd", l)).then_inc(s["wb_in"], 16)
                sp.dma_start(b2c, one("b2col", l)).then_inc(s["wb_in"], 16)
                for g in range(2):
                    held(sp, "f_e", 4 * (2 * mu + g) + 4 + 1)
                    sp.dma_start(fr[g].rearrange("p o c -> p (o c)"), Ft).then_inc(s["fst"], 16)
                    if g == 0:
                        held(sp, "x_e", 12 * (4 * mu + 3) + 12)
                    held(sp, "fst", 16 * (2 * mu + g + 1) + 1)
                    modes_back(g)

            def back(i, k, fronts, edge=False):
                held(sp, "done", i + 1)
                sp.dma_start(out[bass.ds(i, 1)].rearrange("a p d -> (a p) d"), yt[:, k * 64:k * 64 + 64]).then_inc(s[f"out{k}"], 16)
            schedule(sp, dict(begin=begin, spectrum=spectrum, space=space, back=back))
            sp.wait_ge(s["out0"], 16 * (BP // 2) + 1)
            sp.wait_ge(s["out1"], 16 * (BP // 2) + 1)

        @block.tensor
        def _(pe):
            mm, tr = nc.tensor.matmul, nc.tensor.transpose
            Wv = Wt.rearrange("p (m r) -> p m r", m=NM)
            Sv = St.rearrange("p (g k b y) -> p g k b y", g=2, k=MODES, b=8)
            Dv = Dt.rearrange("p (s u c) -> p s u c", s=16, u=2)
            Yv = Yt.rearrange("p (m z o) -> p m z o", m=2, o=16)
            Qv = Qt.rearrange("p (m o b r y) -> p m r o b y", m=2, o=16, b=2, r=2)

            def start():
                pe.wait_ge(s["const"], 16 * NCONST)
                for f in range(2):
                    for k in range(8):
                        r = (f * 8 + k) * 64
                        last = mm(FB[f][0:64, k * 64:k * 64 + 64], wqpk[:, r:r + 64], pkk[:, r:r + 64], start=True, stop=True)
                    last.then_inc(s["swp"], 1)
                pe.wait_ge(s["xload"], 16)
                for f in range(4):
                    for k in range(8):
                        u = f * 8 + k
                        last = mm(bank[f][0:64, k * 48:k * 48 + 48], x_all[:, u * 64:u * 64 + 64], fwdy, start=True, stop=True)
                    last.then_inc(s["fxp"], 1)
                pe.wait_ge(s["prodd"], 1)
                mm(PB[:, 0:16], ones[0:32, :], prod, start=True, stop=True).then_inc(s["cff"], 1)
                xv = xq.rearrange("p (u r y) -> p u r y", r=2, y=K2)
                pe.wait_ge(s["fxq"], 4)
                for f in range(2):
                    for r in range(2):
                        last = mm(TB[f][0:48, 0:384], fwdx0[:, r * 48:r * 48 + 48], xv[:, f * 32:f * 32 + 32, r, :],
                                  start=(r == 0), stop=(r == 1))
                    last.then_inc(s["fxf"], 1)
                pe.wait_ge(s["fxs"], 2)
                pe.wait_ge(s["cfd"], 1)
                pe.wait_ge(s["id"], 2)

            def begin(c):
                if isinstance(c, int) and c == 0:
                    start()
                pe.wait_ge(s["eload"], 80 * c + 80)
                for n in range(6):
                    if n >= 2:
                        pe.wait_ge(s["s0e"], 6 * c + n - 1)
                    mm(TB[n % 2][:, 0:384], p0, Et[:, n * 384:n * 384 + 384], start=True, stop=True).then_inc(s["s0f"], 1)

            def spectrum(lam, f0=0, f1=7):
                if f0 == 0:
                    pe.wait_ge(s["wa_in"], 48 * lam + 48)
                    held(pe, "p_e", 4 * lam + 1)
                    mm(PB[:, 0:4], w2r, tail[:, 4:8], start=True, stop=True).then_inc(s["pwf"], 1)
                    pe.wait_ge(s["s_rdy"], lam + 1)
                    held(pe, "wfix", lam + 1)
                for f in range(f0, f1):
                    if f < 6:
                        if f >= 2:
                            held(pe, "g_e", 6 * lam + f - 1)
                        for k in range(24):
                            for hf in range(2):
                                p = slice(64 * hf, 64 * hf + 64)
                                last = mm(TB[f % 2][p, k * 16:k * 16 + 16], Wv[p, f * 24 + k, :], Sv[p, :, 2 * f + k // K2, :, k % K2],
                                          start=True, stop=True)
                        last.then_inc(s["mixf"], 1)
                    if f >= 1:
                        pe.wait_ge(s["g_e"], 6 * lam + f)
                        if f == 1:
                            pe.wait_ge(s["w1fix"], lam + 1)
                        for v in range(2):
                            if f >= 2:
                                pe.wait_ge(s["gp_e"], 24 * lam + 4 * (f - 2) + 2 * v + 2)
                            mm(RB[v][:, 0:384], w1t[:, v * 128:v * 128 + 128], Gc[:, ((f - 1) % 2) * 384:((f - 1) % 2) * 384 + 384],
                               start=True, stop=True).then_inc(s["w1f"], 1)

            def x_back(lam, sub):
                u = 4 * lam + sub
                if sub % 2 == 0:
                    pe.wait_ge(s["drdy"], 128 * (2 * lam + sub // 2) + 128)
                for q in range(4):
                    if q >= 2:
                        pe.wait_ge(s["t_e"], 4 * u + q - 1)
                    for k in range(4):
                        last = mm(TB[q % 2][0:96, k * 128:k * 128 + 128], Dv[:, q * 4 + k, sub % 2, :], invx, start=True, stop=True)
                    last.then_inc(s["i1"], 1)

            def space(lam, mu, subs, l, c):
                x_back(lam, subs[0])
                for sub in subs:
                    u = 4 * lam + sub
                    pe.wait_ge(s["t_e"], 4 * u + 4)
                    w = None if mu is None else 4 * mu + sub

                    def project(f):
                        pe.wait_ge(s["r_e"], 8 * u + f + 1)
                        for x_ in (2 * f, 2 * f + 1):
                            for m in range(2):
                                o = m * 256 + x_ * 16
                                last = mm(PB[:, o:o + 16], Rt[:, x_ * 256 + m * 128:x_ * 256 + m * 128 + 128], pw,
                                          start=False, stop=f == 7 and x_ == 15 and m == 1, skip_group_check=True)
                        return last
                    pe.wait_ge(s["p_e"], u + 1)
                    pe.wait_ge(s["pw_e"], lam + 1)
                    if sub == 0:
                        pe.wait_ge(s["pinit"], c + 1)
                    if mu is None:
                        mm(PB[:, :], ident, Pt[:, sub * 512:sub * 512 + 512], start=True, stop=False, skip_group_check=True)
                    for f in range(8):
                        if f == 1 and mu is not None:
                            pe.wait_ge(s["f_e"], 2 * w + 1)
                        if f >= 3:
                            pe.wait_ge(s["r_e"], 8 * u + f - 2)
                        for k in range(2):
                            x_ = 2 * f + k
                            last = mm(YB[f % 3][:, k * 256:k * 256 + 256], Tt[:, x_ * 128:x_ * 128 + 128], invy, start=True, stop=True)
                        last.then_inc(s["i2"], 1)
                        if mu is None and f >= 2:
                            project(f - 2)
                    if mu is None:
                        project(6)
                        if sub != subs[-1]:
                            x_back(lam, sub + 1)
                        project(7).then_inc(s["pf"], 1)
                        continue
                    for f, (m, x0, n) in enumerate(FILLS):
                        if f < 3:
                            pe.wait_ge(s["r_e"], 8 * u + 6 + f)
                        else:
                            pe.wait_ge(s["x_e"], 12 * w + f - 2)
                        for k in range(n):
                            o = (x0 + k) * 256 + m * 128
                            last = mm(YB[(8 + f) % 3][:, k * 144:k * 144 + 144], Rt[:, o:o + 128], ipw, start=True, stop=True)
                        last.then_inc(s["xf"], 1)
                    for f in range(4):
                        m = f // 2
                        if f < 3:
                            pe.wait_ge(s["x_e"], 12 * w + (6, 11, 12)[f])
                        if f >= 2:
                            pe.wait_ge(s["q_e"], 4 * w + f - 1)
                        for k in range(8):
                            last = mm(TB[f % 2][:, k * 48:k * 48 + 48], Yv[:, m, :, (f % 2) * 8 + k], fwdy, start=True, stop=True)
                        last.then_inc(s["qf"], 1)
                    mm(PB[:, :], ident, Pt[:, sub * 512:sub * 512 + 512], start=True, stop=False)
                    mm(PB[:, :], ident, Pj, start=False, stop=True).then_inc(s["pf"], 1)
                    pe.wait_ge(s["q_e"], 4 * w + 4)
                    if sub != subs[-1]:
                        x_back(lam, sub + 1)
                    for m in range(2):
                        for r in range(2):
                            last = mm(RB[m][0:96, 0:384], fwdx[:, r * 96:r * 96 + 96], Qv[:, m, r], start=(r == 0), stop=(r == 1))
                        last.then_inc(s["ff"], 1)

            def update(lam, mu):
                pe.wait_ge(s["wb_in"], 32 * mu + 32)
                pe.wait_ge(s["f_e"], 2 * (4 * mu + 4) + 1)
                for n in range(6):
                    if n % 3 == 0:
                        pe.wait_ge(s["frt"], 256 * mu + 128 * (n // 3) + 128)
                    if n >= 2:
                        pe.wait_ge(s["upd_e"], 6 * mu + n - 1)
                    cols = slice(n * 384, n * 384 + 384)
                    mm(RB[n % 2][:, 0:384], ident, St[:, cols], start=True, stop=False)
                    mm(RB[n % 2][:, 0:384], w2t, FRt[:, cols], start=False, stop=True).then_inc(s["upf"], 1)

            def recur(c, tile):
                held(pe, "h_d", c + 1)
                B4 = TB + RB
                for f in range(4):
                    nh, b2 = f % 2, f // 2
                    mm(B4[f][:, :], dxt[64 * b2:64 * b2 + 64, nh * 128:nh * 128 + 128], hTc[64 * b2:64 * b2 + 64, :],
                       start=True, stop=True).then_inc(s["xu_p"], 1)
                held(pe, "h_d", c + 1)
                for u in range(TC):
                    for b2 in range(2):
                        p = slice(64 * b2, 64 * b2 + 64)
                        last = mm(PB[p, u * 64:u * 64 + 64], hTc[p, u * 64:u * 64 + 64], ident[p, 64 * b2:64 * b2 + 64], start=True, stop=True)
                last.then_inc(s["th_p"], 1)
                pe.wait_ge(s["one"], 1)
                pe.wait_ge(s["xu_e"], 4 * c + 4)
                for b2 in range(2):
                    for nh in range(2):
                        last = mm(TB[b2][:, :], ones, X[:, nh * 1024 + b2 * 512:nh * 1024 + b2 * 512 + 512], start=(nh == 0), stop=(nh == 1))
                    last.then_inc(s["cs_p"], 1)
                pe.wait_ge(s["cd"], c + 1)
                for u in range(TC):
                    for b2 in range(2):
                        for nh in range(2):
                            o = nh * 1024 + b2 * 512 + u * 64
                            last = mm(RB[0][64 * b2:64 * b2 + 64, u * 64:u * 64 + 64], X[:, o:o + 64], X[:, o:o + 64], start=(nh == 0), stop=(nh == 1))
                last.then_inc(s["gr_p"], 1)
                held(pe, "lnv_d", c + 1)
                held(pe, "gr_e", c + 1)
                for u in range(TC):
                    for b2 in range(2):
                        p = slice(64 * b2, 64 * b2 + 64)
                        last = mm(RB[1][p, u * 64:u * 64 + 64], gm[p, u * 64:u * 64 + 64], lnv[p, u * 64:u * 64 + 64], start=True, stop=True)
                last.then_inc(s["a_p"], 1)
                held(pe, "la_d", c + 1)
                for f in range(2):
                    for k in range(4):
                        o = (4 * f + k) * 64
                        last = tr(TB[f][0:64, k * 128:k * 128 + 128], la[:, o:o + 64], ident)
                    last.then_inc(s["lt_p"], 1)
                pe.wait_ge(s["lt_e"], 2 * c + 2)
                for f in range(4):
                    nh, b2 = f % 2, f // 2
                    mm((RB + [PB] + TB)[f][:, :], dyt[:, nh * 128:nh * 128 + 128], laT[:, b2 * 512:b2 * 512 + 512], start=True, stop=True)\
                        .then_inc(s["yc_p"], 1)
                pe.wait_ge(s["yc_e"], 4 * c + 4)
                for u in range(TC):
                    for b2 in range(2):
                        for nh in range(2):
                            o = nh * 1024 + b2 * 512 + u * 64
                            last = mm(TB[1][64 * b2:64 * b2 + 64, u * 64:u * 64 + 64], X[:, o:o + 64], et[:, nh * 64:nh * 64 + 64],
                                      start=(nh == 0), stop=(nh == 1))
                last.then_inc(s["v_p"], 1)

            def front(i, k, tile, chunks):
                held(pe, "fr_h", i + 1)
                tr(FB[0][0:64, 0:128], hs[:, k * 64:k * 64 + 64], ident).then_inc(s["fr_t"], 1)
                pe.wait_ge(s["fr_hT"], i + 1)
                if not isinstance(i, int) or i > 0:
                    pe.wait_ge(s["res_d"], i)
                for n in range(2):
                    last = mm(FB[1 + n][:, :], hsT, simw[:, n * 512:n * 512 + 512], start=True, stop=True)
                last.then_inc(s["fr_s"], 1)
                for n in range(4):
                    last = mm(FB[0][:, n * 128:n * 128 + 128], wq[:, n * 128:n * 128 + 128], hsT, start=True, stop=True)
                last.then_inc(s["fr_q"], 1)

            def back(i, k, fronts, edge=False):
                kvs = KVe if edge else KVs
                held(pe, "fr_qe", fronts)
                held(pe, "bch", BCH * i + 2 * H)
                for n in range(4):
                    last = tr(FB[0][:, n * 128:n * 128 + 128], kvs[:, n * 128:n * 128 + 128], ident)
                last.then_inc(s["kt_p"], 1)
                held(pe, "kt_e", i + 1)
                for h in range(H):
                    r, m = 64 * (h % 2), h // 2
                    last = mm(FB[1 + h % 2][:, m * 128:m * 128 + 128], qT[r:r + 64, k * 512 + m * 128:k * 512 + m * 128 + 128],
                              kT[r:r + 64, m * 128:m * 128 + 128], start=True, stop=True)
                last.then_inc(s["sm_p"], 1)
                held(pe, "aw", i + 1)
                for h in range(H):
                    last = tr(FB[1 + h // 4][:, (h % 4) * 128:(h % 4) * 128 + 128], sc[:, h * 128:h * 128 + 128], ident)
                last.then_inc(s["at_p"], 1)
                pe.wait_ge(s["at_e"], i + 1)
                for h in range(H):
                    a = 4 * (h % 2) + h // 2
                    last = mm(FB[0][:, h * 64:h * 64 + 64], at[:, a * 128:a * 128 + 128], kvs[:, 512 + h * 64:512 + h * 64 + 64],
                              start=True, stop=True)
                last.then_inc(s["av_p"], 1)
                pe.wait_ge(s["av_e"], i + 1)
                for n in range(4):
                    last = tr(FB[1][:, n * 128:n * 128 + 128], ao[:, n * 128:n * 128 + 128], ident)
                last.then_inc(s["ot_p"], 1)
                pe.wait_ge(s["ot_e"], i + 1)
                for n in range(4):
                    last = mm(FB[2][:, 0:64], aoT[:, n * 128:n * 128 + 128], wo[:, n * 64:n * 64 + 64], start=(n == 0), stop=(n == 3))
                last.then_inc(s["wo_p"], 1)

            schedule(pe, dict(begin=begin, spectrum=spectrum, space=space, update=update, recur=recur, front=front, back=back))

        @block.scalar
        def _(act):
            A_ = nc.scalar.activation

            def cp(o, i, f=ACT.Copy, **kw):
                return A_(o, i, f, **kw)
            Wn = Wt.rearrange("p (m r o) -> p m r o", m=NM, r=2)
            Gpv = Gp.rearrange("p (k u v y b) -> p k u v y b", k=MODES, u=4, v=2, y=K2)
            Tv = Tt.rearrange("p (x j s) -> p s j x", x=S, j=2)
            Fv = Ft.rearrange("p (o b y) -> p o b y", o=16, b=8)

            def begin(c):
                if isinstance(c, int) and c == 0:
                    for f in range(2):
                        act.wait_ge(s["swp"], f + 1)
                        cp(simw[:, f * 512:f * 512 + 512], FB[f][0:64, :])
                    for f in range(4):
                        act.wait_ge(s["fxp"], f + 1)
                        cp(xq[:, f * 384:f * 384 + 384], bank[f][0:64, 0:384]).then_inc(s["fxq"], 1)
                    for f in range(2):
                        act.wait_ge(s["fxf"], f + 1)
                        cp(xm[:, f * 384:f * 384 + 384], TB[f][0:48, 0:384]).then_inc(s["fxs"], 1)
                for n in range(6):
                    act.wait_ge(s["s0f"], 6 * c + n + 1)
                    cp(St[:, n * 384:n * 384 + 384], TB[n % 2][:, 0:384]).then_inc(s["s0e" if n < 5 else "s_rdy"], 1)
                act.sem_inc(s["s0e"], 1)

            def spectrum(lam, f0=0, f1=7):
                if f0 == 0:
                    act.wait_ge(s["wa_in"], 48 * lam + 48)
                    cp(w1t[:, 128:256], w1t[:, 128:256], scale=sign[:, 1:2]).then_inc(s["w1fix"], 1)
                    cp(dcb[:, 0:1], dcb[:, 0:1], scale=float(S))
                    cp(dcb[:, 1:2], dcb[:, 1:2], scale=-float(S)).then_inc(s["dcfix"], 1)
                    act.wait_ge(s["w_in"], 16 * lam + 16)
                    cp(Wn[:, :, 0, :], Wn[:, :, 0, :], scale=sign[:, 0:1]).then_inc(s["wfix"], 1)
                    act.wait_ge(s["pwf"], lam + 1)
                    for x4 in range(4):
                        last = cp(pw[:, x4 * 4:x4 * 4 + 4], PB[:, 0:4], scale=pmask[:, x4 * 4:x4 * 4 + 1])
                    last.then_inc(s["pw_e"], 1)
                for f in range(f0, f1):
                    if f < 6:
                        act.wait_ge(s["mixf"], 6 * lam + f + 1)
                        if f >= 2:
                            act.wait_ge(s["w1f"], 12 * lam + 2 * (f - 2) + 2)
                        cp(Gc[:, (f % 2) * 384:(f % 2) * 384 + 384], TB[f % 2][:, 0:384]).then_inc(s["g_e"], 1)
                    if f >= 1:
                        for v in range(2):
                            act.wait_ge(s["w1f"], 12 * lam + 2 * (f - 1) + v + 1)
                            for kk in range(2):
                                kx = 2 * (f - 1) + kk
                                src = RB[v][:, kk * 192:kk * 192 + 192].rearrange("p (y u b) -> p y u b", y=K2, u=4)
                                dst = Gpv[:, kx, :, v].rearrange("p u y b -> p y u b")
                                if kx == 0:
                                    if v == 0:
                                        act.wait_ge(s["dcfix"], lam + 1)
                                    cp(dst[:, 0], src[:, 0], ACT.Identity, bias=dcb[:, v:v + 1])
                                    dst, src = dst[:, 1:K2], src[:, 1:K2]
                                cp(dst, src).then_inc(s["gp_e"], 1)

            def x_back(lam, sub):
                u = 4 * lam + sub
                for q in range(4):
                    act.wait_ge(s["i1"], 4 * u + q + 2)
                    cp(Tv[:, q * 4:q * 4 + 4], TB[q % 2][0:96, :].rearrange("p (s j x) -> p s j x", s=4, j=2)).then_inc(s["t_e"], 1)

            def space(lam, mu, subs, l, c):
                x_back(lam, subs[0])
                for sub in subs:
                    u = 4 * lam + sub
                    for f in range(8):
                        act.wait_ge(s["i2"], 8 * u + f + 1)
                        cp(Rt[:, f * 512:f * 512 + 512], YB[f % 3][:, :], ACT.Relu).then_inc(s["r_e"], 1)
                    if mu is None:
                        if sub != subs[-1]:
                            x_back(lam, sub + 1)
                        act.wait_ge(s["pf"], u + 1)
                        cp(Pt[:, sub * 512:sub * 512 + 512], PB[:, :]).then_inc(s["p_e"], 1)
                        continue
                    w = 4 * mu + sub
                    for f, (m, x0, n) in enumerate(FILLS):
                        act.wait_ge(s["xf"], 12 * w + f + 1)
                        both = YB[(8 + f) % 3][:, 0:n * 144].rearrange("p (s c) -> p s c", s=n)
                        y0, j0 = m * 2048 + x0 * 128, m * 256 + x0 * 16
                        cp(Yt[:, y0:y0 + n * 128].rearrange("p (s c) -> p s c", s=n), both[:, :, 0:128])
                        cp(Pj[:, j0:j0 + n * 16].rearrange("p (s c) -> p s c", s=n), both[:, :, 128:144]).then_inc(s["x_e"], 1)
                    for f in range(4):
                        act.wait_ge(s["qf"], 4 * w + f + 1)
                        cp(Qt[:, f * 384:f * 384 + 384], TB[f % 2][:, 0:384]).then_inc(s["q_e"], 1)
                    act.wait_ge(s["pf"], u + 1)
                    cp(Pt[:, sub * 512:sub * 512 + 512], PB[:, :]).then_inc(s["p_e"], 1)
                    if sub != subs[-1]:
                        x_back(lam, sub + 1)
                    for m in range(2):
                        act.wait_ge(s["ff"], 2 * w + m + 1)
                        if m == 0 and sub % 2 == 0:
                            act.wait_ge(s["fst"], 16 * (2 * mu + sub // 2) + 1)
                        b = (sub % 2) * 4 + 2 * m
                        cp(Fv[:, :, b:b + 2, :], RB[m][0:96, 0:384].rearrange("p (o b y) -> p o b y", o=16, b=2)).then_inc(s["f_e"], 1)

            def update(lam, mu):
                act.wait_ge(s["wb_in"], 32 * mu + 32)
                cp(b2c, b2c, scale=float(S)).then_inc(s["b2f"], 1)
                for n in range(6):
                    act.wait_ge(s["upf"], 6 * mu + n + 1)
                    cp(St[:, n * 384:n * 384 + 384], RB[n % 2][:, 0:384]).then_inc(s["upd_e"], 1)
                act.wait_ge(s["upd_e"], 6 * mu + 6)
                act.wait_ge(s["b2f"], mu + 1)
                dc = St.rearrange("p (g k b y) -> p g k b y", g=2, k=MODES, b=8)[:, :, 0, :, 0]
                cp(dc, dc, ACT.Identity, bias=b2c).then_inc(s["s_rdy"], 1)

            def recur(c, tile):
                B4 = TB + RB
                for f in range(4):
                    nh, b2 = f % 2, f // 2
                    act.wait_ge(s["xu_p"], 4 * c + f + 1)
                    cp(X[:, nh * 1024 + b2 * 512:nh * 1024 + b2 * 512 + 512], B4[f][:, :], ACT.Relu).then_inc(s["xu_e"], 1)
                act.wait_ge(s["th_p"], c + 1)
                cp(htok, PB[:, :]).then_inc(s["th_e"], 1)

                def root(n):
                    act.wait_ge(s["ln_in"], 4 * c + n)
                    cp(var, var, ACT.Sqrt).then_inc(s["ln_out"], 1)
                root(1)
                root(2)
                for f in range(2):
                    act.wait_ge(s["lt_p"], 2 * c + f + 1)
                    dst = laT.rearrange("p (b u t) -> p u b t", b=2, u=TC)[:, f * 4:f * 4 + 4]
                    cp(dst, TB[f][0:64, :].rearrange("p (u b t) -> p u b t", u=4, b=2)).then_inc(s["lt_e"], 1)
                root(3)
                root(4)

            def front(i, k, tile, chunks):
                act.wait_ge(s["h1ok"], chunks)
                cp(hs[:, k * 64:k * 64 + 64], h1[:, tile * 64:tile * 64 + 64] if isinstance(tile, int) else h1[:, bass.ds(tile * 64, 64)])\
                    .then_inc(s["fr_h"], 1)
                act.wait_ge(s["fr_t"], i + 1)
                cp(hsT, FB[0][0:64, 0:128]).then_inc(s["fr_hT"], 1)
                act.wait_ge(s["fr_s"], i + 1)
                for n in range(2):
                    last = cp(sim[:, n * 512:n * 512 + 512], FB[1 + n][:, :])
                last.then_inc(s["fr_se"], 1)
                act.wait_ge(s["fr_q"], i + 1)
                cp(qT[:, k * 512:k * 512 + 512], FB[0][:, :], scale=D ** -0.5).then_inc(s["fr_qe"], 1)

            def weigh(i, k):
                act.wait_ge(s["fdif"], i + 1)
                cp(wt[:, k * 128:k * 128 + 128], Vt, ACT.Exp).then_inc(s["fexp"], 1)

            def back(i, k, fronts, edge=False):
                act.wait_ge(s["kt_p"], i + 1)
                cp(kT, FB[0][:, :]).then_inc(s["kt_e"], 1)
                act.wait_ge(s["bdif"], i + 1)
                cp(sc, sc, ACT.Exp).then_inc(s["bexp"], 1)
                act.wait_ge(s["at_p"], i + 1)
                for n in range(2):
                    last = cp(at[:, n * 512:n * 512 + 512], FB[1 + n][:, :])
                last.then_inc(s["at_e"], 1)
                act.wait_ge(s["av_p"], i + 1)
                cp(ao, FB[0][:, :]).then_inc(s["av_e"], 1)
                act.wait_ge(s["ot_p"], i + 1)
                cp(aoT, FB[1][:, :]).then_inc(s["ot_e"], 1)
                act.wait_ge(s["rvv"], i + 1)
                cp(rv[:, 1:2], rv[:, 0:1], ACT.Sqrt).then_inc(s["rst"], 1)

            act.wait_ge(s["const"], 16 * NCONST)
            schedule(act, dict(begin=begin, spectrum=spectrum, space=space, update=update, recur=recur, front=front, weigh=weigh, back=back))

        @block.vector
        def _(dve):
            V = nc.vector

            def start():
                V.memset(ones, 1.0).then_inc(s["one"], 1)
                dve.wait_ge(s["const"], 16 * NCONST)
                pw4, q1 = tail[:, 0:4], tail[:, 4:8]
                V.tensor_tensor(prod.rearrange("p (f m) -> p f m", f=4), pw4.unsqueeze(2).to_broadcast([32, 4, 4]),
                                q1.unsqueeze(1).to_broadcast([32, 4, 4]), ALU.mult).then_inc(s["base_d"], 1)
                V.tensor_reduce(b2sum, tail[:, 8:12], AX.X, ALU.add).then_inc(s["base_d"], 1)
                dve.wait_ge(s["base_d"], 2)
                dve.wait_ge(s["one"], 1)
                V.scalar_tensor_tensor(prod[:, 12:16], q1, b2sum[:, 0:1], prod[:, 12:16], ALU.mult, ALU.add).then_inc(s["prodd"], 1)
                dve.wait_ge(s["cff"], 1)
                V.tensor_copy(cf, PB[:, 0:16]).then_inc(s["cfd"], 1)
                dve.wait_ge(s["cfd"], 1)
                V.scalar_tensor_tensor(t4, cf[:, 8:12], gridc[:, 0:1], cf[:, 12:16], ALU.mult, ALU.add).then_inc(s["base_d"], 1)
                bv = base.rearrange("p (x m) -> p x m", m=MID)
                V.tensor_tensor(bv, gridc[:, 1:65].unsqueeze(2).to_broadcast([128, S, MID]),
                                cf[:, 4:8].unsqueeze(1).to_broadcast([128, S, MID]), ALU.mult).then_inc(s["base_d"], 1)
                dve.wait_ge(s["base_d"], 4)
                V.tensor_tensor(t4, t4, tailb[:, 0:4], ALU.add).then_inc(s["base_d"], 1)
                dve.wait_ge(s["base_d"], 5)
                V.tensor_tensor(bv, bv, t4.unsqueeze(1).to_broadcast([128, S, MID]), ALU.add).then_inc(s["base_d"], 1)
                dve.wait_ge(s["base_d"], 6)

            P4 = Pt.rearrange("p (n m) -> p n m", m=MID)
            Pb = Pt.rearrange("p (u c) -> p u c", u=TC)

            def begin(c):
                if isinstance(c, int) and c == 0:
                    start()
                else:
                    dve.wait_ge(s["xcl"], 16 * c)
                V.tensor_tensor(P4, xc.unsqueeze(2).to_broadcast([128, TC * S, MID]),
                                cf[:, 0:4].unsqueeze(1).to_broadcast([128, TC * S, MID]), ALU.mult).then_inc(s["wch"], 1)
                held(dve, "wch", WCH * c + 1)
                V.tensor_tensor(Pb, Pb, base.unsqueeze(1).to_broadcast([128, TC, 256]), ALU.add).then_inc(s["pinit"], 1)

            view = lambda a: a.rearrange("p (u d) -> p u d", d=D)
            wide = lambda a: a.unsqueeze(2).to_broadcast([128, TC, D])

            def recur(c, tile):
                n = [0]

                def link(ins):
                    n[0] += 1
                    ins.then_inc(s["rec"], 1)
                    dve.wait_ge(s["rec"], NREC * c + n[0])
                roots = [0]

                def layer_norm(dst, src):
                    link(V.tensor_reduce(mean, view(src), AX.X, ALU.add))
                    link(V.tensor_scalar(mean, mean, 1.0 / D, None, ALU.mult))
                    link(V.tensor_tensor(view(dst), view(src), wide(mean), ALU.subtract))
                    link(V.tensor_tensor(sq, dst, dst, ALU.mult))
                    link(V.tensor_reduce(var, view(sq), AX.X, ALU.add))
                    V.tensor_scalar(var, var, 1.0 / D, 1e-5, ALU.mult, ALU.add).then_inc(s["ln_in"], 1)
                    roots[0] += 1
                    dve.wait_ge(s["ln_out"], 4 * c + roots[0])
                    link(V.reciprocal(var, var))
                    return V.tensor_tensor(view(dst), view(dst), wide(var), ALU.mult)

                def meanwhile(h):
                    if tile is not None:
                        head_sum(tile, 1, h, KVe)
                dve.wait_ge(s["p_e"], 4 * L * (c + 1) + 1)
                link(V.scalar_tensor_tensor(P4, P4, 0.0, tailb[:, 4:8].unsqueeze(1).to_broadcast([128, TC * S, MID]), ALU.max, ALU.mult))
                link(V.tensor_reduce(hTc, P4, AX.X, ALU.add))
                V.tensor_scalar(hTc, hTc, tailb[:, 8:9], None, ALU.add).then_inc(s["h_d"], 1)
                link(V.memset(st, 0.0))
                for b2 in range(2):
                    dve.wait_ge(s["cs_p"], 2 * c + b2 + 1)
                    link(V.tensor_copy(nsum[:, b2 * 512:b2 * 512 + 512], TB[b2][:, :]))
                dve.sem_inc(s["passed"], 1)
                nv = nsum.rearrange("p (b t) -> p b t", t=S)
                with dve.Fori(0, S // 8) as t8:
                    for j in range(8):
                        dve.wait_ge(s["rec"], NREC * c + n[0] + 16 * t8 + 2 * j)
                        nt = nv[:, :, bass.ds(8 * t8 + j, 1)].rearrange("p b a -> p (b a)")
                        V.scalar_tensor_tensor(nt, st, DECAY, nt, ALU.mult, ALU.add).then_inc(s["rec"], 1)
                        dve.wait_ge(s["rec"], NREC * c + n[0] + 16 * t8 + 2 * j + 1)
                        V.tensor_scalar(st, nt, 1e12, 1.0, ALU.mult, ALU.min).then_inc(s["rec"], 1)
                n[0] += 2 * S
                dve.wait_ge(s["rec"], NREC * c + n[0])
                link(V.tensor_scalar(nsum, nsum, 1e-12, None, ALU.max))
                link(V.reciprocal(cc, nsum))
                link(V.tensor_scalar(dd, cc, DECAY, None, ALU.mult))
                link(V.memset(dd.rearrange("p (b t) -> p b t", t=S)[:, :, 0], 0.0))
                for nh in range(2):
                    xs = X[:, nh * 1024:nh * 1024 + 1024]
                    link(V.tensor_tensor(xs, xs, cc, ALU.mult))
                    last = V.tensor_tensor_scan(xs, dd, xs, 0.0, ALU.mult, ALU.add)
                    if nh == 0:
                        link(last)
                last.then_inc(s["cd"], 1)
                dve.wait_ge(s["th_e"], c + 1)
                layer_norm(lnv, htok).then_inc(s["lnv_d"], 1)
                dve.wait_ge(s["gr_p"], c + 1)
                V.tensor_tensor(view(gm), view(RB[0][:, :]), decay.unsqueeze(1).to_broadcast([128, TC, 64]), ALU.mult).then_inc(s["gr_e"], 1)
                meanwhile(4)
                dve.wait_ge(s["a_p"], c + 1)
                link(V.tensor_copy(la, RB[1][:, :]))
                layer_norm(la, la).then_inc(s["la_d"], 1)
                meanwhile(5)
                meanwhile(6)
                for f in range(4):
                    nh, b2 = f % 2, f // 2
                    dve.wait_ge(s["yc_p"], 4 * c + f + 1)
                    xs = X[:, nh * 1024 + b2 * 512:nh * 1024 + b2 * 512 + 512]
                    V.scalar_tensor_tensor(xs, (RB + [PB] + TB)[f][:, :], 0.0, xs, ALU.max, ALU.mult).then_inc(s["yc_e"], 1)
                meanwhile(7)
                dve.wait_ge(s["v_p"], c + 1)
                link(V.tensor_copy(la, TB[1][:, :]))
                link(layer_norm(la, la))
                link(V.tensor_tensor(la, la, htok, ALU.add))
                layer_norm(h1, la).then_inc(s["h1ok"], 1)
                assert n[0] == NREC, n[0]

            Av = A.rearrange("p (r k) -> p r k", r=16)
            Iv, Ifv = Iu.rearrange("p (r k) -> p r k", r=16), If.rearrange("p (r k) -> p r k", r=16)
            simv = sim.rearrange("p (r k) -> p r k", r=16)
            candv, payv = cand.rearrange("p (h c) -> p h c", h=H), pay.rearrange("p (h c) -> p h c", h=H)
            Vv, posv = Vt.rearrange("p (h k) -> p h k", h=H), posu.rearrange("p (h k) -> p h k", h=H)

            def top16(i, step, values, best_, index, rows):
                for r in range(rows):
                    last = V.max(best_[:, r, 0:8], values[:, r, :])
                step(last)
                for r in range(rows):
                    last = V.max_index(index[:, r, 0:8], best_[:, r, 0:8], values[:, r, :])
                step(last)
                for r in range(rows):
                    last = V.match_replace(values[:, r, :], best_[:, r, 0:8], values[:, r, :], NEG)
                step(last)
                for r in range(rows):
                    last = V.max(best_[:, r, 8:16], values[:, r, :])
                step(last)
                for r in range(rows):
                    last = V.max_index(index[:, r, 8:16], best_[:, r, 8:16], values[:, r, :])
                step(last)

            def front(i, k, tile, chunks):
                front_a(i)
                if isinstance(i, int) and i == 0:
                    front_b(i, k)

            def front_a(i):
                n = [0]

                def step(ins):
                    n[0] += 1
                    ins.then_inc(s["fch"], 1)
                    held(dve, "fch", FCH * i + n[0])
                held(dve, "fr_se", i + 1)
                top16(i, step, simv, Av, Iv, 16)
                assert n[0] == FCHA

            def front_b(i, k):
                n = [FCHA]

                def step(ins):
                    n[0] += 1
                    ins.then_inc(s["fch"], 1)
                    held(dve, "fch", FCH * i + n[0])
                V.tensor_copy(If[:, 0:128], Iu[:, 0:128])
                step(V.tensor_scalar(If[:, 128:256], Iu[:, 128:256], float(NK), None, ALU.mult))
                for dst, src in ((candv, Av), (payv, Ifv)):
                    o = 0
                    for a, b, m in CAND:
                        shape = [128, H, b - a, m]
                        last = V.tensor_tensor(dst[:, :, o:o + (b - a) * m].rearrange("p h (i j) -> p h i j", j=m),
                                               src[:, 0:8, a:b].unsqueeze(3).to_broadcast(shape),
                                               src[:, 8:16, 0:m].unsqueeze(2).to_broadcast(shape), ALU.add)
                        o += (b - a) * m
                step(last)
                top16(i, step, candv, Vv, posv, H)
                V.tensor_copy(posf, posu)
                step(V.tensor_copy(best, Vv[:, :, 0]))
                V.tensor_tensor(Vv, Vv, best.unsqueeze(2).to_broadcast([128, H, TOPK]), ALU.subtract).then_inc(s["fdif"], 1)
                hh = H // 2
                for z in range(2):
                    g0 = z * 64
                    eqv = eq.rearrange("p (g c) -> p g c", c=NC)
                    e4 = eq.rearrange("p (h k c) -> p h k c", h=hh, k=TOPK)
                    step(V.tensor_tensor(eqv, posf[:, g0:g0 + 64].unsqueeze(2).to_broadcast([128, 64, NC]),
                                         iota.unsqueeze(1).to_broadcast([128, 64, NC]), ALU.is_equal))
                    step(V.tensor_tensor(e4, e4, payv[:, z * hh:z * hh + hh].unsqueeze(2).to_broadcast([128, hh, TOPK, NC]), ALU.mult))
                    step(V.tensor_reduce(pick[:, g0:g0 + 64], eqv, AX.X, ALU.add))
                    V.tensor_tensor(rowidx[:, k * 128 + g0:k * 128 + g0 + 64], pick[:, g0:g0 + 64], rowbase[:, g0:g0 + 64],
                                    ALU.add).then_inc(s["idx"], 1)
                assert n[0] == FCH, n[0]

            def weights_of(i, k):
                w = wt[:, k * 128:k * 128 + 128].rearrange("p (h k) -> p h k", h=H)
                held(dve, "fexp", i + 1)
                V.tensor_reduce(wsum, w, AX.X, ALU.add).then_inc(s["lch"], 1)
                held(dve, "lch", LCH * i + 1)
                V.reciprocal(wsum, wsum).then_inc(s["lch"], 1)
                held(dve, "lch", LCH * i + 2)
                V.tensor_tensor(w, w, wsum.unsqueeze(2).to_broadcast([128, H, TOPK]), ALU.mult).then_inc(s["lch"], 1)
                held(dve, "lch", LCH * i + 3)

            def head_sum(i, k, h, kvs):
                w = wt[:, k * 128:k * 128 + 128].rearrange("p (h k) -> p h k", h=H)
                held(dve, slot[h % 4], 256 * (2 * i + h // 4) + 256)
                kv = KV[:, (h % 4) * 2048:(h % 4) * 2048 + 2048]
                kv3 = kv.rearrange("p (k d) -> p k d", k=TOPK)
                V.tensor_tensor(kv3, kv3, w[:, h, :].unsqueeze(2).to_broadcast([128, TOPK, 128]), ALU.mult).then_inc(s["bch"], 1)
                held(dve, "bch", BCH * i + 2 * h + 1)
                V.tensor_reduce(kvs.rearrange("p (c h d) -> p c h d", c=2, h=H)[:, :, h, :],
                                kv.rearrange("p (k c d) -> p c d k", k=TOPK, c=2), AX.X, ALU.add).then_inc(s["bch"], 1)

            def sums(i, k):
                weights_of(i, k)
                for h in range(4):
                    head_sum(i, k, h, KVe)

            def back(i, k, fronts, edge=False):
                if edge:
                    front_b(i + 1, 1 - k)
                else:
                    weights_of(i, k)
                    for h in range(H):
                        if h == 4 and not (isinstance(i, int) and i == BP - 1):
                            front_b(i + 1, 1 - k)
                        head_sum(i, k, h, KVs)
                nb = [3]

                def step(ins, name="lch", per=LCH):
                    nb[0] += 1
                    ins.then_inc(s[name], 1)
                    held(dve, name, per * i + nb[0])
                scv = sc.rearrange("p (h j) -> p h j", h=H)
                held(dve, "sm_p", i + 1)
                for n in range(2):
                    last = V.tensor_tensor(scv[:, 4 * n:4 * n + 4], FB[1 + n][:, :].rearrange("p (h j) -> p h j", h=4),
                                           causal.unsqueeze(1).to_broadcast([128, 4, 128]), ALU.add)
                step(last)
                step(V.tensor_reduce(mx, scv, AX.X, ALU.max))
                V.tensor_tensor(scv, scv, mx.unsqueeze(2).to_broadcast([128, H, 128]), ALU.subtract).then_inc(s["bdif"], 1)
                held(dve, "bexp", i + 1)
                step(V.tensor_reduce(sm, scv, AX.X, ALU.add))
                step(V.reciprocal(sm, sm))
                V.tensor_tensor(scv, scv, sm.unsqueeze(2).to_broadcast([128, H, 128]), ALU.mult).then_inc(s["aw"], 1)
                held(dve, "wo_p", i + 1)
                V.tensor_tensor(res, hs[:, k * 64:k * 64 + 64], FB[2][:, 0:64], ALU.add).then_inc(s["res_d"], 1)
                held(dve, "res_d", i + 2)
                step(V.tensor_reduce(rv[:, 0:1], res, AX.X, ALU.add))
                step(V.tensor_scalar(rv[:, 0:1], rv[:, 0:1], 1.0 / D, None, ALU.mult))
                step(V.tensor_scalar(rc, res, rv[:, 0:1], None, ALU.subtract))
                step(V.tensor_tensor(rq, rc, rc, ALU.mult))
                step(V.tensor_reduce(rv[:, 2:3], rq, AX.X, ALU.add))
                V.tensor_scalar(rv[:, 0:1], rv[:, 2:3], 1.0 / D, 1e-5, ALU.mult, ALU.add).then_inc(s["rvv"], 1)
                held(dve, "rst", i + 1)
                step(V.reciprocal(rv[:, 3:4], rv[:, 1:2]))
                held(dve, f"out{k}", 8 * (i - k) + 1)
                V.tensor_scalar(yt[:, k * 64:k * 64 + 64], rc, rv[:, 3:4], None, ALU.mult).then_inc(s["done"], 1)
                assert nb[0] == LCH, nb[0]
            schedule(dve, dict(begin=begin, recur=recur, front=front, sums=sums, back=back))

        @block.gpsimd
        def _(pool):
            nc.gpsimd.memset(ident, 0.0).then_inc(s["id"], 1)
            pool.wait_ge(s["id"], 1)
            nc.gpsimd.affine_select(out=ident, in_=ident, compare_op=ALU.not_equal, fill=1.0, base=0,
                                    pattern=[[-1, 128]], channel_multiplier=1).then_inc(s["id"], 1)

            def tile(i, k):
                for h in range(H):
                    if h % 4 == 0:
                        held(pool, "idx", 2 * i + h // 4 + 1)
                    if h >= 4:
                        held(pool, "bch", BCH * i + 2 * (h - 4) + 2)
                    elif not isinstance(i, int) or i > 0:
                        held(pool, "bch", BCH * (i - 1) + 2 * (h + 4) + 2)
                    for j in range(TOPK):
                        n = k * 128 + h * TOPK + j
                        nc.gpsimd.indirect_dma_start(KV[:, (h % 4) * 2048 + j * 128:(h % 4) * 2048 + j * 128 + 128], None, T["kvtab"],
                                                     bass.IndirectOffsetOnAxis(ap=rowidx[:, n:n + 1], axis=0)).then_inc(slot[h % 4], 16)
            tile(0, 0)
            with pool.Fori(0, BP // 2 - 1) as ii:
                for k in range(2):
                    tile(2 * ii + k + 1, 1 - k)
            tile(BP - 1, 1)


FCHA, FCH, LCH, BCH, WCH = 5, 19, 13, 2 * H, 1
NREC = 168


def kernel(**inputs):
    import concourse.bacc as bacc
    from concourse.bass_utils import run_bass_kernel_spmd

    x = {k: np.asarray(v) for k, v in inputs.items()}
    mixer = {k: v for k, v in x.items() if k == "x" or k.startswith("L0_tok")}
    arrays = {**host_constants(), **ffn_constants(), **host_layout(**mixer), **ffn_layout(**{k: v for k, v in x.items() if k not in mixer})}
    nc = bacc.Bacc("TRN2", target_bir_lowering=False, num_devices=1)
    T = {k: nc.dram_tensor(f"in_{k}", v.shape, mybir.dt.from_np(v.dtype), kind="ExternalInput").ap() for k, v in arrays.items()}
    out = nc.dram_tensor("out", (BP, 128, D), F32, kind="ExternalOutput").ap()
    vision_tower(nc, T, out)
    r = run_bass_kernel_spmd(nc, [{f"in_{k}": v for k, v in arrays.items()}], core_ids=[0])
    return r.results[0]["out"].reshape(B, S, S)
```
